# Optimizing a Trainium2 kernel written in Bass

```python
import numpy as np
import jax
import jax.numpy as jnp

def _softmax(x, axis=-1):
    return jax.nn.softmax(x, axis=axis)

def _gelu(x):
    return jax.nn.gelu(x, approximate=True)

def _silu(x):
    return jax.nn.silu(x)

def _sigmoid(x):
    return jax.nn.sigmoid(x)

def _layernorm(x, axis=-1, eps=1e-05):
    m = jnp.mean(x, axis=axis, keepdims=True)
    v = jnp.var(x, axis=axis, keepdims=True)
    return (x - m) / jnp.sqrt(v + eps)

def _scatter_add(tgt, idx, src, axis=0):
    return tgt.at[idx].add(src)

def _segment_sum(src, seg, n):
    return jax.ops.segment_sum(src, seg, n)
kernel_name = 'mk_xattn_ffn_d1_seqx_r2_1de055'

def setup_inputs(seed: int=0):
    np.random.seed(seed)
    _w = jnp.asarray

    def _rec_inputs():
        import jax
        import jax.numpy as jnp
        _rk = jax.random.key(seed)
        x = -0.0003929 + 0.9999 * jax.random.normal(jax.random.fold_in(_rk, 1), (2, 1024, 2048), jnp.float32)
        _lenS = 1024 - jax.random.randint(jax.random.fold_in(_rk, 7), (2,), 0, max(1, 1024 // 4) + 1, jnp.int32)
        _lenS2 = 2048 - jax.random.randint(jax.random.fold_in(_rk, 8), (2,), 0, max(1, 2048 // 4) + 1, jnp.int32)
        pos_BxS = jnp.broadcast_to(jnp.arange(1024, dtype=jnp.int32), (2, 1024))
        _ctx_1024P = jax.random.normal(jax.random.fold_in(_rk, 12), (2, 16, 512), jnp.float32)
        _ctx_1024c = jax.random.dirichlet(jax.random.fold_in(_rk, 512), 0.3 * jnp.ones((16,), jnp.float32), (2, 2048))
        _ctx_1024t = jnp.einsum('bsk,bkd->bsd', _ctx_1024c, _ctx_1024P)
        _ctx_1024t = _ctx_1024t * jax.lax.rsqrt(jnp.mean(jnp.square(_ctx_1024t)) + 1e-12) * 0.953939
        ctx_1024 = 6.77073e-06 + 0.0199965 * (_ctx_1024t + 0.3 * jax.random.normal(jax.random.fold_in(_rk, 612), (2, 2048, 512), jnp.float32))
        return (x, pos_BxS, ctx_1024)
    x, pos_BxS, ctx_1024 = _rec_inputs()

    def _L0_xattn_setup():
        import jax, jax.numpy as jnp
        import numpy as np
        H = 512
        C = 4
        RH = 16
        HS = H // RH
        DR = 8
        M = 2048
        NH = 16
        HD = H // NH
        A_SIZE = (C - 1) * RH
        B_SIZE = C * RH
        EPS = 1e-05
        SSM_EPS = 1e-05

        def rat_read(res, W, gamma, beta, num_outputs):
            b, l, _ = res.shape
            x = res.reshape(b, l, H, C)
            y = jnp.einsum('blhc,hoc->bloh', x, W)
            mu = y.mean(-1, keepdims=True)
            var = y.var(-1, keepdims=True)
            yn = (y - mu) * jax.lax.rsqrt(var + EPS)
            yn = yn * gamma.reshape(num_outputs, H) + beta.reshape(num_outputs, H)
            return yn.reshape(b, l, num_outputs * H)

        def rope(x, pos):
            half = HD // 2
            inv = 1.0 / 10000.0 ** (jnp.arange(half, dtype=jnp.float32) / half)
            ang = pos.astype(jnp.float32)[..., None] * inv
            cos = jnp.cos(ang)[:, :, None, :]
            sin = jnp.sin(ang)[:, :, None, :]
            x1, x2 = (x[..., :half], x[..., half:])
            return jnp.concatenate([x1 * cos - x2 * sin, x2 * cos + x1 * sin], axis=-1)

        def attention(qkv_in, qkv_w, pos):
            b, l, _ = qkv_in.shape
            q, k, v = jnp.split(qkv_in, 3, axis=-1)
            q = jnp.einsum('bli,oi->blo', q, qkv_w[0]).reshape(b, l, NH, HD)
            k = jnp.einsum('bli,oi->blo', k, qkv_w[1]).reshape(b, l, NH, HD)
            v = jnp.einsum('bli,oi->blo', v, qkv_w[2]).reshape(b, l, NH, HD)
            q = rope(q, pos)
            k = rope(k, pos)
            scores = jnp.einsum('bqhd,bkhd->bhqk', q, k) / np.sqrt(HD).astype(np.float32)
            mask = jnp.tril(jnp.ones((l, l), dtype=bool))
            scores = jnp.where(mask, scores, jnp.float32(-1e+30))
            p = jax.nn.softmax(scores, axis=-1)
            o = jnp.einsum('bhqk,bkhd->bqhd', p, v)
            return o.reshape(b, l, H)

        def rat_write(res, y, wod_w, wab_w, wab_b, du_w, du_b):
            b, l, _ = res.shape
            o_d = y @ wod_w.T
            A_B = y @ wab_w.T + wab_b
            out = o_d[..., :H]
            delta_low = o_d[..., H:]
            A_logit = A_B[..., :A_SIZE]
            B_proj = A_B[..., A_SIZE:2 * A_SIZE]
            B_skip = A_B[..., 2 * A_SIZE:]
            delta = jax.nn.softplus(delta_low @ du_w.T + du_b)
            hs = res.reshape(b, l, HS, RH, C)
            out = out.reshape(b, l, HS, RH, 1)
            delta = delta.reshape(b, l, HS, RH, 1)
            A_logit = A_logit.reshape(b, l, 1, RH, C - 1)
            B_proj = B_proj.reshape(b, l, 1, RH, C - 1)
            B_skip = B_skip.reshape(b, l, 1, RH, 1)
            A_neg = -jax.nn.softplus(A_logit)
            A_bar = jnp.exp(delta * A_neg)
            B_bar = (A_bar - 1.0) / (A_neg - SSM_EPS) * B_proj
            B_bar_skip = delta * B_skip
            A_full = jnp.concatenate([A_bar, jnp.ones_like(A_bar[..., :1])], axis=-1)
            B_full = jnp.concatenate([B_bar, B_bar_skip], axis=-1)
            return (hs * A_full + out * B_full).reshape(b, l, H * C)

        def layer_forward(hidden_states, position_ids, attn_read_w, attn_read_g, attn_read_b, qkv_w, attn_wod_w, attn_wab_w, attn_wab_b, attn_du_w, attn_du_b, mlp_read_w, mlp_read_g, mlp_read_b, mlp_in_w, mlp_wod_w, mlp_wab_w, mlp_wab_b, mlp_du_w, mlp_du_b):
            qkv_in = rat_read(hidden_states, attn_read_w, attn_read_g, attn_read_b, 3)
            attn_out = attention(qkv_in, qkv_w, position_ids)
            hidden_states = rat_write(hidden_states, attn_out, attn_wod_w, attn_wab_w, attn_wab_b, attn_du_w, attn_du_b)
            mlp_in = rat_read(hidden_states, mlp_read_w, mlp_read_g, mlp_read_b, 2)
            g_in, u_in = (mlp_in[..., :H], mlp_in[..., H:])
            gate = jnp.einsum('bli,oi->blo', g_in, mlp_in_w[0])
            up = jnp.einsum('bli,oi->blo', u_in, mlp_in_w[1])
            mlp_out = jax.nn.silu(gate) * up
            hidden_states = rat_write(hidden_states, mlp_out, mlp_wod_w, mlp_wab_w, mlp_wab_b, mlp_du_w, mlp_du_b)
            return hidden_states
        key = jax.random.key(seed)
        ks = jax.random.split(key, 20)
        B, L = (2, 1024)
        s = 0.02
        return {'hidden_states': jax.random.normal(ks[0], (B, L, H * C), jnp.float32), 'position_ids': jnp.tile(jnp.arange(L, dtype=jnp.int64), (B, 1)), 'attn_read_w': jax.random.normal(ks[1], (H, 3, C), jnp.float32) / np.sqrt(C).astype(np.float32), 'attn_read_g': jnp.ones((3 * H,), jnp.float32), 'attn_read_b': jnp.zeros((3 * H,), jnp.float32), 'qkv_w': jax.random.normal(ks[2], (3, H, H), jnp.float32) * s, 'attn_wod_w': jax.random.normal(ks[3], (H + DR, H), jnp.float32) * s, 'attn_wab_w': jax.random.normal(ks[4], (A_SIZE + B_SIZE, H), jnp.float32) * s, 'attn_wab_b': jax.random.normal(ks[5], (A_SIZE + B_SIZE,), jnp.float32) * s, 'attn_du_w': jax.random.normal(ks[6], (H, DR), jnp.float32) * s, 'attn_du_b': jax.random.normal(ks[7], (H,), jnp.float32) * s, 'mlp_read_w': jax.random.normal(ks[8], (H, 2, C), jnp.float32) / np.sqrt(C).astype(np.float32), 'mlp_read_g': jnp.ones((2 * H,), jnp.float32), 'mlp_read_b': jnp.zeros((2 * H,), jnp.float32), 'mlp_in_w': jax.random.normal(ks[9], (2, M, H), jnp.float32) * s, 'mlp_wod_w': jax.random.normal(ks[10], (H + DR, M), jnp.float32) * s, 'mlp_wab_w': jax.random.normal(ks[11], (A_SIZE + B_SIZE, M), jnp.float32) * s, 'mlp_wab_b': jax.random.normal(ks[12], (A_SIZE + B_SIZE,), jnp.float32) * s, 'mlp_du_w': jax.random.normal(ks[13], (H, DR), jnp.float32) * s, 'mlp_du_b': jax.random.normal(ks[14], (H,), jnp.float32) * s}
    _L0_xattn_all = _L0_xattn_setup()
    _L0_xattn_in = {k: v for k, v in _L0_xattn_all.items() if k in ('attn_read_w', 'attn_read_g', 'attn_read_b', 'qkv_w', 'attn_wod_w', 'attn_wab_w', 'attn_wab_b', 'attn_du_w', 'attn_du_b', 'mlp_read_w', 'mlp_read_g', 'mlp_read_b', 'mlp_wod_w', 'mlp_wab_w', 'mlp_wab_b', 'mlp_du_w', 'mlp_du_b')}
    del _L0_xattn_all

    def _L0_ffn_setup():
        import jax, jax.numpy as jnp
        import numpy as np

        def _dequant(weight_q, scale, zp):
            N, K = weight_q.shape
            num_groups = scale.shape[1]
            gs = K // num_groups
            q = weight_q.astype(jnp.float32).reshape(N, num_groups, gs)
            w = (q - zp[:, :, None]) * scale[:, :, None]
            return w.reshape(N, K)
        key = jax.random.key(seed)
        k1, k2, k3, k4, k5 = jax.random.split(key, 5)
        B, S, K, N, G = (4, 1024, 2048, 2048, 64)
        x = jax.random.normal(k1, (B, S, K), dtype=jnp.float32)
        weight_q = jax.random.randint(k2, (N, K), 0, 4, dtype=jnp.int32)
        scale = jax.random.uniform(k3, (N, K // G), dtype=jnp.float32) * 0.05 + 0.01
        zp = jax.random.uniform(k4, (N, K // G), dtype=jnp.float32) * 3.0
        bias = jax.random.normal(k5, (N,), dtype=jnp.float32)
        return {'x': x, 'weight_q': weight_q, 'scale': scale, 'zp': zp, 'bias': bias}
    _L0_ffn_all = _L0_ffn_setup()
    _L0_ffn_in = {k: v for k, v in _L0_ffn_all.items() if k in ('weight_q', 'scale', 'zp', 'bias')}
    del _L0_ffn_all
    return {'x': x, 'pos_BxS': pos_BxS, 'ctx_1024': ctx_1024, 'L0_xattn_attn_read_w': _L0_xattn_in['attn_read_w'], 'L0_xattn_attn_read_g': _L0_xattn_in['attn_read_g'], 'L0_xattn_attn_read_b': _L0_xattn_in['attn_read_b'], 'L0_xattn_qkv_w': _L0_xattn_in['qkv_w'], 'L0_xattn_attn_wod_w': _L0_xattn_in['attn_wod_w'], 'L0_xattn_attn_wab_w': _L0_xattn_in['attn_wab_w'], 'L0_xattn_attn_wab_b': _L0_xattn_in['attn_wab_b'], 'L0_xattn_attn_du_w': _L0_xattn_in['attn_du_w'], 'L0_xattn_attn_du_b': _L0_xattn_in['attn_du_b'], 'L0_xattn_mlp_read_w': _L0_xattn_in['mlp_read_w'], 'L0_xattn_mlp_read_g': _L0_xattn_in['mlp_read_g'], 'L0_xattn_mlp_read_b': _L0_xattn_in['mlp_read_b'], 'L0_xattn_mlp_wod_w': _L0_xattn_in['mlp_wod_w'], 'L0_xattn_mlp_wab_w': _L0_xattn_in['mlp_wab_w'], 'L0_xattn_mlp_wab_b': _L0_xattn_in['mlp_wab_b'], 'L0_xattn_mlp_du_w': _L0_xattn_in['mlp_du_w'], 'L0_xattn_mlp_du_b': _L0_xattn_in['mlp_du_b'], 'L0_ffn_weight_q': _L0_ffn_in['weight_q'], 'L0_ffn_scale': _L0_ffn_in['scale'], 'L0_ffn_zp': _L0_ffn_in['zp'], 'L0_ffn_bias': _L0_ffn_in['bias']}

def reference(x, pos_BxS, ctx_1024, L0_xattn_attn_read_w, L0_xattn_attn_read_g, L0_xattn_attn_read_b, L0_xattn_qkv_w, L0_xattn_attn_wod_w, L0_xattn_attn_wab_w, L0_xattn_attn_wab_b, L0_xattn_attn_du_w, L0_xattn_attn_du_b, L0_xattn_mlp_read_w, L0_xattn_mlp_read_g, L0_xattn_mlp_read_b, L0_xattn_mlp_wod_w, L0_xattn_mlp_wab_w, L0_xattn_mlp_wab_b, L0_xattn_mlp_du_w, L0_xattn_mlp_du_b, L0_ffn_weight_q, L0_ffn_scale, L0_ffn_zp, L0_ffn_bias):
    import jax
    import jax.numpy as jnp

    def _L0_xattn_ref(hidden_states, position_ids, attn_read_w, attn_read_g, attn_read_b, qkv_w, attn_wod_w, attn_wab_w, attn_wab_b, attn_du_w, attn_du_b, mlp_read_w, mlp_read_g, mlp_read_b, mlp_in_w, mlp_wod_w, mlp_wab_w, mlp_wab_b, mlp_du_w, mlp_du_b):
        import jax, jax.numpy as jnp
        import numpy as np
        H = 512
        C = 4
        RH = 16
        HS = H // RH
        DR = 8
        M = 2048
        NH = 16
        HD = H // NH
        A_SIZE = (C - 1) * RH
        B_SIZE = C * RH
        EPS = 1e-05
        SSM_EPS = 1e-05

        def rat_read(res, W, gamma, beta, num_outputs):
            b, l, _ = res.shape
            x = res.reshape(b, l, H, C)
            y = jnp.einsum('blhc,hoc->bloh', x, W)
            mu = y.mean(-1, keepdims=True)
            var = y.var(-1, keepdims=True)
            yn = (y - mu) * jax.lax.rsqrt(var + EPS)
            yn = yn * gamma.reshape(num_outputs, H) + beta.reshape(num_outputs, H)
            return yn.reshape(b, l, num_outputs * H)

        def rope(x, pos):
            half = HD // 2
            inv = 1.0 / 10000.0 ** (jnp.arange(half, dtype=jnp.float32) / half)
            ang = pos.astype(jnp.float32)[..., None] * inv
            cos = jnp.cos(ang)[:, :, None, :]
            sin = jnp.sin(ang)[:, :, None, :]
            x1, x2 = (x[..., :half], x[..., half:])
            return jnp.concatenate([x1 * cos - x2 * sin, x2 * cos + x1 * sin], axis=-1)

        def attention(qkv_in, qkv_w, pos):
            b, l, _ = qkv_in.shape
            q, k, v = jnp.split(qkv_in, 3, axis=-1)
            q = jnp.einsum('bli,oi->blo', q, qkv_w[0]).reshape(b, l, NH, HD)
            k = jnp.einsum('bli,oi->blo', k, qkv_w[1]).reshape(b, l, NH, HD)
            v = jnp.einsum('bli,oi->blo', v, qkv_w[2]).reshape(b, l, NH, HD)
            q = rope(q, pos)
            k = rope(k, pos)
            scores = jnp.einsum('bqhd,bkhd->bhqk', q, k) / np.sqrt(HD).astype(np.float32)
            mask = jnp.tril(jnp.ones((l, l), dtype=bool))
            scores = jnp.where(mask, scores, jnp.float32(-1e+30))
            p = jax.nn.softmax(scores, axis=-1)
            o = jnp.einsum('bhqk,bkhd->bqhd', p, v)
            return o.reshape(b, l, H)

        def rat_write(res, y, wod_w, wab_w, wab_b, du_w, du_b):
            b, l, _ = res.shape
            o_d = y @ wod_w.T
            A_B = y @ wab_w.T + wab_b
            out = o_d[..., :H]
            delta_low = o_d[..., H:]
            A_logit = A_B[..., :A_SIZE]
            B_proj = A_B[..., A_SIZE:2 * A_SIZE]
            B_skip = A_B[..., 2 * A_SIZE:]
            delta = jax.nn.softplus(delta_low @ du_w.T + du_b)
            hs = res.reshape(b, l, HS, RH, C)
            out = out.reshape(b, l, HS, RH, 1)
            delta = delta.reshape(b, l, HS, RH, 1)
            A_logit = A_logit.reshape(b, l, 1, RH, C - 1)
            B_proj = B_proj.reshape(b, l, 1, RH, C - 1)
            B_skip = B_skip.reshape(b, l, 1, RH, 1)
            A_neg = -jax.nn.softplus(A_logit)
            A_bar = jnp.exp(delta * A_neg)
            B_bar = (A_bar - 1.0) / (A_neg - SSM_EPS) * B_proj
            B_bar_skip = delta * B_skip
            A_full = jnp.concatenate([A_bar, jnp.ones_like(A_bar[..., :1])], axis=-1)
            B_full = jnp.concatenate([B_bar, B_bar_skip], axis=-1)
            return (hs * A_full + out * B_full).reshape(b, l, H * C)

        def layer_forward(hidden_states, position_ids, attn_read_w, attn_read_g, attn_read_b, qkv_w, attn_wod_w, attn_wab_w, attn_wab_b, attn_du_w, attn_du_b, mlp_read_w, mlp_read_g, mlp_read_b, mlp_in_w, mlp_wod_w, mlp_wab_w, mlp_wab_b, mlp_du_w, mlp_du_b):
            qkv_in = rat_read(hidden_states, attn_read_w, attn_read_g, attn_read_b, 3)
            attn_out = attention(qkv_in, qkv_w, position_ids)
            hidden_states = rat_write(hidden_states, attn_out, attn_wod_w, attn_wab_w, attn_wab_b, attn_du_w, attn_du_b)
            mlp_in = rat_read(hidden_states, mlp_read_w, mlp_read_g, mlp_read_b, 2)
            g_in, u_in = (mlp_in[..., :H], mlp_in[..., H:])
            gate = jnp.einsum('bli,oi->blo', g_in, mlp_in_w[0])
            up = jnp.einsum('bli,oi->blo', u_in, mlp_in_w[1])
            mlp_out = jax.nn.silu(gate) * up
            hidden_states = rat_write(hidden_states, mlp_out, mlp_wod_w, mlp_wab_w, mlp_wab_b, mlp_du_w, mlp_du_b)
            return hidden_states
        return layer_forward(hidden_states, position_ids, attn_read_w, attn_read_g, attn_read_b, qkv_w, attn_wod_w, attn_wab_w, attn_wab_b, attn_du_w, attn_du_b, mlp_read_w, mlp_read_g, mlp_read_b, mlp_in_w, mlp_wod_w, mlp_wab_w, mlp_wab_b, mlp_du_w, mlp_du_b)

    def _L0_ffn_ref(x, weight_q, scale, zp, bias):
        import jax, jax.numpy as jnp
        import numpy as np

        def _dequant(weight_q, scale, zp):
            N, K = weight_q.shape
            num_groups = scale.shape[1]
            gs = K // num_groups
            q = weight_q.astype(jnp.float32).reshape(N, num_groups, gs)
            w = (q - zp[:, :, None]) * scale[:, :, None]
            return w.reshape(N, K)
        w = _dequant(weight_q, scale, zp)
        out = jnp.einsum('bsk,nk->bsn', x, w)
        return out + bias
    x = x + _L0_xattn_ref(_layernorm(x, axis=-1), pos_BxS, L0_xattn_attn_read_w, L0_xattn_attn_read_g, L0_xattn_attn_read_b, L0_xattn_qkv_w, L0_xattn_attn_wod_w, L0_xattn_attn_wab_w, L0_xattn_attn_wab_b, L0_xattn_attn_du_w, L0_xattn_attn_du_b, L0_xattn_mlp_read_w, L0_xattn_mlp_read_g, L0_xattn_mlp_read_b, ctx_1024, L0_xattn_mlp_wod_w, L0_xattn_mlp_wab_w, L0_xattn_mlp_wab_b, L0_xattn_mlp_du_w, L0_xattn_mlp_du_b)
    x = x + _L0_ffn_ref(_layernorm(x, axis=-1), L0_ffn_weight_q, L0_ffn_scale, L0_ffn_zp, L0_ffn_bias)
    return x

_drawn_inputs = setup_inputs


def setup_inputs(seed=0):
    import zlib

    import numpy as np

    out = dict(_drawn_inputs(seed))
    spreads = {'L0_xattn_attn_read_g': (1.0, 0.2),
     'L0_xattn_attn_read_b': (0.0, 0.1),
     'L0_xattn_mlp_read_g': (1.0, 0.2),
     'L0_xattn_mlp_read_b': (0.0, 0.1)}
    factors = {}
    for name, (base, spread) in spreads.items():
        noise = np.random.default_rng([zlib.crc32(name.encode()), seed]).standard_normal(out[name].shape)
        drawn = base * np.exp(spread * noise) if base else spread * noise
        out[name] = jnp.asarray(drawn.astype(out[name].dtype))
    for name, factor in factors.items():
        out[name] = (out[name] * factor).astype(out[name].dtype)
    return out
```

```python
import math
from contextlib import ExitStack

import numpy as np
import concourse.bass as bass
from concourse import mybir

F32 = mybir.dt.float32
F32R = mybir.dt.float32r
I32 = mybir.dt.int32
BF16 = mybir.dt.bfloat16
ALU = mybir.AluOpType
ACT = mybir.ActivationFunctionType
AX = mybir.AxisListType.X
ds = bass.ds

P = 128
B, L, D = 2, 1024, 2048
T = B * L
H, C = 512, 4
RH = 16
HS = H // RH
DR = 8
NH, HD = 16, 32
M = 2048
NA = (C - 1) * RH
NAB = NA + C * RH
NW = H + DR + NAB
G = 64
EPS = 1e-5
TILES = T // P
KD, KH, KM = D // P, H // P, M // P
QT = L // P
HEADS = B * NH
NEG = -1e30
VN = 96


class Step:

    def __init__(self, reg, off, tiles):
        self.reg, self.off, self.tiles = reg, off, tiles

    def __sub__(self, n):
        return Step(self.reg, self.off - n, self.tiles)

    def exists(self):
        return self.reg is not None or self.off >= 0

    def at(self, per=1, extra=0):
        if self.reg is None:
            return per * self.off + extra
        return self.reg * per + (self.off * per + extra)

    def turn(self, ring, per, extra=0):
        if self.reg is None:
            return per * (self.off // ring) + extra
        return self.reg * (per // ring) + (self.off // ring * per + extra)


def steps(eng, tiles, depth, unroll, body, peel=0):
    head = -(-max(depth, peel) // unroll) * unroll
    turns = (tiles - head) // unroll
    for s in range(head):
        body(Step(None, s, tiles), s % unroll, lambda d, s=s: 0 <= s - d < tiles)
    if turns:
        with eng.Fori(0, turns) as i:
            base = i * unroll
            for j in range(unroll):
                body(Step(base, head + j, tiles), j, lambda d: True)
    for s in range(head + turns * unroll, tiles + depth):
        body(Step(None, s, tiles), s % unroll, lambda d, s=s: 0 <= s - d < tiles)


def count(tile, per, event):
    if tile.reg is None and tile.off >= tile.tiles:
        return per * tile.tiles
    assert per * tile.off + event > 0
    return tile.at(per, event)


def due(tile, per, event):
    return tile.reg is not None or per * tile.off + event > 0


def dma_count(tile, ring, dmas):
    assert tile.off // ring >= 0
    return tile.turn(ring, 16 * dmas, 16 * dmas)


def allocators(nc, ctx, tag=""):
    def sb(name, shape, dt=F32):
        return ctx.enter_context(nc.sbuf_tensor(tag + name, shape, dt))

    def ps(name, shape, dt=F32):
        return ctx.enter_context(nc.psum_tensor(tag + name, shape, dt))

    def sem(name):
        return nc.alloc_semaphore(name=tag + name)

    return sb, ps, sem


def spread(ap, *dims):
    return ap.broadcast_to(list(dims))


def build_constants(nc, ctx, io):
    sb, ps, sem = allocators(nc, ctx, "c_")
    k = {}
    k["ident"] = sb("ident", [P, P])
    k["mask_b"] = sb("mask_b", [P, P], BF16)
    k["maskT_b"] = sb("maskT_b", [P, P], BF16)
    k["ident_b"] = sb("ident_b", [P, P], BF16)
    k["ln1"] = sb("ln1", [P, TILES, 2])
    k["settled"] = sem("settled")
    with ExitStack() as c:
        sb2, _, sem = allocators(nc, c, "c_")
        mask = sb2("mask", [P, P])
        maskT = sb2("maskT", [P, P])
        zeroed, chosen = sem("zeroed"), sem("chosen")
        with nc.Block() as block:
            @block.gpsimd
            def _(pool):
                for m in (k["ident"], mask, maskT):
                    pool.memset(m[:], 0.0).then_inc(zeroed, 1)
                pool.wait_ge(zeroed, 3)
                pool.affine_select(out=k["ident"][:], in_=k["ident"][:], compare_op=ALU.not_equal, fill=1.0,
                                   base=0, pattern=[[-1, P]], channel_multiplier=1).then_inc(chosen, 1)
                pool.affine_select(out=mask[:], in_=mask[:], compare_op=ALU.is_ge, fill=NEG,
                                   base=0, pattern=[[-1, P]], channel_multiplier=1).then_inc(chosen, 1)
                pool.affine_select(out=maskT[:], in_=maskT[:], compare_op=ALU.is_ge, fill=NEG,
                                   base=0, pattern=[[1, P]], channel_multiplier=-1).then_inc(chosen, 1)
            @block.vector
            def _(dve):
                dve.wait_ge(chosen, 3)
                dve.tensor_copy(k["ident_b"][:], k["ident"][:])
                dve.tensor_copy(k["mask_b"][:], mask[:])
                dve.tensor_copy(k["maskT_b"][:], maskT[:])
    return k


def allocate_values(nc, ctx, k):
    sb, _, _ = allocators(nc, ctx, "v_")
    k["v_flat"] = sb("v_sb", [P, HEADS * QT * (HD + 1) + VN])
    k["v_sb"] = k["v_flat"][:, 0:HEADS * QT * (HD + 1)].rearrange("p (n t d) -> p n t d", n=HEADS, t=QT)
    with nc.Block() as block:
        @block.gpsimd
        def _(pool):
            pool.memset(k["v_flat"][:], 1.0)


def build_qkv(nc, io, k):
    HD2 = HD // 2
    with ExitStack() as ctx:
        sb, ps, sem = allocators(nc, ctx, "s1_")
        O = 3
        OW = O * HD
        wh = sb("q_wh", [P, KH, O * H], F32R)
        wl = sb("q_wl", [P, KH, O * H], F32R)
        brow = sb("q_brow", [P, O * H], F32R)
        c64 = sb("q_c64", [P, P], F32R)
        spf = sb("q_spf", [P, KD, OW])
        wsum = sb("q_wsum", [P, KD * OW])
        cosT = sb("cosT", [P, TILES, HD2])
        sinT = sb("sinT", [P, TILES, 2, HD2])

        psY = ps("psY", [P, 2, 512])
        psA = ps("psA", [P, KH, P])
        psB = ps("psB", [P, KH, P])
        psC = ps("psC", [P, KH, P])
        psQ = ps("psQ", [P, O, H])
        y_bank, qk_bank = (psA, psB, psA), (psC, psB)

        with ExitStack() as c:
            sb, _, sem = allocators(nc, c, "s1_")
            wraw = sb("q_wraw", [P, KH, O * H])
            gam = sb("q_gam", [P, O, KH])
            bet = sb("q_bet", [P, O, KH])
            rw = sb("q_rw", [P, KD, O])
            m32 = sb("q_m32", [P, HD])
            ones = sb("q_onesf", [P, P])
            betb = sb("q_betb", [P, O, KH, P])
            posi = sb("q_posi", [P, TILES], I32)
            posf = sb("q_posf", [P, TILES])
            inv = sb("q_inv", [P, HD2])
            ang = sb("q_ang", [P, TILES, HD2])
            turn = sb("q_turn", [P, TILES, HD2])
            red = sb("q_red", [P, TILES, HD2])
            w_in, small_in, blk, dve_w, act_w, pe_w, d = (sem(n) for n in
                ("w_in", "small_in", "blk", "dve_w", "act_w", "pe_w", "d"))
            trig, wsum_ok = sem("trig"), sem("wsum_ok")
            with nc.Block() as block:
                @block.sync
                def _(sp):
                    sp.dma_start(rw[:], io["wr1"]).then_inc(small_in, 16)
                    sp.dma_start(gam[:], io["g1"]).then_inc(small_in, 16)
                    sp.dma_start(bet[:], io["b1"]).then_inc(small_in, 16)
                    sp.dma_start(posi[:], io["pos"]).then_inc(small_in, 16)
                    sp.dma_start(wraw[:], io["wqkv"]).then_inc(w_in, 16)

                @block.gpsimd
                def _(pool):
                    pool.memset(m32[:], 1.0).then_inc(blk, 1)
                    pool.wait_ge(blk, 1)
                    pool.affine_select(out=m32[:], in_=m32[:], compare_op=ALU.is_ge, fill=0.0, base=0,
                                       pattern=[[-C, HD]], channel_multiplier=1).then_inc(blk, 1)
                    pool.wait_ge(blk, 2)
                    pool.affine_select(out=m32[:], in_=m32[:], compare_op=ALU.is_ge, fill=0.0, base=C - 1,
                                       pattern=[[C, HD]], channel_multiplier=-1).then_inc(blk, 1)

                @block.vector
                def _(dve):
                    n = 0

                    def chain(ins):
                        nonlocal n
                        n += 1
                        ins.then_inc(d, 1)
                        dve.wait_ge(d, n)

                    for j in range(HD2):
                        f = np.float32(1.0) / np.float32(10000.0) ** (np.float32(j) / np.float32(HD2))
                        dve.memset(inv[:, j:j + 1], float(f))
                    dve.memset(ones[:], 1.0)
                    chain(dve.memset(turn[:], 1.0 / 64))
                    chain(dve.tensor_copy(c64[:], turn[:, 0:P // HD2, :].rearrange("p a b -> p (a b)")))
                    dve.wait_ge(small_in, 64)
                    dve.wait_ge(blk, 3)
                    chain(dve.tensor_tensor(spf[:].rearrange("p t (o j) -> p (t o) j", o=O),
                                            spread(rw[:].rearrange("p t o -> p (t o)").unsqueeze(2), P, KD * O, HD),
                                            spread(m32[:].unsqueeze(1), P, KD * O, HD), ALU.mult))
                    dve.tensor_copy(betb[:], spread(bet[:].unsqueeze(3), P, O, KH, P)).then_inc(dve_w, 1)
                    chain(dve.tensor_copy(posf[:], posi[:]))
                    chain(dve.tensor_tensor(ang[:], spread(posf[:].unsqueeze(2), P, TILES, HD2),
                                            spread(inv[:].unsqueeze(1), P, TILES, HD2), ALU.mult))
                    two_pi = 2 * math.pi
                    c1 = 6.28125
                    c2 = float(np.float32(round((two_pi - c1) * 2**19) / 2**19))
                    c3 = two_pi - c1 - c2
                    magic = 1.5 * 2.0**23
                    for which, shift in ((0, 0.0), (1, 0.25)):
                        chain(dve.tensor_scalar(turn[:], ang[:], 1 / two_pi, shift, ALU.mult, ALU.add))
                        chain(dve.tensor_scalar(turn[:], turn[:], magic, None, ALU.add))
                        chain(dve.tensor_scalar(turn[:], turn[:], magic, None, ALU.subtract))
                        if which:
                            dve.wait_ge(trig, 2)
                        chain(dve.scalar_tensor_tensor(red[:], turn[:], -c1, ang[:], ALU.mult, ALU.add))
                        chain(dve.scalar_tensor_tensor(red[:], turn[:], -c2, red[:], ALU.mult, ALU.add))
                        chain(dve.scalar_tensor_tensor(red[:], turn[:], -c3, red[:], ALU.mult, ALU.add))
                        if which:
                            chain(dve.tensor_scalar(red[:], red[:], math.pi / 2, None, ALU.add))
                        lim = 3.1415925
                        dve.tensor_scalar(red[:], red[:], lim, -lim, ALU.min, ALU.max).then_inc(trig, 1)
                    for o in range(O):
                        for kt in range(KH):
                            i = o * KH + kt
                            cols = slice(o * H, (o + 1) * H)
                            dve.wait_ge(act_w, i + 1)
                            dve.scalar_tensor_tensor(wl[:, kt, cols], wraw[:, kt, cols], gam[:, o, kt:kt + 1],
                                                     wh[:, kt, cols], ALU.mult, ALU.subtract)
                    for half in range(2):
                        dve.wait_ge(pe_w, half + 1)
                        dve.tensor_copy(wsum[:, half * 8 * OW:(half + 1) * 8 * OW].rearrange("p (b j) -> p b j", b=2),
                                        psY[:, :, 0:4 * OW]).then_inc(wsum_ok, 1)
                    dve.wait_ge(pe_w, 3)
                    chain(dve.tensor_copy(brow[:], psQ[:].rearrange("p o n -> p (o n)")))
                    dve.tensor_tensor(brow[64:P, :], psQ[64:P].rearrange("p o n -> p (o n)"), brow[64:P, :],
                                      ALU.subtract)

                @block.scalar
                def _(act):
                    act.wait_ge(small_in, 64)
                    act.wait_ge(w_in, 16)
                    for o in range(O):
                        for kt in range(KH):
                            cols = slice(o * H, (o + 1) * H)
                            act.activation(wh[:, kt, cols], wraw[:, kt, cols], ACT.Copy,
                                           scale=gam[:, o, kt:kt + 1]).then_inc(act_w, 1)
                    act.wait_ge(trig, 1)
                    act.activation(sinT[:, :, 1, :], red[:], ACT.Sin)
                    act.activation(sinT[:, :, 0, :], red[:], ACT.Sin, scale=-1.0).then_inc(trig, 1)
                    act.wait_ge(trig, 3)
                    act.activation(cosT[:], red[:], ACT.Sin)

                @block.tensor
                def _(pe):
                    pe.wait_ge(dve_w, 1)
                    for half in range(2):
                        if half:
                            pe.wait_ge(wsum_ok, 1)
                        for kt in range(8 * half, 8 * half + 8):
                            out = psY[:, kt // 4 % 2, (kt % 4) * OW:(kt % 4 + 1) * OW]
                            mm = pe.matmul(out, ones[:], spf[:, kt, :], start=True, stop=True)
                        mm.then_inc(pe_w, 1)
                    pe.wait_ge(w_in, 16)
                    for o in range(O):
                        for kt in range(KH):
                            mm = pe.matmul(psQ[:, o, :], betb[:, o, kt, :], wraw[:, kt, o * H:(o + 1) * H],
                                           start=(kt == 0), stop=(kt == KH - 1))
                    mm.then_inc(pe_w, 1)

        sb, ps, sem = allocators(nc, ctx, "s1_")
        xt = sb("q_xt", [P, 2, KD, P])
        xc = sb("q_xc", [P, 2, D])
        yr = sb("q_yr", [P, KD, OW])
        yn = sb("q_yn", [P, O, H])
        yth = sb("q_yth", [P, O, KH, P], F32R)
        ytl = sb("q_ytl", [P, O, KH, P], F32R)
        ra = sb("q_ra", [P, 2 * H])
        rb = sb("q_rb", [P, 2 * H])
        qk = sb("q_qk", [P, 2 * H])
        qth = sb("q_qth", [P, 2, KH, P], F32R)
        qtl = sb("q_qtl", [P, 2, KH, P], F32R)
        bst = sb("q_bst", [P, 4, 6])
        bsy = sb("q_bsy", [P, O, 6])
        mv = sb("q_mv", [P, O, 2])
        sx = sb("q_sx", [P, 2, 5])
        sy = sb("q_sy", [P, 5, O])

        X_AGG, X_EPS, X_NEG, X_INV = 5, 6, 7, 8
        Y_LESS, Y_AGG, Y_VAR, Y_INV, Y_SQ = 2, 8, 9, 10, 11

        x_in = [sem(f"x_in{p}") for p in range(2)]
        y_mm = sem("y_mm")
        x_norm, y_norm = sem("x_norm"), sem("y_norm")
        rr_ok, sh_ok = sem("rr_ok"), sem("sh_ok")
        yn_ok = sem("yn_ok")
        yt_mm, yt_hi, yt_lo = sem("yt_mm"), sem("yt_hi"), sem("yt_lo")
        qkv_mm = sem("qkv_mm")
        rot_ab, rot = sem("rot_ab"), sem("rot")
        v_ok = sem("v_ok")
        qt_mm, qt_hi, qt_lo = sem("qt_mm"), sem("qt_hi"), sem("qt_lo")
        qk_out = sem("qk_out")

        def place(tile):
            n = tile.at()
            return n // QT, n % QT

        with nc.Block() as block:
            @block.sync
            def _(sp):
                def body(s, p, live):
                    if live(0):
                        if (s - 2).exists():
                            sp.wait_ge(y_mm, count(s - 2, 4, 4))
                        sp.sem_inc(k["settled"], 1)
                        if (s - 2).exists():
                            sp.wait_ge(x_norm, count(s - 2, 8, 4))
                        sp.sem_inc(k["settled"], 1)
                        tok = s.at(P)
                        sp.dma_start(xt[:, p], io["xT"][:, :, ds(tok, P)]).then_inc(x_in[p], 16)
                        sp.dma_start(xc[:, p], io["xP"][ds(tok, P), :]).then_inc(x_in[p], 16)
                    if live(4):
                        sp.wait_ge(qt_hi, count(s - 4, 2, 2))
                        sp.sem_inc(k["settled"], 1)
                        sp.wait_ge(qt_lo, count(s - 4, 2, 2))
                        sp.sem_inc(k["settled"], 1)
                        b_, kt_ = place(s - 4)
                        for side in range(2):
                            for hl, buf in ((0, qth), (1, qtl)):
                                dst = io["qkT"][side, hl].rearrange("(g p) t -> p g t", p=P)
                                dst = dst[:, ds(b_ * KH, KH), ds(kt_ * P, P)]
                                sp.dma_start(dst, buf[:, side].bitcast(F32)).then_inc(qk_out, 16)
                steps(sp, TILES, 4, 2, body)
                sp.wait_ge(qk_out, 16 * 4 * TILES)

            @block.gpsimd
            def _(pool):
                def body(s, p, live):
                    if live(2):
                        pool.wait_ge(rot_ab, count(s - 2, 2, 2))
                        if (s - 3).exists():
                            pool.wait_ge(qt_mm, count(s - 3, 2, 2))
                        pool.tensor_tensor(qk[:], ra[:], rb[:], ALU.add).then_inc(rot, 1)
                steps(pool, TILES, 3, 2, body)

            @block.scalar
            def _(act):
                def hi_y(s, o):
                    act.wait_ge(yt_mm, count(s - 2, 3, o + 1))
                    if (s - 3).exists():
                        act.wait_ge(qkv_mm, count(s - 3, 3, o + 1))
                    act.activation(yth[:, o], y_bank[o][:], ACT.Copy).then_inc(yt_hi, 1)

                def hi_qk(s, r):
                    act.wait_ge(qt_mm, count(s - 3, 2, r + 1))
                    if (s - 4).exists():
                        act.wait_ge(qk_out, dma_count(s - 4, 1, 4))
                    act.activation(qth[:, r], qk_bank[r][:], ACT.Copy).then_inc(qt_hi, 1)

                def body(s, p, live):
                    if live(2):
                        hi_y(s, 0)
                        hi_y(s, 1)
                    if live(2):
                        hi_y(s, 2)
                    if live(1):
                        act.wait_ge(y_norm, count(s - 1, 11, Y_SQ))
                        act.activation(sy[:, 2, :], sy[:, 1, :], ACT.Sqrt).then_inc(rr_ok, 1)
                        act.wait_ge(sh_ok, count(s - 1, 1, 1))
                        if (s - 2).exists():
                            act.wait_ge(yt_mm, count(s - 2, 3, 3))
                        for o in range(O):
                            act.activation(yn[:, o].rearrange("p (t j) -> p t j", j=HD),
                                           yr[:, :, o * HD:(o + 1) * HD], ACT.Identity,
                                           scale=sy[:, 2, o:o + 1], bias=sy[:, 3, o:o + 1]).then_inc(yn_ok, 1)
                    if live(3):
                        hi_qk(s, 0)
                    if live(2):
                        act.wait_ge(qkv_mm, count(s - 2, 3, 3))
                        b_, kt_ = place(s - 2)
                        dst = k["v_sb"].rearrange("p (b n) t d -> p b n t d", b=B)
                        dst = dst[:, ds(b_, 1), :, ds(kt_, 1), 0:HD].rearrange("p b n t d -> p (b n) (t d)")
                        act.activation(dst, psQ[:, 2].rearrange("p (n d) -> p n d", d=HD), ACT.Copy).then_inc(v_ok, 1)
                    if live(3):
                        hi_qk(s, 1)
                steps(act, TILES, 3, 2, body)

            @block.tensor
            def _(pe):
                def turn_qk(s, r):
                    pe.wait_ge(rot, count(s - 3, 1, 1))
                    if r == 0:
                        if (s - 4).exists():
                            pe.wait_ge(qt_hi, count(s - 4, 2, 1))
                        if (s - 4).exists():
                            pe.wait_ge(qt_lo, count(s - 4, 2, 1))
                    else:
                        pe.wait_ge(yt_hi, count(s - 2, 3, 2))
                        pe.wait_ge(yt_lo, count(s - 2, 3, 2))
                        if (s - 4).exists():
                            pe.wait_ge(qt_hi, count(s - 4, 2, 2))
                        if (s - 4).exists():
                            pe.wait_ge(qt_lo, count(s - 4, 2, 2))
                    for c in range(KH):
                        mm = pe.transpose(qk_bank[r][:, c], qk[:, r * H + c * P:r * H + (c + 1) * P], k["ident"][:])
                    mm.then_inc(qt_mm, 1)

                def turn_y(s, o):
                    pe.wait_ge(yn_ok, count(s - 2, 3, o + 1))
                    if o == 1:
                        if (s - 4).exists():
                            pe.wait_ge(qt_hi, count(s - 4, 2, 2))
                        if (s - 4).exists():
                            pe.wait_ge(qt_lo, count(s - 4, 2, 2))
                    before = s - 3 if o == 0 else s - 2
                    if o != 1:
                        if before.exists():
                            pe.wait_ge(yt_hi, count(before, 3, 3 if o == 0 else 1))
                        if before.exists():
                            pe.wait_ge(yt_lo, count(before, 3, 3 if o == 0 else 1))
                    for c in range(KH):
                        mm = pe.transpose(y_bank[o][:, c], yn[:, o, c * P:(c + 1) * P], k["ident"][:])
                    mm.then_inc(yt_mm, 1)

                def read(s, p, grp):
                    if grp == 0:
                        pe.wait_ge(x_in[1 - p], dma_count(s - 1, 2, 2))
                        if (s - 2).exists():
                            pe.wait_ge(y_norm, count(s - 2, 11, Y_LESS))
                    if grp == 2:
                        pe.wait_ge(y_norm, count(s - 1, 11, 1))
                    for kt in range(4 * grp, 4 * grp + 4):
                        out = psY[:, grp % 2, (kt % 4) * OW:(kt % 4 + 1) * OW]
                        mm = pe.matmul(out, xt[:, 1 - p, kt], spf[:, kt], start=True, stop=True)
                    mm.then_inc(y_mm, 1)

                def project(s, o):
                    pe.wait_ge(yt_hi, count(s - 2, 3, o + 1))
                    pe.wait_ge(yt_lo, count(s - 2, 3, o + 1))
                    if o < 2:
                        if (s - 3).exists():
                            pe.wait_ge(rot_ab, count(s - 3, 2, 2))
                    else:
                        if (s - 3).exists():
                            pe.wait_ge(v_ok, count(s - 3, 1, 1))
                    cols = slice(o * H, (o + 1) * H)
                    pe.matmul(psQ[:, o], c64[:], brow[:, cols], start=True, stop=False)
                    for kt in range(KH):
                        pe.matmul(psQ[:, o], yth[:, o, kt], wh[:, kt, cols], start=False, stop=False)
                        pe.matmul(psQ[:, o], yth[:, o, kt], wl[:, kt, cols], start=False, stop=False)
                        mm = pe.matmul(psQ[:, o], ytl[:, o, kt], wh[:, kt, cols], start=False, stop=(kt == KH - 1))
                    mm.then_inc(qkv_mm, 1)

                def body(s, p, live):
                    if live(1):
                        read(s, p, 0)
                        read(s, p, 1)
                    if live(2):
                        turn_y(s, 0)
                        turn_y(s, 1)
                        project(s, 0)
                    if live(1):
                        read(s, p, 2)
                        read(s, p, 3)
                    if live(2):
                        turn_y(s, 2)
                        project(s, 1)
                    if live(3):
                        turn_qk(s, 0)
                    if live(2):
                        project(s, 2)
                    if live(3):
                        turn_qk(s, 1)
                steps(pe, TILES, 3, 2, body)

            @block.vector
            def _(dve):
                def lo_y(s, o):
                    dve.wait_ge(yt_hi, count(s - 2, 3, o + 1))
                    dve.tensor_tensor(ytl[:, o], y_bank[o][:], yth[:, o], ALU.subtract).then_inc(yt_lo, 1)

                def lo_qk(s, r):
                    dve.wait_ge(qt_hi, count(s - 3, 2, r + 1))
                    dve.tensor_tensor(qtl[:, r], qk_bank[r][:], qth[:, r], ALU.subtract).then_inc(qt_lo, 1)

                lin = k["ln1"][:].rearrange("p t s -> p (t s)")

                def less_mean(s, half):
                    dve.wait_ge(x_norm, count(s - 1, 8, X_NEG))
                    dve.wait_ge(y_mm, count(s - 1, 4, 2 * half + 2))
                    if (s - 2).exists():
                        dve.wait_ge(yn_ok, count(s - 2, 3, 3))
                    tiles = slice(half * KD // 2, (half + 1) * KD // 2)
                    dve.scalar_tensor_tensor(yr[:, tiles].rearrange("p (b t) n -> p b (t n)", b=2),
                                             wsum[:].rearrange("p (h b n) -> p h b n", h=2, b=2)[:, half],
                                             sx[:, 1 - p_of(s), 1:2], psY[:, :, 0:4 * OW], ALU.mult, ALU.add)\
                       .then_inc(y_norm, 1)

                def p_of(s):
                    return s.off % 2

                def x_statistics(s, p):
                    dve.wait_ge(x_in[p], dma_count(s, 2, 2))
                    for j in range(4):
                        dve.bn_stats(bst[:, j], xc[:, p, j * 512:(j + 1) * 512]).then_inc(x_norm, 1)
                    dve.wait_ge(x_norm, count(s, 8, 4))
                    dve.sem_inc(k["settled"], 1)
                    dve.bn_aggr(sx[:, p, 3:5], bst[:]).then_inc(x_norm, 1)
                    dve.wait_ge(x_norm, count(s, 8, X_AGG))
                    dve.tensor_copy(lin[:, ds(s.at(2), 2)], sx[:, p, 3:5])
                    dve.tensor_scalar(sx[:, p, 0:1], sx[:, p, 4:5], EPS, None, ALU.add).then_inc(x_norm, 1)
                    dve.tensor_scalar(sx[:, p, 1:2], sx[:, p, 3:4], -1.0, None, ALU.mult).then_inc(x_norm, 1)
                    dve.wait_ge(x_norm, count(s, 8, X_EPS))
                    dve.reciprocal(sx[:, p, 2:3], sx[:, p, 0:1]).then_inc(x_norm, 1)

                def body(s, p, live):
                    if live(2):
                        lo_y(s, 0)
                        lo_y(s, 1)
                    if live(1):
                        less_mean(s, 0)
                    if live(0):
                        x_statistics(s, p)
                    if live(1):
                        less_mean(s, 1)
                    if live(2):
                        lo_y(s, 2)
                    if live(1):
                        dve.wait_ge(y_norm, count(s - 1, 11, Y_LESS))
                        for o in range(O):
                            dve.bn_stats(bsy[:, o], yr[:, :, o * HD:(o + 1) * HD]).then_inc(y_norm, 1)
                        dve.wait_ge(y_norm, count(s - 1, 11, Y_LESS + O))
                        dve.sem_inc(k["settled"], 1)
                        for o in range(O):
                            dve.bn_aggr(mv[:, o], bsy[:, o]).then_inc(y_norm, 1)
                        dve.wait_ge(y_norm, count(s - 1, 11, Y_AGG))
                        dve.tensor_scalar(sy[:, 0], mv[:, :, 1], sx[:, 1 - p, 2:3], EPS, ALU.mult, ALU.add).then_inc(y_norm, 1)
                        dve.wait_ge(y_norm, count(s - 1, 11, Y_VAR))
                        dve.reciprocal(sy[:, 4], sy[:, 0]).then_inc(y_norm, 1)
                        dve.wait_ge(y_norm, count(s - 1, 11, Y_INV))
                        dve.tensor_scalar(sy[:, 1], sy[:, 4], sx[:, 1 - p, 2:3], None, ALU.mult).then_inc(y_norm, 1)
                        dve.wait_ge(rr_ok, count(s - 1, 1, 1))
                        dve.scalar_tensor_tensor(sy[:, 3], mv[:, :, 0], -1.0, sy[:, 2], ALU.mult, ALU.mult)\
                           .then_inc(sh_ok, 1)
                    if live(2):
                        dve.wait_ge(qkv_mm, count(s - 2, 3, 2))
                        if (s - 3).exists():
                            dve.wait_ge(rot, count(s - 3, 1, 1))
                        src = psQ[:, 0:2].rearrange("p s (n j) -> p (s n) j", j=HD2)
                        cos = cosT[:].rearrange("p t j -> p (t j)")[:, ds((s - 2).at(HD2), HD2)]
                        sin = sinT[:].rearrange("p t s j -> p (t s j)")[:, ds((s - 2).at(HD), HD)]
                        dve.tensor_tensor(ra[:].rearrange("p (n j) -> p n j", j=HD2), src,
                                          spread(cos.unsqueeze(1), P, 2 * 2 * NH, HD2), ALU.mult).then_inc(rot_ab, 1)
                        swapped = psQ[:, 0:2].rearrange("p s (n x j) -> p (s n) x j", x=2, j=HD2)[:, :, ::-1, :]
                        dve.tensor_tensor(rb[:].rearrange("p (n x j) -> p n x j", x=2, j=HD2), swapped,
                                          spread(sin.rearrange("p (x j) -> p x j", x=2).unsqueeze(1),
                                                 P, 2 * NH, 2, HD2), ALU.mult).then_inc(rot_ab, 1)
                    if live(3):
                        lo_qk(s, 0)
                        lo_qk(s, 1)
                steps(dve, TILES, 3, 2, body)


def build_attention(nc, io, k):
    with ExitStack() as ctx:
        sb, ps, sem = allocators(nc, ctx, "s2_")
        RING = 4
        K3 = 3 * HD
        KM_ = K3 + 2
        qa = sb("a_q", [P, RING, L], F32R)
        ka = sb("a_k", [P, RING, L], F32R)
        base = [sum((QT - j) * P for j in range(ki)) for ki in range(QT + 1)]
        pt = sb("a_p", [P, 2, base[QT]])
        mx = sb("a_mx", [P, 12])
        mhl = sb("a_mhl", [P, 2, QT])
        mt = sb("a_mt", [2 * QT, P])
        rc = sb("a_rc", [P, QT])
        psS = [ps(f"psS{i}", [P, 512]) for i in range(2)]
        psX = [ps(f"psX{i}", [P, 512]) for i in range(3)]
        psO = ps("psO", [P, 2, 512])
        psM = ps("psM", [P, 512])

        units = []
        for qi in range(QT):
            end = (qi + 1) * P
            units += [(qi, a, min(end, a + 512) - a) for a in range(0, end, 512)]
        unitsT = []
        for ki in range(QT):
            a = ki * P
            while a < L:
                e = min(L, (a // 512 + 1) * 512)
                unitsT.append((ki, a, e - a))
                a = e
        U = len(units)
        assert U == len(unitsT) == 12
        halves = [u for u, (qi, a, n) in enumerate(units) if a]
        mcol = {u: (qi if a == 0 else QT + qi - 4) for u, (qi, a, n) in enumerate(units)}

        in_ = [sem(f"a_in{i}") for i in range(RING)]
        ones_ok = sem("a_ones")
        s_mm, mx_ok = sem("s_mm"), sem("mx_ok")
        m_ok = sem("m_ok")
        mt_mm, mt_ok, m_in = sem("mt_mm"), sem("mt_ok"), sem("m_in")
        x_mm, exp_ok = sem("x_mm"), sem("exp_ok")
        av_mm, rc_ok, o_ok = sem("av_mm"), sem("rc_ok"), sem("o_ok")

        with nc.Block() as block:
            @block.sync
            def _(sp):
                def body(s, p, live):
                    if live(2):
                        sp.wait_ge(mt_ok, count(s - 2, 1, 1))
                        sp.sem_inc(k["settled"], 1)
                        slot = (s.off - 2) % RING
                        for hl in range(2):
                            sp.dma_start(qa[K3 + hl:K3 + hl + 1, slot, :].bitcast(F32).rearrange("o (q j) -> o q j", j=P),
                                         mt[hl * QT:(hl + 1) * QT, :]).then_inc(m_in, 16)
                    if live(0):
                        if (s - 4).exists():
                            sp.wait_ge(x_mm, count(s - 4, U, U))
                        sp.sem_inc(k["settled"], 1)
                        rows = ds(s.at(HD), HD)
                        for dst, parts in ((qa, ((0, 0), (0, 0), (0, 1))), (ka, ((1, 0), (1, 1), (1, 0)))):
                            for j, (side, hl) in enumerate(parts):
                                sp.dma_start(dst[j * HD:(j + 1) * HD, p, :].bitcast(F32),
                                             io["qkT"][side, hl, rows, :]).then_inc(in_[p], 16)
                steps(sp, HEADS, 2, RING, body)

            @block.gpsimd
            def _(pool):
                pool.memset(ka[K3:KM_, :, :].bitcast(F32), 1.0).then_inc(ones_ok, 1)

            @block.tensor
            def _(pe):
                def scores(s, p, u):
                    qi, a, n = units[u]
                    if u == 0:
                        pe.wait_ge(in_[p], dma_count(s, RING, 6))
                    if due(s, U, u - 1):
                        pe.wait_ge(mx_ok, count(s, U, u - 1))
                    out = psS[u % 2]
                    diag = a + n == (qi + 1) * P
                    mm = pe.matmul(out[:, 0:n], qa[0:K3, p, qi * P:(qi + 1) * P], ka[0:K3, p, a:a + n],
                                   start=True, stop=not diag)
                    if diag:
                        mm = pe.matmul(out[:, n - P:n], k["ident_b"][:], k["mask_b"][:], start=False, stop=True)
                    mm.then_inc(s_mm, 1)

                def turn_max(s):
                    pe.wait_ge(m_ok, count(s - 1, 3, 3))
                    if (s - 2).exists():
                        pe.wait_ge(mt_ok, count(s - 2, 1, 1))
                    pe.transpose(psM[0:2 * QT, 0:P], mhl[:].rearrange("p h q -> p (h q)"), k["ident"][:])\
                      .then_inc(mt_mm, 1)

                def scoresT(s, slot, u):
                    ki, a, n = unitsT[u]
                    if u == 0:
                        pe.wait_ge(m_in, dma_count(s - 1, 1, 2))
                    if due(s - 1, U, u - 2):
                        pe.wait_ge(exp_ok, count(s - 1, U, u - 2))
                    out = psX[u % 3]
                    diag = a == ki * P
                    mm = pe.matmul(out[:, 0:n], ka[0:KM_, slot, ki * P:(ki + 1) * P], qa[0:KM_, slot, a:a + n],
                                   start=True, stop=not diag)
                    if diag:
                        mm = pe.matmul(out[:, 0:P], k["ident_b"][:], k["maskT_b"][:], start=False, stop=True)
                    mm.then_inc(x_mm, 1)

                def values(s, p, qi):
                    if qi == 0:
                        pe.wait_ge(exp_ok, count(s - 2, U, U))
                    if qi % 4 == 0:
                        if (s - 3).exists():
                            pe.wait_ge(o_ok, count(s - 3, 2, qi // 4 + 1))
                    out = psO[:, qi // 4, qi % 4 * VN:(qi % 4 + 1) * VN]
                    for ki in range(qi + 1):
                        at = base[ki] + (qi - ki) * P
                        mm = pe.matmul(out, pt[:, p, at:at + P],
                                       k["v_flat"][:, ds((s - 2).at(QT * (HD + 1), ki * (HD + 1)), VN)],
                                       start=(ki == 0), stop=(ki == qi))
                    if qi % 4 == 3:
                        mm.then_inc(av_mm, 1)

                pe.wait_ge(ones_ok, 1)

                def body(s, slot, live):
                    S = (lambda u: scores(s, slot, u)) if live(0) else (lambda u: None)
                    X = (lambda u: scoresT(s, (slot - 1) % RING, u)) if live(1) else (lambda u: None)
                    V = (lambda qi: values(s, slot % 2, qi)) if live(2) else (lambda qi: None)
                    S(0), V(0), S(1), V(1)
                    if live(1):
                        turn_max(s)
                    V(2), S(2), V(3), S(3), V(4)
                    for u in range(U):
                        X(u)
                        if u + 4 < U:
                            S(u + 4)
                        if u in (2, 5, 8):
                            V(5 + u // 3)
                steps(pe, HEADS, 2, RING, body)

            @block.vector
            def _(dve):
                def normalise(s, half):
                    dve.wait_ge(av_mm, count(s - 2, 2, half + 1))
                    view = psO[:, half, 0:4 * VN].rearrange("p (q n) -> p q n", n=VN)
                    dve.reciprocal(rc[:, 4 * half:4 * half + 4], view[:, :, HD]).then_inc(rc_ok, 1)
                    dve.wait_ge(rc_ok, count(s - 2, 2, half + 1))
                    at = (s - 2).at(QT * HD, 4 * half * HD)
                    out = k["o_sb"][:].rearrange("p n t d -> p (n t d)")[:, ds(at, 4 * HD)]
                    dve.tensor_tensor(out.rearrange("p (q d) -> p q d", d=HD), view[:, :, 0:HD],
                                      spread(rc[:, 4 * half:4 * half + 4].unsqueeze(2), P, 4, HD), ALU.mult)\
                       .then_inc(o_ok, 1)

                def body(s, slot, live):
                    for u in range(U):
                        if u == 4 and live(2):
                            normalise(s, 0)
                        if live(0):
                            qi, a, n = units[u]
                            dve.wait_ge(s_mm, count(s, U, u + 1))
                            if u == 0:
                                if (s - 1).exists():
                                    dve.wait_ge(m_ok, count(s - 1, 3, 3))
                            dve.tensor_reduce(mx[:, mcol[u]:mcol[u] + 1], psS[u % 2][:, 0:n], AX, ALU.max)\
                               .then_inc(mx_ok, 1)
                    if live(0):
                        dve.wait_ge(mx_ok, count(s, U, U))
                        dve.tensor_tensor(mx[:, 4:8], mx[:, 4:8], mx[:, 8:12], ALU.max).then_inc(m_ok, 1)
                        dve.wait_ge(m_ok, count(s, 3, 1))
                        if (s - 1).exists():
                            dve.wait_ge(mt_mm, count(s - 1, 1, 1))
                        dve.tensor_scalar(mhl[:, 0].bitcast(F32R), mx[:, 0:QT], -1.0, None, ALU.mult).then_inc(m_ok, 1)
                        dve.wait_ge(m_ok, count(s, 3, 2))
                        dve.scalar_tensor_tensor(mhl[:, 1].bitcast(F32R), mx[:, 0:QT], -1.0, mhl[:, 0], ALU.mult,
                                                 ALU.subtract).then_inc(m_ok, 1)
                    if live(2):
                        normalise(s, 1)
                steps(dve, HEADS, 2, RING, body)

            @block.scalar
            def _(act):
                def body(s, slot, live):
                    if live(1):
                        act.wait_ge(mt_mm, count(s - 1, 1, 1))
                        if (s - 2).exists():
                            act.wait_ge(m_in, dma_count(s - 2, 1, 2))
                        act.activation(mt[:].bitcast(F32R), psM[0:2 * QT, 0:P], ACT.Copy).then_inc(mt_ok, 1)
                        for u, (ki, a, n) in enumerate(unitsT):
                            act.wait_ge(x_mm, count(s - 1, U, u + 1))
                            if u == 0:
                                if (s - 3).exists():
                                    act.wait_ge(av_mm, count(s - 3, 2, 2))
                            at = base[ki] + a - ki * P
                            act.activation(pt[:, (slot - 1) % 2, at:at + n], psX[u % 3][:, 0:n], ACT.Exp,
                                           scale=float(1 / np.sqrt(np.float32(HD)))).then_inc(exp_ok, 1)
                steps(act, HEADS, 2, RING, body)


def build_write(nc, io, k, first):
    tag = "s3_" if first else "s5_"
    KY = KH if first else KM
    HW = H // 2
    S0 = DR + 1
    SA, SB, SK = slice(S0, S0 + NA), slice(S0 + NA, S0 + 2 * NA), slice(S0 + 2 * NA, S0 + 2 * NA + RH)
    WA, WB = HW + DR + NA, HW + NA + RH
    with ExitStack() as ctx:
        sb, ps, sem = allocators(nc, ctx, tag)
        wh = sb("w_wh", [P, KY, NW], F32R)
        wl = sb("w_wl", [P, KY, NW], F32R)
        bsm = sb("w_bsm", [P, DR + NAB])
        du = sb("w_du", [S0, H])
        one_c = sb("w_one", [P, 1])
        eps_c = sb("w_eps", [P, 1])
        sm = sb("w_sm", [P, 2, S0 + NAB])
        if first:
            spf = sb("w_spf", [P, KD * 2 * HD + HD])
        else:
            fbias = sb("w_fb", [P, D])
        psA, psB, psD, psL = (ps(n, [P, 512]) for n in ("w_psA", "w_psB", "w_psD", "w_psL"))
        psT = [ps(f"w_psT{i}", [P, 4, P]) for i in range(2)]
        if first:
            psR = ps("w_psR", [P, 2, 512])

        with ExitStack() as c:
            sb, _, sem = allocators(nc, c, tag)
            wraw = sb("w_raw", [P, KH, NW])
            w_in, small_in, w_hi, w_lo = (sem(n) for n in ("w_in", "small_in", "w_hi", "w_lo"))
            if first:
                prep = sem("prep")
                rw = sb("w_rw", [P, KD, 2])
                m32 = sb("w_m32", [P, HD])
            name = "1" if first else "2"
            parts = KY // KH
            with nc.Block() as block:
                @block.sync
                def _(sp):
                    sp.dma_start(bsm[:], io["bsm" + name]).then_inc(small_in, 16)
                    sp.dma_start(du[:], io["du" + name]).then_inc(small_in, 16)
                    if first:
                        sp.dma_start(rw[:], io["wr2"]).then_inc(small_in, 16)
                    else:
                        sp.dma_start(fbias[:], io["fbias"]).then_inc(small_in, 16)
                    for i in range(parts):
                        if i:
                            sp.wait_ge(w_lo, i)
                        sp.dma_start(wraw[:], io["wo" + name][:, i * KH:(i + 1) * KH]).then_inc(w_in, 16)
                    sp.wait_ge(small_in, 48)

                @block.scalar
                def _(act):
                    for i in range(parts):
                        act.wait_ge(w_in, 16 * (i + 1))
                        act.activation(wh[:, i * KH:(i + 1) * KH], wraw[:], ACT.Copy).then_inc(w_hi, 1)

                @block.vector
                def _(dve):
                    dve.memset(one_c[:], 1.0)
                    dve.memset(eps_c[:], EPS)
                    dve.memset(sm[:, :, DR:S0], 1.0)
                    if first:
                        dve.wait_ge(small_in, 48)
                        dve.memset(spf[:, 0:HD], 0.0)
                        dve.tensor_reduce(m32[:], k["ident"][:].rearrange("p (c j) -> p j c", c=C), AX, ALU.max)\
                           .then_inc(prep, 1)
                        dve.wait_ge(prep, 1)
                        dve.tensor_tensor(spf[:, HD:].rearrange("p (t j) -> p t j", j=HD),
                                          spread(rw[:].rearrange("p t o -> p (t o)").unsqueeze(2), P, KD * 2, HD),
                                          spread(m32[:].unsqueeze(1), P, KD * 2, HD), ALU.mult)
                    for i in range(parts):
                        dve.wait_ge(w_hi, i + 1)
                        part = slice(i * KH, (i + 1) * KH)
                        dve.tensor_tensor(wl[:, part], wraw[:], wh[:, part], ALU.subtract).then_inc(w_lo, 1)

        sb, ps, sem = allocators(nc, ctx, tag)
        yraw = sb("w_y", [P, 1 if first else 2, KY, P])
        yh = sb("w_yh", [P, KY, P], F32R)
        yl = sb("w_yl", [P, KY, P], F32R)
        hin = sb("w_hin", [P, D])
        hs = sb("w_hs", [P, D]) if first else None
        xin = None if first else sb("w_xin", [P, D])
        outs = sb("w_out", [P, 2, H])
        sp_ = sb("w_sp", [P, H + NA])
        delta = sb("w_delta", [P, H])
        gate = sb("w_gate", [P, 3, NA])
        ab = sb("w_ab", [P, C - 1, H])
        g = sb("w_g", [P, C - 1, H])
        ha = sb("w_ha", [P, C - 1, H])
        sk = sb("w_sk", [P, H])
        res = sb("w_res", [P, 2 if first else 1, D])
        hT = sb("w_hT", [P, KD, P])
        dlT = sb("w_dlT", [S0, P])
        st = sb("w_st", [P, 4])
        if first:
            yn = sb("w_yn", [P, 2, H])
            gT = sb("w_gT", [P, 2, KH, P])
            nst = sb("w_nst", [P, 2, 6])
            nmv = sb("w_nmv", [P, 2, 2])
            nsc = sb("w_nsc", [P, 3, 2])
        else:
            xn = sb("w_xn", [P, D])
            xb = sb("w_xb", [P, D])
            nst = sb("w_nst", [P, 4, 6])
            nsc = sb("w_nsc", [P, 1])

        if first:
            o_ok, o_mm = sem("o_ok"), sem("o_mm")
            hs_ok = sem("hs_ok")
            r_mm, n_e = sem("r_mm"), sem("n_e")
            nrm_ok = sem("nrm_ok")
            g_mm, g_ev, g_ev2 = sem("g_mm"), sem("g_ev"), sem("g_ev2")
        else:
            y_in = [sem(f"y_in{p}") for p in range(2)]
            xn_ok, xb_ok = sem("xn_ok"), sem("xb_ok")
        h_in = [sem(f"h_in{p}") for p in range(2)]
        y_hi, y_lo = sem("y_hi"), sem("y_lo")
        ab_mm = sem("ab_mm")
        sm_ok, out_ok = sem("sm_ok"), sem("out_ok")
        dl_mm, dl_ok, d_mm = sem("dl_mm"), sem("dl_ok"), sem("d_mm")
        sp_e = sem("sp_e")
        gate_e = sem("gate_e")
        g_ok, skip_e = sem("g_ok"), sem("skip_e")
        bar_ok, ha_ok = sem("bar_ok"), sem("ha_ok")
        b_ok = sem("b_ok")
        res_e = sem("res_e")
        R = 2 if first else 3
        st_e, sc_ok = sem("st_e"), sem("sc_ok")
        t_mm, t_ev = sem("t_mm"), sem("t_ev")
        t_ev2 = sem("t_ev2")
        ln_e = sem("ln_e")
        st_out = [sem(f"st_out{p}") for p in range(2 if first else 1)]
        t_out = sem("t_out")
        NE = 7

        def place(tile):
            n = tile.at()
            return n // QT, n % QT

        def planes(ap, blocks=False):
            return ap.rearrange("p (t c j) -> p c t j" if blocks else "p (c t j) -> p c t j", c=C, j=HD)

        def cells(ap):
            return ap.rearrange("p c (t j) -> p c t j", j=HD)

        LAST = 4 if first else 3
        with nc.Block() as block:
            @block.sync
            def _(sp):
                def body(s, p, live):
                    if live(0) and not first:
                        if (s - 2).exists():
                            sp.wait_ge(y_lo, count(s - 2, 2, 2))
                        sp.sem_inc(k["settled"], 1)
                        sp.dma_start(yraw[:, p].rearrange("p t j -> p (t j)"),
                                     io["mlpT"][ds(s.at(), 1)].rearrange("o p f -> (o p) f"))\
                          .then_inc(y_in[p], 16)
                    if live(1):
                        q = 1 - p
                        if first:
                            if (s - 2).exists():
                                sp.wait_ge(hs_ok, count(s - 2, 1, 1))
                        else:
                            if (s - 2).exists():
                                sp.wait_ge(res_e, count(s - 2, R, R))
                        sp.sem_inc(k["settled"], 1)
                        sp.dma_start(hin[:], io["xP" if first else "hs2"][ds((s - 1).at(P), P), :])\
                          .then_inc(h_in[q], 16)
                        if not first:
                            sp.dma_start(xin[:], io["xP"][ds((s - 1).at(P), P), :]).then_inc(h_in[q], 16)
                    if live(3):
                        q = 1 - p
                        if first:
                            sp.wait_ge(res_e, count(s - 3, R, R))
                            sp.sem_inc(k["settled"], 1)
                            sp.dma_start(io["hs2"][ds((s - 3).at(P), P), :], res[:, q]).then_inc(st_out[q], 16)
                        else:
                            sp.wait_ge(xb_ok, count(s - 3, 1, 1))
                            sp.sem_inc(k["settled"], 1)
                            sp.dma_start(io["xb"][ds((s - 3).at(P), P), :], xb[:]).then_inc(st_out[0], 16)
                    d = LAST + 1
                    if live(d):
                        ev, ev2, buf, name = (g_ev, g_ev2, gT, "giT") if first else (t_ev, t_ev2, hT, "xnT")
                        n = 1 if first else 2
                        sp.wait_ge(ev, count(s - d, n, n))
                        sp.sem_inc(k["settled"], 1)
                        sp.wait_ge(ev2, count(s - d, n, n))
                        sp.sem_inc(k["settled"], 1)
                        src = buf[:].rearrange("p o t j -> p (o t j)") if first else buf[:].rearrange("p t j -> p (t j)")
                        sp.dma_start(io[name][ds((s - d).at(), 1)].rearrange("o p f -> (o p) f"), src)\
                          .then_inc(t_out, 16)
                steps(sp, TILES, LAST + 1, 2, body, LAST + 1)
                sp.wait_ge(t_out, 16 * TILES)
                for out in st_out:
                    sp.wait_ge(out, 16 * TILES // len(st_out))

            @block.tensor
            def _(pe):
                def bank_free(s, bank, j):
                    if j < 2:
                        if first:
                            if bank == 0:
                                pe.wait_ge(y_hi, count(s - 1, 2, 2))
                                pe.wait_ge(y_lo, count(s - 1, 2, 2))
                                if (s - 5).exists():
                                    pe.wait_ge(g_ev, count(s - 5, 1, 1))
                            else:
                                if (s - 5).exists():
                                    pe.wait_ge(g_ev2, count(s - 5, 1, 1))
                        else:
                            if (s - 4).exists():
                                pe.wait_ge(t_ev if bank == 0 else t_ev2, count(s - 4, 2, 2))
                    else:
                        pe.wait_ge(t_ev if bank == 0 else t_ev2, count(s - 3, 2, 1))

                def turn_residual(s, p):
                    src = res[:, 1 - p] if first else xn[:]
                    if first:
                        pe.wait_ge(res_e, count(s - 3, R, R))
                    else:
                        pe.wait_ge(xn_ok, count(s - 3, 1, 1))
                    for j in range(4):
                        bank_free(s, j % 2, j)
                        for i in range(4):
                            kt = 4 * j + i
                            mm = pe.transpose(psT[j % 2][:, i], src[:, kt * P:(kt + 1) * P], k["ident"][:])
                        mm.then_inc(t_mm, 1)

                def read(s):
                    if (s - 4).exists():
                        pe.wait_ge(n_e, count(s - 4, NE, 2))
                    if (s - 4).exists():
                        pe.wait_ge(nrm_ok, count(s - 4, 2, 2))
                    pe.wait_ge(t_ev, count(s - 3, 2, 2))
                    pe.wait_ge(t_ev2, count(s - 3, 2, 2))
                    for half in range(2):
                        for i in reversed(range(8)):
                            kt = 8 * half + i
                            lead = HD if i else 0
                            mm = pe.matmul(psR[:, half, i * 2 * HD - lead:(i + 1) * 2 * HD], hT[:, kt],
                                           spf[:, HD + kt * 2 * HD - lead:HD + (kt + 1) * 2 * HD],
                                           start=True, stop=True)
                    mm.then_inc(r_mm, 1)

                def product(s):
                    if (s - 2).exists():
                        pe.wait_ge(sm_ok, count(s - 2, 2, 2))
                    if (s - 2).exists():
                        pe.wait_ge(out_ok, count(s - 2, 2, 2))
                    for kt in range(KY):
                        if kt % (KY // 2) == 0:
                            pe.wait_ge(y_hi, count(s - 1, 2, kt // (KY // 2) + 1))
                            pe.wait_ge(y_lo, count(s - 1, 2, kt // (KY // 2) + 1))
                        for a, b in ((yh, wh), (yh, wl), (yl, wh)):
                            for bank, cols in ((psA, slice(0, WA)), (psB, slice(WA, NW))):
                                mm = pe.matmul(bank[:, 0:cols.stop - cols.start], a[:, kt], b[:, kt, cols],
                                               start=(kt == 0 and b is wh and a is yh), stop=(kt == KY - 1 and a is yl))
                        if kt % (KY // 2) == KY // 2 - 1:
                            mm.then_inc(ab_mm, 1)

                def body(s, p, live):
                    if live(1):
                        product(s)
                        pe.wait_ge(sm_ok, count(s - 1, 2, 1))
                        if (s - 2).exists():
                            pe.wait_ge(dl_ok, count(s - 2, 1, 1))
                        pe.transpose(psL[0:S0, 0:P], sm[:, 1 - p, 0:S0], k["ident"][:]).then_inc(dl_mm, 1)
                    if live(3):
                        turn_residual(s, p)
                    if live(1):
                        pe.wait_ge(dl_ok, count(s - 1, 1, 1))
                        if (s - 2).exists():
                            pe.wait_ge(gate_e, count(s - 2, 6, 1))
                        pe.matmul(psD[:], dlT[:], du[:], start=True, stop=True).then_inc(d_mm, 1)
                    if live(4) and first:
                        for o in range(2):
                            pe.wait_ge(nrm_ok, count(s - 4, 2, o + 1))
                            pe.wait_ge(t_ev if o == 0 else t_ev2, count(s - 3, 2, 2))
                            if not live(3):
                                pe.wait_ge(g_ev if o == 0 else g_ev2, count(s - 5, 1, 1))
                            for c in range(KH):
                                mm = pe.transpose(psT[o][:, c], yn[:, o, c * P:(c + 1) * P], k["ident"][:])
                            mm.then_inc(g_mm, 1)
                    if live(3) and first:
                        read(s)
                    if live(0) and first:
                        pe.wait_ge(o_ok, count(s, 1, 1))
                        if (s - 4).exists():
                            pe.wait_ge(g_ev, count(s - 4, 1, 1))
                        if not live(4):
                            if (s - 3).exists():
                                pe.wait_ge(t_ev, count(s - 3, 2, 2))
                            if (s - 1).exists():
                                pe.wait_ge(y_hi, count(s - 1, 2, 2))
                            if (s - 1).exists():
                                pe.wait_ge(y_lo, count(s - 1, 2, 2))
                        for c in range(KH):
                            mm = pe.transpose(psT[0][:, c], yraw[:, 0, c], k["ident"][:])
                        mm.then_inc(o_mm, 1)
                steps(pe, TILES, LAST, 2, body, LAST + 1)

            @block.scalar
            def _(act):
                def hi_y(s, p, half):
                    part = slice(half * KY // 2, (half + 1) * KY // 2)
                    if (s - 1).exists():
                        act.wait_ge(ab_mm, count(s - 1, 2, half + 1))
                    if half == 0 and first:
                        act.wait_ge(o_mm, count(s, 1, 1))
                    if half == 0 and not first:
                        act.wait_ge(y_in[p], dma_count(s, 2, 1))
                    src = psT[0][:, part] if first else yraw[:, p, part]
                    act.activation(yh[:, part], src, ACT.Copy).then_inc(y_hi, 1)

                def body(s, p, live):
                    q = p
                    if live(4) and first:
                        act.wait_ge(n_e, count(s - 4, NE, 4))
                        act.activation(nsc[:, 0], nmv[:, :, 1], ACT.Ln, bias=eps_c[:]).then_inc(n_e, 1)
                        act.wait_ge(n_e, count(s - 4, NE, 5))
                        act.activation(nsc[:, 1], nsc[:, 0], ACT.Exp, scale=-0.5).then_inc(n_e, 1)
                    if live(2):
                        act.wait_ge(d_mm, count(s - 2, 1, 1))
                        if (s - 3).exists():
                            act.wait_ge(gate_e, count(s - 3, 6, 2))
                        act.activation(sp_[:, 0:H], psD[:], ACT.Abs).then_inc(sp_e, 1)
                        act.wait_ge(sm_ok, count(s - 2, 2, 1))
                        act.activation(sp_[:, H:], sm[:, q, SA], ACT.Abs).then_inc(sp_e, 1)
                        act.wait_ge(sp_e, count(s - 2, 4, 2))
                        act.activation(sp_[:], sp_[:], ACT.Exp, scale=-1.0).then_inc(sp_e, 1)
                        act.wait_ge(sp_e, count(s - 2, 4, 3))
                        act.activation(sp_[:], sp_[:], ACT.Ln, bias=one_c[:]).then_inc(sp_e, 1)
                        if first:
                            act.wait_ge(st_e, count(s - 2, 1, 1))
                            act.activation(st[:, 3:4], st[:, 1:2], ACT.Ln, bias=eps_c[:]).then_inc(ln_e, 1)
                            act.wait_ge(ln_e, count(s - 2, 2, 1))
                            act.activation(st[:, 2:3], st[:, 3:4], ACT.Exp, scale=-0.5).then_inc(ln_e, 1)
                            act.wait_ge(sc_ok, count(s - 2, 1, 1))
                            act.wait_ge(h_in[q], dma_count(s - 2, 2, 1))
                            if (s - 3).exists():
                                act.wait_ge(ha_ok, count(s - 3, 1, 1))
                            if (s - 3).exists():
                                act.wait_ge(res_e, count(s - 3, R, 2))
                            act.activation(hs[:], hin[:], ACT.Identity, scale=st[:, 2:3], bias=st[:, 0:1])\
                               .then_inc(hs_ok, 1)
                    if live(4) and first:
                        act.wait_ge(n_e, count(s - 4, NE, 7))
                        if (s - 5).exists():
                            act.wait_ge(g_mm, count(s - 5, 2, 2))
                        for o in range(2):
                            act.activation(yn[:, o].rearrange("p (b t j) -> p b t j", b=2, j=HD),
                                           psR[:].rearrange("p b (t o j) -> p b t o j", o=2, j=HD)[:, :, :, o],
                                           ACT.Identity, scale=nsc[:, 1, o:o + 1], bias=nsc[:, 2, o:o + 1])\
                               .then_inc(nrm_ok, 1)
                    if live(2):
                        act.wait_ge(gate_e, count(s - 2, 6, 6))
                        act.activation(ab[:], ab[:], ACT.Exp).then_inc(bar_ok, 1)
                    if live(0) and not first:
                        hi_y(s, p, 0)
                    if live(1):
                        act.wait_ge(ab_mm, count(s - 1, 2, 2))
                        if (s - 3).exists():
                            act.wait_ge(g_ok, count(s - 3, 1, 1))
                        if (s - 3).exists():
                            act.wait_ge(skip_e, count(s - 3, 2, 2))
                        act.wait_ge(sm_ok, count(s - 1, 2, 1))
                        act.activation(outs[:, 1 - p, 0:HW], psA[:, 0:HW], ACT.Copy).then_inc(out_ok, 1)
                        act.wait_ge(sm_ok, count(s - 1, 2, 2))
                        act.activation(outs[:, 1 - p, HW:H], psB[:, 0:HW], ACT.Copy).then_inc(out_ok, 1)
                        act.wait_ge(dl_mm, count(s - 1, 1, 1))
                        if (s - 2).exists():
                            act.wait_ge(d_mm, count(s - 2, 1, 1))
                        act.activation(dlT[:], psL[0:S0, 0:P], ACT.Copy).then_inc(dl_ok, 1)
                    if live(0) and not first:
                        hi_y(s, p, 1)
                    if live(3):
                        for j in (0, 2):
                            act.wait_ge(t_mm, count(s - 3, 4, j + 1))
                            if first:
                                if (s - 4).exists():
                                    act.wait_ge(r_mm, count(s - 4, 1, 1))
                            else:
                                if (s - 4).exists():
                                    act.wait_ge(t_out, dma_count(s - 4, 1, 1))
                            act.activation(hT[:, 4 * j:4 * j + 4], psT[0][:], ACT.Copy).then_inc(t_ev, 1)
                    if live(4) and first:
                        act.wait_ge(g_mm, count(s - 4, 2, 1))
                        if (s - 5).exists():
                            act.wait_ge(t_out, dma_count(s - 5, 1, 1))
                        act.activation(gT[:, 0], psT[0][:], ACT.Copy).then_inc(g_ev, 1)
                    if live(0) and first:
                        b_, kt_ = place(s)
                        if (s - 1).exists():
                            act.wait_ge(o_mm, count(s - 1, 1, 1))
                        src = k["o_sb"][:].rearrange("p (b n) t d -> p b n t d", b=B)
                        src = src[:, ds(b_, 1), :, ds(kt_, 1), :].rearrange("p b n t d -> p (b n) (t d)")
                        act.activation(yraw[:, 0].rearrange("p t (n d) -> p (t n) d", d=HD), src, ACT.Copy)\
                           .then_inc(o_ok, 1)
                        hi_y(s, p, 0)
                        hi_y(s, p, 1)
                    if live(2) and not first:
                        act.wait_ge(st_e, count(s - 2, 5, 5))
                        act.activation(nsc[:], st[:, 1:2], ACT.Ln, bias=eps_c[:]).then_inc(ln_e, 1)
                        act.wait_ge(ln_e, count(s - 2, 2, 1))
                        act.activation(st[:, 2:3], nsc[:], ACT.Exp, scale=-0.5).then_inc(ln_e, 1)
                        act.wait_ge(sc_ok, count(s - 2, 1, 1))
                        if (s - 3).exists():
                            act.wait_ge(t_mm, count(s - 3, 4, 4))
                        act.activation(xn[:], res[:, 0], ACT.Identity, scale=st[:, 2:3], bias=st[:, 3:4])\
                           .then_inc(xn_ok, 1)
                steps(act, TILES, LAST, 2, body, LAST + 1)

            @block.gpsimd
            def _(pool):
                def body(s, p, live):
                    q = p
                    if live(2):
                        pool.wait_ge(gate_e, count(s - 2, 6, 1))
                        if (s - 3).exists():
                            pool.wait_ge(res_e, count(s - 3, R, 2))
                        pool.tensor_tensor(sk[:].rearrange("p (s r) -> p s r", r=RH),
                                           delta[:].rearrange("p (s r) -> p s r", r=RH),
                                           spread(sm[:, q, SK].unsqueeze(1), P, HS, RH), ALU.mult).then_inc(skip_e, 1)
                        pool.wait_ge(gate_e, count(s - 2, 6, 5))
                        pool.wait_ge(out_ok, count(s - 2, 2, 2))
                        for c in range(C - 1):
                            mm = pool.tensor_tensor(
                                g[:, c].rearrange("p (s r) -> p s r", r=RH),
                                outs[:, q].rearrange("p (s r) -> p s r", r=RH),
                                spread(gate[:, 2].rearrange("p (r c) -> p c r", c=C - 1)[:, c:c + 1], P, HS, RH), ALU.mult)
                        mm.then_inc(g_ok, 1)
                        pool.wait_ge(skip_e, count(s - 2, 2, 1))
                        pool.tensor_tensor(sk[:], sk[:], outs[:, q], ALU.mult).then_inc(skip_e, 1)
                        pool.wait_ge(bar_ok, count(s - 2, 1, 1))
                        if first:
                            pool.wait_ge(hs_ok, count(s - 2, 1, 1))
                            src = planes(hs[:])
                        else:
                            pool.wait_ge(h_in[q], dma_count(s - 2, 2, 2))
                            src = planes(hin[:], blocks=True)
                        pool.tensor_tensor(cells(ha[:]), cells(ab[:]), src[:, 0:C - 1], ALU.mult).then_inc(ha_ok, 1)
                        if not first:
                            pool.wait_ge(res_e, count(s - 2, R, R))
                            if (s - 3).exists():
                                pool.wait_ge(st_out[0], dma_count(s - 3, 1, 1))
                            pool.tensor_tensor(xb[:], res[:, 0], fbias[:], ALU.add).then_inc(xb_ok, 1)
                steps(pool, TILES, LAST, 2, body, LAST + 1)

            @block.vector
            def _(dve):
                lin = k["ln1"][:].rearrange("p t s -> p (t s)")

                def gates(s, q):
                    dve.wait_ge(sp_e, count(s - 2, 4, 4))
                    if (s - 3).exists():
                        dve.wait_ge(g_ok, count(s - 3, 1, 1))
                    if (s - 3).exists():
                        dve.wait_ge(skip_e, count(s - 3, 2, 1))
                    dve.scalar_tensor_tensor(delta[:], psD[:], 0.0, sp_[:, 0:H], ALU.max, ALU.add).then_inc(gate_e, 1)
                    dve.scalar_tensor_tensor(gate[:, 1], sm[:, q, SA], 0.0, sp_[:, H:], ALU.max, ALU.add)\
                       .then_inc(gate_e, 1)
                    dve.wait_ge(gate_e, count(s - 2, 6, 2))
                    dve.tensor_scalar(gate[:, 0], gate[:, 1], -1.0, None, ALU.mult)
                    dve.tensor_scalar(gate[:, 1], gate[:, 1], -1.0, -1e-5, ALU.mult, ALU.add).then_inc(gate_e, 1)
                    dve.wait_ge(gate_e, count(s - 2, 6, 3))
                    dve.reciprocal(gate[:, 1], gate[:, 1]).then_inc(gate_e, 1)
                    dve.wait_ge(gate_e, count(s - 2, 6, 4))
                    dve.tensor_tensor(gate[:, 2], gate[:, 1], sm[:, q, SB], ALU.mult).then_inc(gate_e, 1)
                    if (s - 3).exists():
                        dve.wait_ge(ha_ok, count(s - 3, 1, 1))
                    for c in range(C - 1):
                        mm = dve.tensor_tensor(
                            ab[:, c].rearrange("p (s r) -> p s r", r=RH), delta[:].rearrange("p (s r) -> p s r", r=RH),
                            spread(gate[:, 0].rearrange("p (r c) -> p c r", c=C - 1)[:, c:c + 1], P, HS, RH), ALU.mult)
                    mm.then_inc(gate_e, 1)

                def update(s, q):
                    flat = lambda b: b[:].rearrange("p c h -> p (c h)")
                    dve.wait_ge(bar_ok, count(s - 2, 1, 1))
                    dve.wait_ge(g_ok, count(s - 2, 1, 1))
                    dve.scalar_tensor_tensor(flat(g), flat(ab), -1.0, flat(g), ALU.add, ALU.mult).then_inc(b_ok, 1)
                    dve.wait_ge(skip_e, count(s - 2, 2, 2))
                    if first:
                        if (s - 4).exists():
                            dve.wait_ge(t_mm, count(s - 4, 4, 4))
                        if (s - 4).exists():
                            dve.wait_ge(st_out[q], dma_count(s - 4, 2, 1))
                        row = res[:, q]
                        dst, src = planes(row, blocks=True), planes(hs[:])
                        dve.wait_ge(hs_ok, count(s - 2, 1, 1))
                    else:
                        if (s - 3).exists():
                            dve.wait_ge(xn_ok, count(s - 3, 1, 1))
                        if (s - 3).exists():
                            dve.wait_ge(xb_ok, count(s - 3, 1, 1))
                        row = res[:, 0]
                        dst, src = planes(row), planes(hin[:], blocks=True)
                        dve.wait_ge(h_in[q], dma_count(s - 2, 2, 2))
                    dve.tensor_tensor(dst[:, C - 1], sk[:].rearrange("p (t j) -> p t j", j=HD), src[:, C - 1], ALU.add).then_inc(res_e, 1)
                    dve.wait_ge(ha_ok, count(s - 2, 1, 1))
                    dve.wait_ge(b_ok, count(s - 2, 1, 1))
                    dve.tensor_tensor(dst[:, 0:C - 1], cells(ha[:]), cells(g[:]), ALU.add).then_inc(res_e, 1)
                    if not first:
                        dve.wait_ge(res_e, count(s - 2, R, 2))
                        dve.tensor_tensor(row, row, xin[:], ALU.add).then_inc(res_e, 1)
                        dve.wait_ge(res_e, count(s - 2, R, 3))
                        for j in range(4):
                            dve.bn_stats(nst[:, j], row[:, j * 512:(j + 1) * 512]).then_inc(st_e, 1)
                        dve.wait_ge(st_e, count(s - 2, 5, 4))
                        dve.sem_inc(k["settled"], 1)
                        dve.bn_aggr(st[:, 0:2], nst[:]).then_inc(st_e, 1)

                def lo_y(s, p, half):
                    part = slice(half * KY // 2, (half + 1) * KY // 2)
                    dve.wait_ge(y_hi, count(s, 2, 2 if first else half + 1))
                    src = psT[0][:, part] if first else yraw[:, p, part]
                    dve.tensor_tensor(yl[:, part], src, yh[:, part], ALU.subtract).then_inc(y_lo, 1)

                def body(s, p, live):
                    q = p
                    if live(4) and first:
                        dve.wait_ge(r_mm, count(s - 4, 1, 1))
                        view = psR[:].rearrange("p b (t o j) -> p b t o j", o=2, j=HD)
                        for o in range(2):
                            dve.bn_stats(nst[:, o], view[:, :, :, o]).then_inc(n_e, 1)
                        dve.wait_ge(n_e, count(s - 4, NE, 2))
                        dve.sem_inc(k["settled"], 1)
                        for o in range(2):
                            dve.bn_aggr(nmv[:, o], nst[:, o:o + 1]).then_inc(n_e, 1)
                    if live(2) and first:
                        if (s - 3).exists():
                            dve.wait_ge(hs_ok, count(s - 3, 1, 1))
                        dve.tensor_copy(st[:, 0:2], lin[:, ds((s - 2).at(2), 2)]).then_inc(st_e, 1)
                    if live(4) and first:
                        dve.wait_ge(n_e, count(s - 4, NE, 6))
                        dve.scalar_tensor_tensor(nsc[:, 2], nmv[:, :, 0], -1.0, nsc[:, 1], ALU.mult, ALU.mult)\
                           .then_inc(n_e, 1)
                    if live(2):
                        gates(s, q)
                        if first:
                            dve.wait_ge(ln_e, count(s - 2, 2, 2))
                            dve.scalar_tensor_tensor(st[:, 0:1], st[:, 0:1], -1.0, st[:, 2:3], ALU.mult, ALU.mult)\
                               .then_inc(sc_ok, 1)
                    if live(0) and not first:
                        lo_y(s, p, 0)
                    if live(2) and not first:
                        update(s, q)
                    if live(1):
                        r = 1 - p
                        dve.wait_ge(ab_mm, count(s - 1, 2, 2))
                        dve.tensor_tensor(sm[:, r, 0:DR], psA[:, HW:HW + DR], bsm[:, 0:DR], ALU.add)
                        dve.tensor_tensor(sm[:, r, SA], psA[:, HW + DR:WA], bsm[:, DR:DR + NA], ALU.add)\
                           .then_inc(sm_ok, 1)
                        dve.tensor_tensor(sm[:, r, S0 + NA:], psB[:, HW:WB], bsm[:, DR + NA:], ALU.add).then_inc(sm_ok, 1)
                    if live(0) and not first:
                        lo_y(s, p, 1)
                    if live(2) and not first:
                        dve.wait_ge(ln_e, count(s - 2, 2, 2))
                        dve.scalar_tensor_tensor(st[:, 3:4], st[:, 0:1], -1.0, st[:, 2:3], ALU.mult, ALU.mult)\
                           .then_inc(sc_ok, 1)
                    if live(3):
                        for j in (1, 3):
                            dve.wait_ge(t_mm, count(s - 3, 4, j + 1))
                            if first:
                                if (s - 4).exists():
                                    dve.wait_ge(r_mm, count(s - 4, 1, 1))
                            else:
                                if (s - 4).exists():
                                    dve.wait_ge(t_out, dma_count(s - 4, 1, 1))
                            dve.tensor_copy(hT[:, 4 * j:4 * j + 4], psT[1][:]).then_inc(t_ev2, 1)
                    if live(4) and first:
                        dve.wait_ge(g_mm, count(s - 4, 2, 2))
                        if (s - 5).exists():
                            dve.wait_ge(t_out, dma_count(s - 5, 1, 1))
                        dve.tensor_copy(gT[:, 1], psT[1][:]).then_inc(g_ev2, 1)
                    if live(2) and first:
                        update(s, q)
                    if live(0) and first:
                        lo_y(s, p, 0)
                        lo_y(s, p, 1)
                steps(dve, TILES, LAST, 2, body, LAST + 1)


def build_mlp(nc, io, k):
    CH = 4
    NC_ = TILES // CH
    with ExitStack() as ctx:
        sb, ps, sem = allocators(nc, ctx, "s4_")
        xh = sb("m_xh", [P, TILES, 2 * KH, P], F32R)
        xl = sb("m_xl", [P, TILES, 2 * KH, P], F32R)
        raw = sb("m_raw", [P, 2, 2 * KH, P])
        gam = sb("m_gam", [P, 2 * KH])
        bet = sb("m_bet", [P, 2 * KH])
        wraw = sb("m_wraw", [P, 2, 2 * KH, P])
        wh = sb("m_wh", [P, 2, 2 * KH, P], F32R)
        wl = sb("m_wl", [P, 2, 2 * KH, P], F32R)
        sil = sb("m_sil", [P, 2, CH * P])
        mo = sb("m_mo", [P, 2, NC_, CH * P])
        psG = [ps(f"m_psG{i}", [P, CH * P]) for i in range(NC_)]
        psU = [ps(f"m_psU{i}", [P, CH * P]) for i in range(NC_)]

        small_in = sem("small_in")
        r_in = [sem(f"r_in{p}") for p in range(2)]
        gam_ok, bet_ok, x_hi, x_lo = sem("gam_ok"), sem("bet_ok"), sem("x_hi"), sem("x_lo")
        w_in = [sem(f"w_in{p}") for p in range(2)]
        w_hi, w_lo = sem("w_hi"), sem("w_lo")
        mm_g, mm_u = sem("mm_g"), sem("mm_u")
        sil_ok, mo_ok = sem("sil_ok"), sem("mo_ok")
        mo_out = [sem(f"mo_out{p}") for p in range(2)]

        with nc.Block() as block:
            @block.sync
            def _(sp):
                sp.dma_start(gam[:], io["g2"]).then_inc(small_in, 16)
                sp.dma_start(bet[:], io["b2"]).then_inc(small_in, 16)

                def load_weights(s, p):
                    if (s - 2).exists():
                        sp.wait_ge(w_lo, count(s - 2, 1, 1))
                    sp.sem_inc(k["settled"], 1)
                    sp.dma_start(wraw[:, p].rearrange("p t j -> p (t j)"),
                                 io["wmlp"][ds(s.at(), 1)].rearrange("o p f -> (o p) f")).then_inc(w_in[p], 16)

                def load_reads(s, p, live):
                    if not live(0):
                        return
                    if (s - 2).exists():
                        sp.wait_ge(x_lo, count(s - 2, 1, 1))
                    sp.sem_inc(k["settled"], 1)
                    sp.dma_start(raw[:, p].rearrange("p t j -> p (t j)"),
                                 io["giT"][ds(s.at(), 1)].rearrange("o p f -> (o p) f")).then_inc(r_in[p], 16)

                def body(s, p, live):
                    if live(0):
                        load_weights(s, p)
                    if live(2):
                        sp.wait_ge(mo_ok, count(s - 2, NC_, NC_))
                        sp.sem_inc(k["settled"], 1)
                        dst = io["mlpT"].rearrange("t p (m j) -> p t m j", j=P)[:, :, ds((s - 2).at(), 1), :]
                        dst = dst.rearrange("p t o j -> p t (o j)")
                        sp.dma_start(dst, mo[:, p].rearrange("p c (t j) -> p (c t) j", j=P)).then_inc(mo_out[p], 16)
                steps(sp, TILES, 2, 2, load_reads)
                steps(sp, KM, 2, 2, body)
                for p in range(2):
                    sp.wait_ge(mo_out[p], 16 * KM // 2)

            @block.gpsimd
            def _(pool):
                pool.wait_ge(small_in, 32)

                def shift(s, p, live):
                    pool.wait_ge(gam_ok, count(s, 1, 1))
                    pool.tensor_tensor(raw[:, p], raw[:, p], spread(bet[:].unsqueeze(2), P, 2 * KH, P), ALU.add)\
                        .then_inc(bet_ok, 1)
                steps(pool, TILES, 0, 2, shift)

            @block.scalar
            def _(act):
                def hi_x(s, p, live):
                    act.wait_ge(bet_ok, count(s, 1, 1))
                    dst = xh[:].rearrange("p t k j -> p (t k j)")[:, ds(s.at(2 * KH * P), 2 * KH * P)]
                    act.activation(dst, raw[:, p].rearrange("p k j -> p (k j)"), ACT.Copy).then_inc(x_hi, 1)

                def body(s, p, live):
                    if live(0):
                        act.wait_ge(w_in[p], dma_count(s, 2, 1))
                        if (s - 2).exists():
                            act.wait_ge(mm_u, count(s - 2, NC_, NC_))
                        act.activation(wh[:, p], wraw[:, p], ACT.Copy).then_inc(w_hi, 1)
                    if live(1):
                        for c in range(NC_):
                            act.wait_ge(mm_g, count(s - 1, NC_, c + 1))
                            if c >= 2:
                                act.wait_ge(mo_ok, count(s - 1, NC_, c - 1))
                            else:
                                if (s - 2).exists():
                                    act.wait_ge(mo_ok, count(s - 2, NC_, c + 3))
                            act.activation(sil[:, c % 2], psG[c][:], ACT.Silu).then_inc(sil_ok, 1)
                steps(act, TILES, 0, 2, hi_x)
                steps(act, KM, 1, 2, body)

            @block.tensor
            def _(pe):
                def body(s, p, live):
                    for c in range(NC_):
                        if c == 0:
                            pe.wait_ge(w_hi, count(s, 1, 1))
                            pe.wait_ge(w_lo, count(s, 1, 1))
                        if s.reg is None and s.off == 0:
                            pe.wait_ge(x_lo, CH * (c + 1))
                        for side, bank, done, freed in ((0, psG, mm_g, sil_ok), (1, psU, mm_u, mo_ok)):
                            if (s - 1).exists():
                                pe.wait_ge(freed, count(s - 1, NC_, c + 1))
                            for i in range(KH):
                                kt = side * KH + i
                                for w, x in ((wh, xh), (wh, xl), (wl, xh)):
                                    mm = pe.matmul(bank[c][:], w[:, p, kt], x[:, CH * c:CH * (c + 1), kt],
                                                   start=(i == 0 and w is wh and x is xh),
                                                   stop=(i == KH - 1 and w is wl))
                            mm.then_inc(done, 1)
                steps(pe, KM, 2, 2, lambda s, p, live: body(s, p, live) if live(0) else None)

            @block.vector
            def _(dve):
                def scale(s, p):
                    if s.reg is None and s.off == 0:
                        dve.wait_ge(small_in, 32)
                    dve.wait_ge(r_in[p], dma_count(s, 2, 1))
                    dve.tensor_tensor(raw[:, p], raw[:, p], spread(gam[:].unsqueeze(2), P, 2 * KH, P), ALU.mult)\
                       .then_inc(gam_ok, 1)

                def lo_x(s, p):
                    dve.wait_ge(x_hi, count(s, 1, 1))
                    at = ds(s.at(2 * KH * P), 2 * KH * P)
                    dve.tensor_tensor(xl[:].rearrange("p t k j -> p (t k j)")[:, at],
                                      raw[:, p].rearrange("p k j -> p (k j)"),
                                      xh[:].rearrange("p t k j -> p (t k j)")[:, at], ALU.subtract).then_inc(x_lo, 1)

                def reads(s, p, live):
                    if live(0):
                        scale(s, p)
                    if live(1):
                        lo_x(s - 1, 1 - p)

                def body(s, p, live):
                    if live(0):
                        dve.wait_ge(w_hi, count(s, 1, 1))
                        dve.tensor_tensor(wl[:, p], wraw[:, p], wh[:, p], ALU.subtract).then_inc(w_lo, 1)
                    if live(1):
                        if (s - 3).exists():
                            dve.wait_ge(mo_out[1 - p], dma_count(s - 3, 2, 1))
                        for c in range(NC_):
                            dve.wait_ge(sil_ok, count(s - 1, NC_, c + 1))
                            dve.wait_ge(mm_u, count(s - 1, NC_, c + 1))
                            dve.tensor_tensor(mo[:, 1 - p, c], psU[c][:], sil[:, c % 2], ALU.mult).then_inc(mo_ok, 1)
                steps(dve, TILES, 1, 2, reads)
                steps(dve, KM, 1, 2, body, 3)


def timeline(eng, end, unroll, spans, body):
    def alive(s):
        return frozenset(n for n, (a, c) in spans.items() if a <= s < a + c)

    def run(reg, off, s0, slot):
        names = alive(s0)
        body(lambda n, back=0: Step(reg, off - spans[n][0] - back, spans[n][1]), slot, lambda n: n in names)

    signs = [tuple(alive(s) for s in range(t, min(t + unroll, end))) for t in range(0, end, unroll)]
    t = 0
    while t < len(signs):
        n = 1
        while t and t + n < len(signs) and signs[t + n] == signs[t]:
            n += 1
        if n > 1:
            with eng.Fori(0, n) as i:
                base = i * unroll
                for j in range(unroll):
                    run(base, t * unroll + j, t * unroll + j, j)
        else:
            for j in range(len(signs[t])):
                run(None, t * unroll + j, t * unroll + j, j)
        t += n


def build_ffn(nc, io, k):
    NP = C
    PIECES = NP * KD
    GR = P // (G // C)
    with ExitStack() as ctx:
        sb, ps, sem = allocators(nc, ctx, "s6_")
        wh = sb("f_wh", [P, 2, KD, H], F32R)
        wl = sb("f_wl", [P, 2, KD, H], F32R)
        xr = sb("f_xr", [P, 2, KD, P])
        xh = sb("f_xh", [P, 2, KD, P], F32R)
        xl = sb("f_xl", [P, 2, KD, P], F32R)
        q = sb("f_q", [P, 2, H], I32)
        w = sb("f_w", [P, 2, H])
        sz = sb("f_sz", [P, 2, 2, H])
        xb = sb("f_xb", [P, 2, H])
        y = sb("f_y", [P, 2, H])
        psF = [ps(f"psF{i}", [P, H]) for i in range(2)]

        q_in = [sem(f"q_in{p}") for p in range(2)]
        sz_in = [sem(f"sz_in{p}") for p in range(2)]
        x_in = [sem(f"fx_in{p}") for p in range(2)]
        xb_in = [sem(f"xb_in{p}") for p in range(2)]
        y_out = [sem(f"y_out{p}") for p in range(2)]
        less_zp, w_ok, w_hi, w_lo = sem("less_zp"), sem("w_ok"), sem("fw_hi"), sem("fw_lo")
        x_hi, x_lo, mm_ok, y_ok = sem("fx_hi"), sem("fx_lo"), sem("mm_ok"), sem("y_ok")

        assert TILES == KD
        U = NP * TILES
        spans = {"piece": (0, PIECES), "x": (KD, U), "mm": (KD + 1, U), "done": (KD + 2, U)}
        end = KD + 2 + U
        UN = 8

        def at_piece(v):
            n = v.at()
            return n // KD % 2, n % C * KH + n % KD // C

        def plane(u):
            n = u.at()
            return n // TILES, n % TILES

        with nc.Block() as block:
            @block.sync
            def _(sp):
                def body(tile, j, live):
                    p = j % 2
                    if live("piece"):
                        v = tile("piece")
                        if j % 4 == 0:
                            r = j // 4
                            if (tile("piece", 8)).exists():
                                sp.wait_ge(w_ok, count(tile("piece", 8), 1, 4))
                            sp.sem_inc(k["settled"], 1)
                            for i, name in enumerate(("scT", "zpT")):
                                src = io[name][ds(v.at() // 4, 1)].rearrange("o g n -> (o g) n")
                                src = spread(src.unsqueeze(1), GR, P // GR, H)
                                sp.dma_start(sz[:, r, i], src).then_inc(sz_in[r], 16)
                        if (tile("piece", 2)).exists():
                            sp.wait_ge(less_zp, count(tile("piece", 2), 1, 1))
                        sp.sem_inc(k["settled"], 1)
                        sp.dma_start(q[:, p], io["wq"][ds(v.at(), 1)].rearrange("o p f -> (o p) f")).then_inc(q_in[p], 16)
                    if live("x"):
                        u = tile("x")
                        c_, t_ = plane(u)
                        if (tile("x", 2)).exists():
                            sp.wait_ge(x_lo, count(tile("x", 2), 1, 1))
                        sp.sem_inc(k["settled"], 1)
                        sp.dma_start(xr[:, p].rearrange("p t j -> p (t j)"),
                                     io["xnT"][ds(t_, 1)].rearrange("o p f -> (o p) f")).then_inc(x_in[p], 16)
                        if (tile("x", 2)).exists():
                            sp.wait_ge(y_ok, count(tile("x", 2), 1, 1))
                        sp.sem_inc(k["settled"], 1)
                        sp.dma_start(xb[:, p], io["xb"][ds(t_ * P, P), ds(c_ * H, H)]).then_inc(xb_in[p], 16)
                    if live("done"):
                        c_, t_ = plane(tile("done"))
                        sp.wait_ge(y_ok, count(tile("done"), 1, 1))
                        sp.sem_inc(k["settled"], 1)
                        sp.dma_start(io["y"][ds(t_ * P, P), ds(c_ * H, H)], y[:, p]).then_inc(y_out[p], 16)
                timeline(sp, end, UN, spans, body)
                for p in range(2):
                    sp.wait_ge(y_out[p], 16 * U // 2)

            @block.gpsimd
            def _(pool):
                def body(tile, j, live):
                    if live("piece"):
                        p = j % 2
                        pool.wait_ge(less_zp, count(tile("piece"), 1, 1))
                        pool.tensor_tensor(w[:, p], w[:, p], sz[:, j // 4, 0], ALU.mult).then_inc(w_ok, 1)
                timeline(pool, end, UN, spans, body)

            @block.scalar
            def _(act):
                def body(tile, j, live):
                    p = j % 2
                    if live("x"):
                        act.wait_ge(x_in[p], dma_count(tile("x"), 2, 1))
                        if live("mm"):
                            if (tile("mm", 1)).exists():
                                act.wait_ge(mm_ok, count(tile("mm", 1), 1, 1))
                        act.activation(xh[:, p], xr[:, p], ACT.Copy).then_inc(x_hi, 1)
                    if live("piece"):
                        v = tile("piece")
                        b_, kt_ = at_piece(v)
                        act.wait_ge(w_ok, count(v, 1, 1))
                        if live("mm"):
                            act.wait_ge(mm_ok, count(tile("mm"), 1, 1))
                        dst = wh[:].rearrange("p b k n -> p (b k n)")[:, ds(b_ * (KD * H) + kt_ * H, H)]
                        act.activation(dst, w[:, p], ACT.Copy).then_inc(w_hi, 1)
                timeline(act, end, UN, spans, body)

            @block.tensor
            def _(pe):
                def body(tile, j, live):
                    if not live("mm"):
                        return
                    u, p = tile("mm"), (j - 1) % 2
                    pe.wait_ge(x_hi, count(u, 1, 1))
                    pe.wait_ge(x_lo, count(u, 1, 1))
                    if live("piece"):
                        pe.wait_ge(w_lo, count(tile("piece", 2), 1, 1))
                    else:
                        pe.wait_ge(w_lo, PIECES)
                    if (tile("mm", 2)).exists():
                        pe.wait_ge(y_ok, count(tile("mm", 2), 1, 1))
                    buf = (u.at() // TILES) % 2
                    for kt in range(KD):
                        rh = wh[:].rearrange("p b k n -> p (b k n)")[:, ds(buf * (KD * H) + kt * H, H)]
                        rl = wl[:].rearrange("p b k n -> p (b k n)")[:, ds(buf * (KD * H) + kt * H, H)]
                        pe.matmul(psF[p][:], xh[:, p, kt], rh, start=(kt == 0), stop=False)
                        pe.matmul(psF[p][:], xh[:, p, kt], rl, start=False, stop=False)
                        mm = pe.matmul(psF[p][:], xl[:, p, kt], rh, start=False, stop=(kt == KD - 1))
                    mm.then_inc(mm_ok, 1)
                timeline(pe, end, UN, spans, body)

            @block.vector
            def _(dve):
                def body(tile, j, live):
                    p = j % 2
                    if live("x"):
                        dve.wait_ge(x_hi, count(tile("x"), 1, 1))
                        dve.tensor_tensor(xl[:, p], xr[:, p], xh[:, p], ALU.subtract).then_inc(x_lo, 1)
                    if live("piece"):
                        v = tile("piece")
                        dve.wait_ge(q_in[p], dma_count(v, 2, 1))
                        if j % 4 == 0:
                            dve.wait_ge(sz_in[j // 4], v.turn(8, 32, 32))
                        if (tile("piece", 2)).exists():
                            dve.wait_ge(w_lo, count(tile("piece", 2), 1, 1))
                        dve.tensor_tensor(w[:, p], q[:, p], sz[:, j // 4, 1], ALU.subtract).then_inc(less_zp, 1)
                    if live("done"):
                        dve.wait_ge(mm_ok, count(tile("done"), 1, 1))
                        dve.wait_ge(xb_in[p], dma_count(tile("done"), 2, 1))
                        if (tile("done", 2)).exists():
                            dve.wait_ge(y_out[p], dma_count(tile("done", 2), 2, 1))
                        dve.tensor_tensor(y[:, p], psF[p][:], xb[:, p], ALU.add).then_inc(y_ok, 1)
                    if live("piece"):
                        b_, kt_ = at_piece(v)
                        dve.wait_ge(w_hi, count(v, 1, 1))
                        at = ds(b_ * (KD * H) + kt_ * H, H)
                        dve.tensor_tensor(wl[:].rearrange("p b k n -> p (b k n)")[:, at], w[:, p],
                                          wh[:].rearrange("p b k n -> p (b k n)")[:, at], ALU.subtract).then_inc(w_lo, 1)
                timeline(dve, end, UN, spans, body)


def build(nc, io):
    for name, shape in (("qkT", (2, 2, HEADS * HD, L)), ("hs2", (T, D)), ("giT", (TILES, P, 2 * H)),
                        ("mlpT", (TILES, P, M)), ("xnT", (TILES, P, D)), ("xb", (T, D))):
        io[name] = nc.dram_tensor(name, shape, F32).ap()
    with ExitStack() as ctx:
        k = build_constants(nc, ctx, io)
        with ExitStack() as ctx_v:
            allocate_values(nc, ctx_v, k)
            build_qkv(nc, io, k)
            sb, _, _ = allocators(nc, ctx_v)
            k["o_sb"] = sb("o_sb", [P, HEADS, QT, HD])
            build_attention(nc, io, k)
            build_write(nc, io, k, True)
        build_mlp(nc, io, k)
        build_write(nc, io, k, False)
        build_ffn(nc, io, k)


def kernel(x, pos_BxS, ctx_1024, L0_xattn_attn_read_w, L0_xattn_attn_read_g, L0_xattn_attn_read_b, L0_xattn_qkv_w,
           L0_xattn_attn_wod_w, L0_xattn_attn_wab_w, L0_xattn_attn_wab_b, L0_xattn_attn_du_w, L0_xattn_attn_du_b,
           L0_xattn_mlp_read_w, L0_xattn_mlp_read_g, L0_xattn_mlp_read_b, L0_xattn_mlp_wod_w, L0_xattn_mlp_wab_w,
           L0_xattn_mlp_wab_b, L0_xattn_mlp_du_w, L0_xattn_mlp_du_b, L0_ffn_weight_q, L0_ffn_scale, L0_ffn_zp,
           L0_ffn_bias):
    import concourse.bacc as bacc
    from concourse.bass_utils import run_bass_kernel_spmd

    def columns(w, outputs):
        return w.reshape(outputs, KH, P).transpose(2, 0, 1)

    def rows(v):
        return np.broadcast_to(v, (P,) + v.shape)

    def write_weights(wod, wab):
        w = np.concatenate([wod[:H // 2], wod[H:], wab[:NA], wod[H // 2:H], wab[NA:]], 0)
        return w.T.reshape(-1, P, NW).transpose(1, 0, 2)

    def small_bias(b):
        return rows(np.concatenate([np.zeros(DR, np.float32), b]))

    def delta_weights(w, b):
        return np.concatenate([w.T, b[None]], 0)

    def groups(s):
        return s.reshape(H, C, KH, KD // 2).transpose(1, 2, 3, 0).reshape(C * KH, KD // 2, H)

    a = {n: np.asarray(v) for n, v in dict(
        x=x, pos=pos_BxS, win=ctx_1024, arw=L0_xattn_attn_read_w, arg=L0_xattn_attn_read_g, arb=L0_xattn_attn_read_b,
        qkv=L0_xattn_qkv_w, awod=L0_xattn_attn_wod_w, awab=L0_xattn_attn_wab_w, awabb=L0_xattn_attn_wab_b,
        aduw=L0_xattn_attn_du_w, adub=L0_xattn_attn_du_b, mrw=L0_xattn_mlp_read_w, mrg=L0_xattn_mlp_read_g,
        mrb=L0_xattn_mlp_read_b, mwod=L0_xattn_mlp_wod_w, mwab=L0_xattn_mlp_wab_w, mwabb=L0_xattn_mlp_wab_b,
        mduw=L0_xattn_mlp_du_w, mdub=L0_xattn_mlp_du_b, wq=L0_ffn_weight_q, sc=L0_ffn_scale, zp=L0_ffn_zp,
        bias=L0_ffn_bias).items()}
    xt = a["x"].reshape(T, D)
    arrays = {
        "xT": xt.T.reshape(KD, P, T).transpose(1, 0, 2),
        "xP": xt.reshape(T, H, C).transpose(0, 2, 1).reshape(T, D),
        "pos": a["pos"].reshape(TILES, P).T,
        "wr1": a["arw"].transpose(0, 2, 1).reshape(KD, P, 3).transpose(1, 0, 2),
        "g1": columns(a["arg"], 3),
        "b1": columns(a["arb"], 3),
        "wqkv": a["qkv"].transpose(2, 0, 1).reshape(KH, P, 3 * H).transpose(1, 0, 2),
        "wo1": write_weights(a["awod"], a["awab"]),
        "bsm1": small_bias(a["awabb"]),
        "du1": delta_weights(a["aduw"], a["adub"]),
        "wr2": a["mrw"].reshape(KD, HD, 2, C).transpose(3, 1, 0, 2).reshape(P, KD, 2),
        "g2": columns(a["mrg"], 2).reshape(P, 2 * KH),
        "b2": columns(a["mrb"], 2).reshape(P, 2 * KH),
        "wmlp": a["win"].reshape(2, KM, P, KH, P).transpose(1, 4, 0, 3, 2).reshape(KM, P, 2 * H),
        "wo2": write_weights(a["mwod"], a["mwab"]),
        "bsm2": small_bias(a["mwabb"]),
        "du2": delta_weights(a["mduw"], a["mdub"]),
        "fbias": rows(a["bias"].reshape(H, C).T.reshape(D)),
        "wq": a["wq"].reshape(H, C, KH, P, C).transpose(1, 2, 4, 3, 0).reshape(C * KD, P, H),
        "scT": groups(a["sc"]),
        "zpT": groups(a["zp"]),
    }
    arrays = {n: np.ascontiguousarray(v) for n, v in arrays.items()}
    nc = bacc.Bacc("TRN2", target_bir_lowering=False, num_devices=1)
    io = {n: nc.dram_tensor(n, v.shape, mybir.dt.from_np(v.dtype), kind="ExternalInput").ap() for n, v in arrays.items()}
    io["y"] = nc.dram_tensor("y", (T, D), F32, kind="ExternalOutput").ap()
    build(nc, io)
    r = run_bass_kernel_spmd(nc, [arrays], core_ids=[0])
    return r.results[0]["y"].reshape(B, L, C, H).transpose(0, 1, 3, 2).reshape(B, L, D)
```

```python
import math
from contextlib import ExitStack

import numpy as np
import concourse.bass as bass
from concourse import mybir

F32 = mybir.dt.float32
F32R = mybir.dt.float32r
I32 = mybir.dt.int32
BF16 = mybir.dt.bfloat16
ALU = mybir.AluOpType
ACT = mybir.ActivationFunctionType
AX = mybir.AxisListType.X
ds = bass.ds

P = 128
B, L, D = 2, 1024, 2048
T = B * L
H, C = 512, 4
RH = 16
HS = H // RH
DR = 8
NH, HD = 16, 32
M = 2048
NA = (C - 1) * RH
NAB = NA + C * RH
NW = H + DR + NAB
G = 64
EPS = 1e-5
TILES = T // P
KD, KH, KM = D // P, H // P, M // P
QT = L // P
HEADS = B * NH
NEG = -1e30
EXP_LN_SET = 6
VN = 96


class Step:

    def __init__(self, reg, off, tiles):
        self.reg, self.off, self.tiles = reg, off, tiles

    def __sub__(self, n):
        return Step(self.reg, self.off - n, self.tiles)

    def exists(self):
        return self.reg is not None or self.off >= 0

    def at(self, per=1, extra=0):
        if self.reg is None:
            return per * self.off + extra
        return self.reg * per + (self.off * per + extra)

    def turn(self, ring, per, extra=0):
        if self.reg is None:
            return per * (self.off // ring) + extra
        return self.reg * (per // ring) + (self.off // ring * per + extra)


def steps(eng, tiles, depth, unroll, body, peel=0):
    head = -(-max(depth, peel) // unroll) * unroll
    turns = (tiles - head) // unroll
    for s in range(head):
        body(Step(None, s, tiles), s % unroll, lambda d, s=s: 0 <= s - d < tiles)
    if turns:
        with eng.Fori(0, turns) as i:
            base = i * unroll
            for j in range(unroll):
                body(Step(base, head + j, tiles), j, lambda d: True)
    for s in range(head + turns * unroll, tiles + depth):
        body(Step(None, s, tiles), s % unroll, lambda d, s=s: 0 <= s - d < tiles)


def count(tile, per, event):
    if tile.reg is None and tile.off >= tile.tiles:
        return per * tile.tiles
    assert per * tile.off + event > 0
    return tile.at(per, event)


def due(tile, per, event):
    return tile.reg is not None or per * tile.off + event > 0


def dma_count(tile, ring, dmas):
    assert tile.off // ring >= 0
    return tile.turn(ring, 16 * dmas, 16 * dmas)


TAKEN = []


def retire(nc, keep):
    done = [h for h in TAKEN if h is not keep]
    with nc.Block() as block:
        @block.gpsimd
        def _(pool):
            for handle in done:
                pool.sem_clear(handle)
    for handle in done:
        nc.release_semaphore(handle)
    TAKEN[:] = [keep]


def allocators(nc, ctx, tag=""):
    def sb(name, shape, dt=F32):
        return ctx.enter_context(nc.sbuf_tensor(tag + name, shape, dt))

    def ps(name, shape, dt=F32):
        return ctx.enter_context(nc.psum_tensor(tag + name, shape, dt))

    def sem(name):
        handle = nc.alloc_semaphore(name=tag + name)
        TAKEN.append(handle)
        return handle

    return sb, ps, sem


def spread(ap, *dims):
    return ap.broadcast_to(list(dims))


def build_constants(nc, ctx, io):
    sb, ps, sem = allocators(nc, ctx, "c_")
    k = {}
    k["ident"] = sb("ident", [P, P])
    k["mask_b"] = sb("mask_b", [P, P], BF16)
    k["maskT_b"] = sb("maskT_b", [P, P], BF16)
    k["ident_b"] = sb("ident_b", [P, P], BF16)
    k["ln1"] = sb("ln1", [P, TILES, 2])
    k["settled"] = sem("settled")
    with ExitStack() as c:
        sb2, _, sem = allocators(nc, c, "c_")
        mask = sb2("mask", [P, P])
        maskT = sb2("maskT", [P, P])
        zeroed, chosen = sem("zeroed"), sem("chosen")
        with nc.Block() as block:
            @block.gpsimd
            def _(pool):
                for m in (k["ident"], mask, maskT):
                    pool.memset(m[:], 0.0).then_inc(zeroed, 1)
                pool.wait_ge(zeroed, 3)
                pool.affine_select(out=k["ident"][:], in_=k["ident"][:], compare_op=ALU.not_equal, fill=1.0,
                                   base=0, pattern=[[-1, P]], channel_multiplier=1).then_inc(chosen, 1)
                pool.affine_select(out=mask[:], in_=mask[:], compare_op=ALU.is_ge, fill=NEG,
                                   base=0, pattern=[[-1, P]], channel_multiplier=1).then_inc(chosen, 1)
                pool.affine_select(out=maskT[:], in_=maskT[:], compare_op=ALU.is_ge, fill=NEG,
                                   base=0, pattern=[[1, P]], channel_multiplier=-1).then_inc(chosen, 1)
            @block.vector
            def _(dve):
                dve.wait_ge(chosen, 3)
                dve.tensor_copy(k["ident_b"][:], k["ident"][:])
                dve.tensor_copy(k["mask_b"][:], mask[:])
                dve.tensor_copy(k["maskT_b"][:], maskT[:])
    return k


def allocate_values(nc, ctx, k):
    sb, _, _ = allocators(nc, ctx, "v_")
    k["v_flat"] = sb("v_sb", [P, HEADS * QT * (HD + 1) + VN])
    k["v_sb"] = k["v_flat"][:, 0:HEADS * QT * (HD + 1)].rearrange("p (n t d) -> p n t d", n=HEADS, t=QT)
    with nc.Block() as block:
        @block.gpsimd
        def _(pool):
            pool.memset(k["v_flat"][:], 1.0)


def build_qkv(nc, io, k):
    HD2 = HD // 2
    with ExitStack() as ctx:
        sb, ps, sem = allocators(nc, ctx, "s1_")
        O = 3
        OW = O * HD
        wh = sb("q_wh", [P, KH, O * H], F32R)
        wl = sb("q_wl", [P, KH, O * H], F32R)
        brow = sb("q_brow", [P, O * H], F32R)
        c64 = sb("q_c64", [P, P], F32R)
        spf = sb("q_spf", [P, KD, OW])
        wsum = sb("q_wsum", [P, KD * OW])
        cosT = sb("cosT", [P, TILES, HD2])
        sinT = sb("sinT", [P, TILES, 2, HD2])

        psY = ps("psY", [P, 2, 512])
        psA = ps("psA", [P, KH, P])
        psB = ps("psB", [P, KH, P])
        psC = ps("psC", [P, KH, P])
        psQ = ps("psQ", [P, O, H])
        y_bank, qk_bank = (psA, psB, psA), (psC, psB)

        with ExitStack() as c:
            sb, _, sem = allocators(nc, c, "s1_")
            wraw = sb("q_wraw", [P, KH, O * H])
            gam = sb("q_gam", [P, O, KH])
            bet = sb("q_bet", [P, O, KH])
            rw = sb("q_rw", [P, KD, O])
            m32 = sb("q_m32", [P, HD])
            ones = sb("q_onesf", [P, P])
            betb = sb("q_betb", [P, O, KH, P])
            posi = sb("q_posi", [P, TILES], I32)
            posf = sb("q_posf", [P, TILES])
            inv = sb("q_inv", [P, HD2])
            ang = sb("q_ang", [P, TILES, HD2])
            turn = sb("q_turn", [P, TILES, HD2])
            red = sb("q_red", [P, TILES, HD2])
            w_in, small_in, blk, dve_w, act_w, pe_w, d = (sem(n) for n in
                ("w_in", "small_in", "blk", "dve_w", "act_w", "pe_w", "d"))
            trig, wsum_ok = sem("trig"), sem("wsum_ok")
            with nc.Block() as block:
                @block.sync
                def _(sp):
                    sp.dma_start(rw[:], io["wr1"]).then_inc(small_in, 16)
                    sp.dma_start(gam[:], io["g1"]).then_inc(small_in, 16)
                    sp.dma_start(bet[:], io["b1"]).then_inc(small_in, 16)
                    sp.dma_start(posi[:], io["pos"]).then_inc(small_in, 16)
                    sp.dma_start(wraw[:], io["wqkv"]).then_inc(w_in, 16)

                @block.gpsimd
                def _(pool):
                    pool.memset(m32[:], 1.0).then_inc(blk, 1)
                    pool.wait_ge(blk, 1)
                    pool.affine_select(out=m32[:], in_=m32[:], compare_op=ALU.is_ge, fill=0.0, base=0,
                                       pattern=[[-C, HD]], channel_multiplier=1).then_inc(blk, 1)
                    pool.wait_ge(blk, 2)
                    pool.affine_select(out=m32[:], in_=m32[:], compare_op=ALU.is_ge, fill=0.0, base=C - 1,
                                       pattern=[[C, HD]], channel_multiplier=-1).then_inc(blk, 1)

                @block.vector
                def _(dve):
                    n = 0

                    def chain(ins):
                        nonlocal n
                        n += 1
                        ins.then_inc(d, 1)
                        dve.wait_ge(d, n)

                    for j in range(HD2):
                        f = np.float32(1.0) / np.float32(10000.0) ** (np.float32(j) / np.float32(HD2))
                        dve.memset(inv[:, j:j + 1], float(f))
                    dve.memset(ones[:], 1.0)
                    chain(dve.memset(turn[:], 1.0 / 64))
                    chain(dve.tensor_copy(c64[:], turn[:, 0:P // HD2, :].rearrange("p a b -> p (a b)")))
                    dve.wait_ge(small_in, 64)
                    dve.wait_ge(blk, 3)
                    chain(dve.tensor_tensor(spf[:].rearrange("p t (o j) -> p (t o) j", o=O),
                                            spread(rw[:].rearrange("p t o -> p (t o)").unsqueeze(2), P, KD * O, HD),
                                            spread(m32[:].unsqueeze(1), P, KD * O, HD), ALU.mult))
                    dve.tensor_copy(betb[:], spread(bet[:].unsqueeze(3), P, O, KH, P)).then_inc(dve_w, 1)
                    chain(dve.tensor_copy(posf[:], posi[:]))
                    chain(dve.tensor_tensor(ang[:], spread(posf[:].unsqueeze(2), P, TILES, HD2),
                                            spread(inv[:].unsqueeze(1), P, TILES, HD2), ALU.mult))
                    two_pi = 2 * math.pi
                    c1 = 6.28125
                    c2 = float(np.float32(round((two_pi - c1) * 2**19) / 2**19))
                    c3 = two_pi - c1 - c2
                    magic = 1.5 * 2.0**23
                    for which, shift in ((0, 0.0), (1, 0.25)):
                        chain(dve.tensor_scalar(turn[:], ang[:], 1 / two_pi, shift, ALU.mult, ALU.add))
                        chain(dve.tensor_scalar(turn[:], turn[:], magic, None, ALU.add))
                        chain(dve.tensor_scalar(turn[:], turn[:], magic, None, ALU.subtract))
                        if which:
                            dve.wait_ge(trig, 2)
                        chain(dve.scalar_tensor_tensor(red[:], turn[:], -c1, ang[:], ALU.mult, ALU.add))
                        chain(dve.scalar_tensor_tensor(red[:], turn[:], -c2, red[:], ALU.mult, ALU.add))
                        chain(dve.scalar_tensor_tensor(red[:], turn[:], -c3, red[:], ALU.mult, ALU.add))
                        if which:
                            chain(dve.tensor_scalar(red[:], red[:], math.pi / 2, None, ALU.add))
                        lim = 3.1415925
                        dve.tensor_scalar(red[:], red[:], lim, -lim, ALU.min, ALU.max).then_inc(trig, 1)
                    for o in range(O):
                        for kt in range(KH):
                            i = o * KH + kt
                            cols = slice(o * H, (o + 1) * H)
                            dve.wait_ge(act_w, i + 1)
                            dve.scalar_tensor_tensor(wl[:, kt, cols], wraw[:, kt, cols], gam[:, o, kt:kt + 1],
                                                     wh[:, kt, cols], ALU.mult, ALU.subtract)
                    for half in range(2):
                        dve.wait_ge(pe_w, half + 1)
                        dve.tensor_copy(wsum[:, half * 8 * OW:(half + 1) * 8 * OW].rearrange("p (b j) -> p b j", b=2),
                                        psY[:, :, 0:4 * OW]).then_inc(wsum_ok, 1)
                    dve.wait_ge(pe_w, 3)
                    chain(dve.tensor_copy(brow[:], psQ[:].rearrange("p o n -> p (o n)")))
                    dve.tensor_tensor(brow[64:P, :], psQ[64:P].rearrange("p o n -> p (o n)"), brow[64:P, :],
                                      ALU.subtract)

                @block.scalar
                def _(act):
                    act.wait_ge(small_in, 64)
                    act.wait_ge(w_in, 16)
                    for o in range(O):
                        for kt in range(KH):
                            cols = slice(o * H, (o + 1) * H)
                            act.activation(wh[:, kt, cols], wraw[:, kt, cols], ACT.Copy,
                                           scale=gam[:, o, kt:kt + 1]).then_inc(act_w, 1)
                    act.wait_ge(trig, 1)
                    act.activation(sinT[:, :, 1, :], red[:], ACT.Sin)
                    act.activation(sinT[:, :, 0, :], red[:], ACT.Sin, scale=-1.0).then_inc(trig, 1)
                    act.wait_ge(trig, 3)
                    act.activation(cosT[:], red[:], ACT.Sin)

                @block.tensor
                def _(pe):
                    pe.wait_ge(dve_w, 1)
                    for half in range(2):
                        if half:
                            pe.wait_ge(wsum_ok, 1)
                        for kt in range(8 * half, 8 * half + 8):
                            out = psY[:, kt // 4 % 2, (kt % 4) * OW:(kt % 4 + 1) * OW]
                            mm = pe.matmul(out, ones[:], spf[:, kt, :], start=True, stop=True)
                        mm.then_inc(pe_w, 1)
                    pe.wait_ge(w_in, 16)
                    for o in range(O):
                        for kt in range(KH):
                            mm = pe.matmul(psQ[:, o, :], betb[:, o, kt, :], wraw[:, kt, o * H:(o + 1) * H],
                                           start=(kt == 0), stop=(kt == KH - 1))
                    mm.then_inc(pe_w, 1)

        sb, ps, sem = allocators(nc, ctx, "s1_")
        xt = sb("q_xt", [P, 2, KD, P])
        xc = sb("q_xc", [P, 2, D])
        yr = sb("q_yr", [P, KD, OW])
        yn = sb("q_yn", [P, O, H])
        yth = sb("q_yth", [P, O, KH, P], F32R)
        ytl = sb("q_ytl", [P, O, KH, P], F32R)
        ra = sb("q_ra", [P, 2 * H])
        rb = sb("q_rb", [P, 2 * H])
        qk = sb("q_qk", [P, 2 * H])
        qth = sb("q_qth", [P, 2, KH, P], F32R)
        qtl = sb("q_qtl", [P, 2, KH, P], F32R)
        bst = sb("q_bst", [P, 4, 6])
        bsy = sb("q_bsy", [P, O, 6])
        mv = sb("q_mv", [P, O, 2])
        sx = sb("q_sx", [P, 2, 5])
        sy = sb("q_sy", [P, 5, O])

        X_AGG, X_EPS, X_NEG, X_INV = 5, 6, 7, 8
        Y_LESS, Y_AGG, Y_VAR, Y_INV, Y_SQ = 2, 8, 9, 10, 11

        x_in = [sem(f"x_in{p}") for p in range(2)]
        y_mm = sem("y_mm")
        x_norm, y_norm = sem("x_norm"), sem("y_norm")
        rr_ok, sh_ok = sem("rr_ok"), sem("sh_ok")
        yn_ok = sem("yn_ok")
        yt_mm, yt_hi, yt_lo = sem("yt_mm"), sem("yt_hi"), sem("yt_lo")
        qkv_mm = sem("qkv_mm")
        rot_ab, rot = sem("rot_ab"), sem("rot")
        v_ok = sem("v_ok")
        qt_mm, qt_hi, qt_lo = sem("qt_mm"), sem("qt_hi"), sem("qt_lo")
        qk_out = sem("qk_out")

        def place(tile):
            n = tile.at()
            return n // QT, n % QT

        with nc.Block() as block:
            @block.sync
            def _(sp):
                def body(s, p, live):
                    if live(0):
                        if (s - 2).exists():
                            sp.wait_ge(y_mm, count(s - 2, 4, 4))
                        sp.sem_inc(k["settled"], 1)
                        if (s - 2).exists():
                            sp.wait_ge(x_norm, count(s - 2, 8, 4))
                        sp.sem_inc(k["settled"], 1)
                        tok = s.at(P)
                        sp.dma_start(xt[:, p], io["xT"][:, :, ds(tok, P)]).then_inc(x_in[p], 16)
                        sp.dma_start(xc[:, p], io["xP"][ds(tok, P), :]).then_inc(x_in[p], 16)
                    if live(4):
                        sp.wait_ge(qt_hi, count(s - 4, 2, 2))
                        sp.sem_inc(k["settled"], 1)
                        sp.wait_ge(qt_lo, count(s - 4, 2, 2))
                        sp.sem_inc(k["settled"], 1)
                        b_, kt_ = place(s - 4)
                        for side in range(2):
                            for hl, buf in ((0, qth), (1, qtl)):
                                dst = io["qkT"][side, hl].rearrange("(g p) t -> p g t", p=P)
                                dst = dst[:, ds(b_ * KH, KH), ds(kt_ * P, P)]
                                sp.dma_start(dst, buf[:, side].bitcast(F32)).then_inc(qk_out, 16)
                steps(sp, TILES, 4, 2, body)
                sp.wait_ge(qk_out, 16 * 4 * TILES)

            @block.gpsimd
            def _(pool):
                def body(s, p, live):
                    if live(2):
                        pool.wait_ge(rot_ab, count(s - 2, 2, 2))
                        if (s - 3).exists():
                            pool.wait_ge(qt_mm, count(s - 3, 2, 2))
                        pool.tensor_tensor(qk[:], ra[:], rb[:], ALU.add).then_inc(rot, 1)
                steps(pool, TILES, 3, 2, body)

            @block.scalar
            def _(act):
                def hi_y(s, o):
                    act.wait_ge(yt_mm, count(s - 2, 3, o + 1))
                    if (s - 3).exists():
                        act.wait_ge(qkv_mm, count(s - 3, 3, o + 1))
                    act.activation(yth[:, o], y_bank[o][:], ACT.Copy).then_inc(yt_hi, 1)

                def hi_qk(s, r):
                    act.wait_ge(qt_mm, count(s - 3, 2, r + 1))
                    if (s - 4).exists():
                        act.wait_ge(qk_out, dma_count(s - 4, 1, 4))
                    act.activation(qth[:, r], qk_bank[r][:], ACT.Copy).then_inc(qt_hi, 1)

                def body(s, p, live):
                    if live(2):
                        hi_y(s, 0)
                        hi_y(s, 1)
                    if live(2):
                        hi_y(s, 2)
                    if live(1):
                        act.wait_ge(y_norm, count(s - 1, 11, Y_SQ))
                        act.activation(sy[:, 2, :], sy[:, 1, :], ACT.Sqrt).then_inc(rr_ok, 1)
                        act.wait_ge(sh_ok, count(s - 1, 1, 1))
                        if (s - 2).exists():
                            act.wait_ge(yt_mm, count(s - 2, 3, 3))
                        for o in range(O):
                            act.activation(yn[:, o].rearrange("p (t j) -> p t j", j=HD),
                                           yr[:, :, o * HD:(o + 1) * HD], ACT.Identity,
                                           scale=sy[:, 2, o:o + 1], bias=sy[:, 3, o:o + 1]).then_inc(yn_ok, 1)
                    if live(3):
                        hi_qk(s, 0)
                    if live(2):
                        act.wait_ge(qkv_mm, count(s - 2, 3, 3))
                        b_, kt_ = place(s - 2)
                        dst = k["v_sb"].rearrange("p (b n) t d -> p b n t d", b=B)
                        dst = dst[:, ds(b_, 1), :, ds(kt_, 1), 0:HD].rearrange("p b n t d -> p (b n) (t d)")
                        act.activation(dst, psQ[:, 2].rearrange("p (n d) -> p n d", d=HD), ACT.Copy).then_inc(v_ok, 1)
                    if live(3):
                        hi_qk(s, 1)
                steps(act, TILES, 3, 2, body)

            @block.tensor
            def _(pe):
                def turn_qk(s, r):
                    pe.wait_ge(rot, count(s - 3, 1, 1))
                    if r == 0:
                        if (s - 4).exists():
                            pe.wait_ge(qt_hi, count(s - 4, 2, 1))
                        if (s - 4).exists():
                            pe.wait_ge(qt_lo, count(s - 4, 2, 1))
                    else:
                        pe.wait_ge(yt_hi, count(s - 2, 3, 2))
                        pe.wait_ge(yt_lo, count(s - 2, 3, 2))
                        if (s - 4).exists():
                            pe.wait_ge(qt_hi, count(s - 4, 2, 2))
                        if (s - 4).exists():
                            pe.wait_ge(qt_lo, count(s - 4, 2, 2))
                    for c in range(KH):
                        mm = pe.transpose(qk_bank[r][:, c], qk[:, r * H + c * P:r * H + (c + 1) * P], k["ident"][:])
                    mm.then_inc(qt_mm, 1)

                def turn_y(s, o):
                    pe.wait_ge(yn_ok, count(s - 2, 3, o + 1))
                    if o == 1:
                        if (s - 4).exists():
                            pe.wait_ge(qt_hi, count(s - 4, 2, 2))
                        if (s - 4).exists():
                            pe.wait_ge(qt_lo, count(s - 4, 2, 2))
                    before = s - 3 if o == 0 else s - 2
                    if o != 1:
                        if before.exists():
                            pe.wait_ge(yt_hi, count(before, 3, 3 if o == 0 else 1))
                        if before.exists():
                            pe.wait_ge(yt_lo, count(before, 3, 3 if o == 0 else 1))
                    for c in range(KH):
                        mm = pe.transpose(y_bank[o][:, c], yn[:, o, c * P:(c + 1) * P], k["ident"][:])
                    mm.then_inc(yt_mm, 1)

                def read(s, p, grp):
                    if grp == 0:
                        pe.wait_ge(x_in[1 - p], dma_count(s - 1, 2, 2))
                        if (s - 2).exists():
                            pe.wait_ge(y_norm, count(s - 2, 11, Y_LESS))
                    if grp == 2:
                        pe.wait_ge(y_norm, count(s - 1, 11, 1))
                    for kt in range(4 * grp, 4 * grp + 4):
                        out = psY[:, grp % 2, (kt % 4) * OW:(kt % 4 + 1) * OW]
                        mm = pe.matmul(out, xt[:, 1 - p, kt], spf[:, kt], start=True, stop=True)
                    mm.then_inc(y_mm, 1)

                def project(s, o):
                    pe.wait_ge(yt_hi, count(s - 2, 3, o + 1))
                    pe.wait_ge(yt_lo, count(s - 2, 3, o + 1))
                    if o < 2:
                        if (s - 3).exists():
                            pe.wait_ge(rot_ab, count(s - 3, 2, 2))
                    else:
                        if (s - 3).exists():
                            pe.wait_ge(v_ok, count(s - 3, 1, 1))
                    cols = slice(o * H, (o + 1) * H)
                    pe.matmul(psQ[:, o], c64[:], brow[:, cols], start=True, stop=False)
                    for kt in range(KH):
                        pe.matmul(psQ[:, o], yth[:, o, kt], wh[:, kt, cols], start=False, stop=False)
                        pe.matmul(psQ[:, o], yth[:, o, kt], wl[:, kt, cols], start=False, stop=False)
                        mm = pe.matmul(psQ[:, o], ytl[:, o, kt], wh[:, kt, cols], start=False, stop=(kt == KH - 1))
                    mm.then_inc(qkv_mm, 1)

                def body(s, p, live):
                    if live(1):
                        read(s, p, 0)
                        read(s, p, 1)
                    if live(2):
                        turn_y(s, 0)
                        turn_y(s, 1)
                        project(s, 0)
                    if live(1):
                        read(s, p, 2)
                        read(s, p, 3)
                    if live(2):
                        turn_y(s, 2)
                        project(s, 1)
                    if live(3):
                        turn_qk(s, 0)
                    if live(2):
                        project(s, 2)
                    if live(3):
                        turn_qk(s, 1)
                steps(pe, TILES, 3, 2, body)

            @block.vector
            def _(dve):
                def lo_y(s, o):
                    dve.wait_ge(yt_hi, count(s - 2, 3, o + 1))
                    dve.tensor_tensor(ytl[:, o], y_bank[o][:], yth[:, o], ALU.subtract).then_inc(yt_lo, 1)

                def lo_qk(s, r):
                    dve.wait_ge(qt_hi, count(s - 3, 2, r + 1))
                    dve.tensor_tensor(qtl[:, r], qk_bank[r][:], qth[:, r], ALU.subtract).then_inc(qt_lo, 1)

                lin = k["ln1"][:].rearrange("p t s -> p (t s)")

                def less_mean(s, half):
                    dve.wait_ge(x_norm, count(s - 1, 8, X_NEG))
                    dve.wait_ge(y_mm, count(s - 1, 4, 2 * half + 2))
                    if (s - 2).exists():
                        dve.wait_ge(yn_ok, count(s - 2, 3, 3))
                    tiles = slice(half * KD // 2, (half + 1) * KD // 2)
                    dve.scalar_tensor_tensor(yr[:, tiles].rearrange("p (b t) n -> p b (t n)", b=2),
                                             wsum[:].rearrange("p (h b n) -> p h b n", h=2, b=2)[:, half],
                                             sx[:, 1 - p_of(s), 1:2], psY[:, :, 0:4 * OW], ALU.mult, ALU.add)\
                       .then_inc(y_norm, 1)

                def p_of(s):
                    return s.off % 2

                def x_statistics(s, p):
                    dve.wait_ge(x_in[p], dma_count(s, 2, 2))
                    for j in range(4):
                        dve.bn_stats(bst[:, j], xc[:, p, j * 512:(j + 1) * 512]).then_inc(x_norm, 1)
                    dve.wait_ge(x_norm, count(s, 8, 4))
                    dve.sem_inc(k["settled"], 1)
                    dve.bn_aggr(sx[:, p, 3:5], bst[:]).then_inc(x_norm, 1)
                    dve.wait_ge(x_norm, count(s, 8, X_AGG))
                    dve.tensor_copy(lin[:, ds(s.at(2), 2)], sx[:, p, 3:5])
                    dve.tensor_scalar(sx[:, p, 0:1], sx[:, p, 4:5], EPS, None, ALU.add).then_inc(x_norm, 1)
                    dve.tensor_scalar(sx[:, p, 1:2], sx[:, p, 3:4], -1.0, None, ALU.mult).then_inc(x_norm, 1)
                    dve.wait_ge(x_norm, count(s, 8, X_EPS))
                    dve.reciprocal(sx[:, p, 2:3], sx[:, p, 0:1]).then_inc(x_norm, 1)

                def body(s, p, live):
                    if live(2):
                        lo_y(s, 0)
                        lo_y(s, 1)
                    if live(1):
                        less_mean(s, 0)
                    if live(0):
                        x_statistics(s, p)
                    if live(1):
                        less_mean(s, 1)
                    if live(2):
                        lo_y(s, 2)
                    if live(1):
                        dve.wait_ge(y_norm, count(s - 1, 11, Y_LESS))
                        for o in range(O):
                            dve.bn_stats(bsy[:, o], yr[:, :, o * HD:(o + 1) * HD]).then_inc(y_norm, 1)
                        dve.wait_ge(y_norm, count(s - 1, 11, Y_LESS + O))
                        dve.sem_inc(k["settled"], 1)
                        for o in range(O):
                            dve.bn_aggr(mv[:, o], bsy[:, o]).then_inc(y_norm, 1)
                        dve.wait_ge(y_norm, count(s - 1, 11, Y_AGG))
                        dve.tensor_scalar(sy[:, 0], mv[:, :, 1], sx[:, 1 - p, 2:3], EPS, ALU.mult, ALU.add).then_inc(y_norm, 1)
                        dve.wait_ge(y_norm, count(s - 1, 11, Y_VAR))
                        dve.reciprocal(sy[:, 4], sy[:, 0]).then_inc(y_norm, 1)
                        dve.wait_ge(y_norm, count(s - 1, 11, Y_INV))
                        dve.tensor_scalar(sy[:, 1], sy[:, 4], sx[:, 1 - p, 2:3], None, ALU.mult).then_inc(y_norm, 1)
                        dve.wait_ge(rr_ok, count(s - 1, 1, 1))
                        dve.scalar_tensor_tensor(sy[:, 3], mv[:, :, 0], -1.0, sy[:, 2], ALU.mult, ALU.mult)\
                           .then_inc(sh_ok, 1)
                    if live(2):
                        dve.wait_ge(qkv_mm, count(s - 2, 3, 2))
                        if (s - 3).exists():
                            dve.wait_ge(rot, count(s - 3, 1, 1))
                        src = psQ[:, 0:2].rearrange("p s (n j) -> p (s n) j", j=HD2)
                        cos = cosT[:].rearrange("p t j -> p (t j)")[:, ds((s - 2).at(HD2), HD2)]
                        sin = sinT[:].rearrange("p t s j -> p (t s j)")[:, ds((s - 2).at(HD), HD)]
                        dve.tensor_tensor(ra[:].rearrange("p (n j) -> p n j", j=HD2), src,
                                          spread(cos.unsqueeze(1), P, 2 * 2 * NH, HD2), ALU.mult).then_inc(rot_ab, 1)
                        swapped = psQ[:, 0:2].rearrange("p s (n x j) -> p (s n) x j", x=2, j=HD2)[:, :, ::-1, :]
                        dve.tensor_tensor(rb[:].rearrange("p (n x j) -> p n x j", x=2, j=HD2), swapped,
                                          spread(sin.rearrange("p (x j) -> p x j", x=2).unsqueeze(1),
                                                 P, 2 * NH, 2, HD2), ALU.mult).then_inc(rot_ab, 1)
                    if live(3):
                        lo_qk(s, 0)
                        lo_qk(s, 1)
                steps(dve, TILES, 3, 2, body)


def build_attention(nc, io, k):
    with ExitStack() as ctx:
        sb, ps, sem = allocators(nc, ctx, "s2_")
        RING = 4
        K3 = 3 * HD
        KM_ = K3 + 2
        qa = sb("a_q", [P, RING, L], F32R)
        ka = sb("a_k", [P, RING, L], F32R)
        base = [sum((QT - j) * P for j in range(ki)) for ki in range(QT + 1)]
        pt = sb("a_p", [P, 2, base[QT]])
        mx = sb("a_mx", [P, 12])
        mhl = sb("a_mhl", [P, 2, QT])
        mt = sb("a_mt", [2 * QT, P])
        rc = sb("a_rc", [P, QT])
        psS = [ps(f"psS{i}", [P, 512]) for i in range(2)]
        psX = [ps(f"psX{i}", [P, 512]) for i in range(3)]
        psO = ps("psO", [P, 2, 512])
        psM = ps("psM", [P, 512])

        units = []
        for qi in range(QT):
            end = (qi + 1) * P
            units += [(qi, a, min(end, a + 512) - a) for a in range(0, end, 512)]
        unitsT = []
        for ki in range(QT):
            a = ki * P
            while a < L:
                e = min(L, (a // 512 + 1) * 512)
                unitsT.append((ki, a, e - a))
                a = e
        U = len(units)
        assert U == len(unitsT) == 12
        halves = [u for u, (qi, a, n) in enumerate(units) if a]
        mcol = {u: (qi if a == 0 else QT + qi - 4) for u, (qi, a, n) in enumerate(units)}

        in_ = [sem(f"a_in{i}") for i in range(RING)]
        ones_ok = sem("a_ones")
        s_mm, mx_ok = sem("s_mm"), sem("mx_ok")
        m_ok = sem("m_ok")
        mt_mm, mt_ok, m_in = sem("mt_mm"), sem("mt_ok"), sem("m_in")
        x_mm, exp_ok = sem("x_mm"), sem("exp_ok")
        av_mm, rc_ok, o_ok = sem("av_mm"), sem("rc_ok"), sem("o_ok")

        with nc.Block() as block:
            @block.sync
            def _(sp):
                def body(s, p, live):
                    if live(2):
                        sp.wait_ge(mt_ok, count(s - 2, 1, 1))
                        sp.sem_inc(k["settled"], 1)
                        slot = (s.off - 2) % RING
                        for hl in range(2):
                            sp.dma_start(qa[K3 + hl:K3 + hl + 1, slot, :].bitcast(F32).rearrange("o (q j) -> o q j", j=P),
                                         mt[hl * QT:(hl + 1) * QT, :]).then_inc(m_in, 16)
                    if live(0):
                        if (s - 4).exists():
                            sp.wait_ge(x_mm, count(s - 4, U, U))
                        sp.sem_inc(k["settled"], 1)
                        rows = ds(s.at(HD), HD)
                        for dst, parts in ((qa, ((0, 0), (0, 0), (0, 1))), (ka, ((1, 0), (1, 1), (1, 0)))):
                            for j, (side, hl) in enumerate(parts):
                                sp.dma_start(dst[j * HD:(j + 1) * HD, p, :].bitcast(F32),
                                             io["qkT"][side, hl, rows, :]).then_inc(in_[p], 16)
                steps(sp, HEADS, 2, RING, body)

            @block.gpsimd
            def _(pool):
                pool.memset(ka[K3:KM_, :, :].bitcast(F32), 1.0).then_inc(ones_ok, 1)

            @block.tensor
            def _(pe):
                def scores(s, p, u):
                    qi, a, n = units[u]
                    if u == 0:
                        pe.wait_ge(in_[p], dma_count(s, RING, 6))
                    if due(s, U, u - 1):
                        pe.wait_ge(mx_ok, count(s, U, u - 1))
                    out = psS[u % 2]
                    diag = a + n == (qi + 1) * P
                    mm = pe.matmul(out[:, 0:n], qa[0:K3, p, qi * P:(qi + 1) * P], ka[0:K3, p, a:a + n],
                                   start=True, stop=not diag)
                    if diag:
                        mm = pe.matmul(out[:, n - P:n], k["ident_b"][:], k["mask_b"][:], start=False, stop=True)
                    mm.then_inc(s_mm, 1)

                def turn_max(s):
                    pe.wait_ge(m_ok, count(s - 1, 3, 3))
                    if (s - 2).exists():
                        pe.wait_ge(mt_ok, count(s - 2, 1, 1))
                    pe.transpose(psM[0:2 * QT, 0:P], mhl[:].rearrange("p h q -> p (h q)"), k["ident"][:])\
                      .then_inc(mt_mm, 1)

                def scoresT(s, slot, u):
                    ki, a, n = unitsT[u]
                    if u == 0:
                        pe.wait_ge(m_in, dma_count(s - 1, 1, 2))
                    if due(s - 1, U, u - 2):
                        pe.wait_ge(exp_ok, count(s - 1, U, u - 2))
                    out = psX[u % 3]
                    diag = a == ki * P
                    mm = pe.matmul(out[:, 0:n], ka[0:KM_, slot, ki * P:(ki + 1) * P], qa[0:KM_, slot, a:a + n],
                                   start=True, stop=not diag)
                    if diag:
                        mm = pe.matmul(out[:, 0:P], k["ident_b"][:], k["maskT_b"][:], start=False, stop=True)
                    mm.then_inc(x_mm, 1)

                def values(s, p, qi):
                    if qi == 0:
                        pe.wait_ge(exp_ok, count(s - 2, U, U))
                    if qi % 4 == 0:
                        if (s - 3).exists():
                            pe.wait_ge(o_ok, count(s - 3, 2, qi // 4 + 1))
                    out = psO[:, qi // 4, qi % 4 * VN:(qi % 4 + 1) * VN]
                    for ki in range(qi + 1):
                        at = base[ki] + (qi - ki) * P
                        mm = pe.matmul(out, pt[:, p, at:at + P],
                                       k["v_flat"][:, ds((s - 2).at(QT * (HD + 1), ki * (HD + 1)), VN)],
                                       start=(ki == 0), stop=(ki == qi))
                    if qi % 4 == 3:
                        mm.then_inc(av_mm, 1)

                pe.wait_ge(ones_ok, 1)

                def body(s, slot, live):
                    S = (lambda u: scores(s, slot, u)) if live(0) else (lambda u: None)
                    X = (lambda u: scoresT(s, (slot - 1) % RING, u)) if live(1) else (lambda u: None)
                    V = (lambda qi: values(s, slot % 2, qi)) if live(2) else (lambda qi: None)
                    S(0), V(0), S(1), V(1)
                    if live(1):
                        turn_max(s)
                    V(2), S(2), V(3), S(3), V(4)
                    for u in range(U):
                        X(u)
                        if u + 4 < U:
                            S(u + 4)
                        if u in (2, 5, 8):
                            V(5 + u // 3)
                steps(pe, HEADS, 2, RING, body)

            @block.vector
            def _(dve):
                def normalise(s, half):
                    dve.wait_ge(av_mm, count(s - 2, 2, half + 1))
                    view = psO[:, half, 0:4 * VN].rearrange("p (q n) -> p q n", n=VN)
                    dve.reciprocal(rc[:, 4 * half:4 * half + 4], view[:, :, HD]).then_inc(rc_ok, 1)
                    dve.wait_ge(rc_ok, count(s - 2, 2, half + 1))
                    at = (s - 2).at(QT * HD, 4 * half * HD)
                    out = k["o_sb"][:].rearrange("p n t d -> p (n t d)")[:, ds(at, 4 * HD)]
                    dve.tensor_tensor(out.rearrange("p (q d) -> p q d", d=HD), view[:, :, 0:HD],
                                      spread(rc[:, 4 * half:4 * half + 4].unsqueeze(2), P, 4, HD), ALU.mult)\
                       .then_inc(o_ok, 1)

                def body(s, slot, live):
                    for u in range(U):
                        if u == 4 and live(2):
                            normalise(s, 0)
                        if live(0):
                            qi, a, n = units[u]
                            dve.wait_ge(s_mm, count(s, U, u + 1))
                            if u == 0:
                                if (s - 1).exists():
                                    dve.wait_ge(m_ok, count(s - 1, 3, 3))
                            dve.tensor_reduce(mx[:, mcol[u]:mcol[u] + 1], psS[u % 2][:, 0:n], AX, ALU.max)\
                               .then_inc(mx_ok, 1)
                    if live(0):
                        dve.wait_ge(mx_ok, count(s, U, U))
                        dve.tensor_tensor(mx[:, 4:8], mx[:, 4:8], mx[:, 8:12], ALU.max).then_inc(m_ok, 1)
                        dve.wait_ge(m_ok, count(s, 3, 1))
                        if (s - 1).exists():
                            dve.wait_ge(mt_mm, count(s - 1, 1, 1))
                        dve.tensor_scalar(mhl[:, 0].bitcast(F32R), mx[:, 0:QT], -1.0, None, ALU.mult).then_inc(m_ok, 1)
                        dve.wait_ge(m_ok, count(s, 3, 2))
                        dve.scalar_tensor_tensor(mhl[:, 1].bitcast(F32R), mx[:, 0:QT], -1.0, mhl[:, 0], ALU.mult,
                                                 ALU.subtract).then_inc(m_ok, 1)
                    if live(2):
                        normalise(s, 1)
                steps(dve, HEADS, 2, RING, body)

            @block.scalar
            def _(act):
                def body(s, slot, live):
                    if live(1):
                        act.wait_ge(mt_mm, count(s - 1, 1, 1))
                        if (s - 2).exists():
                            act.wait_ge(m_in, dma_count(s - 2, 1, 2))
                        act.activation(mt[:].bitcast(F32R), psM[0:2 * QT, 0:P], ACT.Copy).then_inc(mt_ok, 1)
                        for u, (ki, a, n) in enumerate(unitsT):
                            act.wait_ge(x_mm, count(s - 1, U, u + 1))
                            if u == 0:
                                if (s - 3).exists():
                                    act.wait_ge(av_mm, count(s - 3, 2, 2))
                            at = base[ki] + a - ki * P
                            act.activation(pt[:, (slot - 1) % 2, at:at + n], psX[u % 3][:, 0:n], ACT.Exp,
                                           scale=float(1 / np.sqrt(np.float32(HD)))).then_inc(exp_ok, 1)
                steps(act, HEADS, 2, RING, body)


def build_write(nc, io, k, first):
    tag = "s3_" if first else "s5_"
    KY = KH if first else KM
    HW = H // 2
    S0 = DR + 1
    SA, SB, SK = slice(S0, S0 + NA), slice(S0 + NA, S0 + 2 * NA), slice(S0 + 2 * NA, S0 + 2 * NA + RH)
    WA, WB = HW + DR + NA, HW + NA + RH
    with ExitStack() as ctx:
        sb, ps, sem = allocators(nc, ctx, tag)
        wh = sb("w_wh", [P, KY, NW], F32R)
        wl = sb("w_wl", [P, KY, NW], F32R)
        bsm = sb("w_bsm", [P, DR + NAB])
        du = sb("w_du", [S0, H])
        one_c = sb("w_one", [P, 1])
        eps_c = sb("w_eps", [P, 1])
        sm = sb("w_sm", [P, 2, S0 + NAB])
        if first:
            lnx = sb("w_lnx", [P, TILES, 2])
            spf = sb("w_spf", [P, KD * 2 * HD + HD])
        psA, psB, psD, psL = (ps(n, [P, 512]) for n in ("w_psA", "w_psB", "w_psD", "w_psL"))
        psT = [ps(f"w_psT{i}", [P, 4, P]) for i in range(2)]
        if first:
            psR = ps("w_psR", [P, 2, 512])

        with ExitStack() as c:
            sb, _, sem = allocators(nc, c, tag)
            PT = 2
            RW = 2 if first else 4
            wraw = sb("w_raw", [P, RW, PT, NW])
            w_in = [sem(f"w_in{i}") for i in range(RW)]
            small_in, w_hi, w_lo = (sem(n) for n in ("small_in", "w_hi", "w_lo"))
            if first:
                prep, ln_e = sem("prep"), sem("ln_e")
                rw = sb("w_rw", [P, KD, 2])
                m32 = sb("w_m32", [P, HD])
            name = "1" if first else "2"
            parts = KY // PT
            with nc.Block() as block:
                @block.sync
                def _(sp):
                    sp.dma_start(bsm[:], io["bsm" + name]).then_inc(small_in, 16)
                    sp.dma_start(du[:], io["du" + name]).then_inc(small_in, 16)
                    if first:
                        sp.dma_start(rw[:], io["wr2"]).then_inc(small_in, 16)
                    for i in range(parts):
                        if i >= RW:
                            sp.wait_ge(w_lo, i + 1 - RW)
                        sp.dma_start(wraw[:, i % RW], io["wo" + name][:, i * PT:(i + 1) * PT]).then_inc(w_in[i % RW], 16)
                    sp.wait_ge(small_in, 48 if first else 32)

                @block.scalar
                def _(act):
                    if first:
                        act.wait_ge(ln_e, 1)
                        act.activation(lnx[:, :, 1], k["ln1"][:, :, 1], ACT.Ln, bias=eps_c[:]).then_inc(ln_e, 1)
                        act.wait_ge(ln_e, 2)
                        act.activation(lnx[:, :, 0], lnx[:, :, 1], ACT.Exp, scale=-0.5).then_inc(ln_e, 1)
                    for i in range(parts):
                        act.wait_ge(w_in[i % RW], 16 * (i // RW + 1))
                        act.activation(wh[:, i * PT:(i + 1) * PT], wraw[:, i % RW], ACT.Copy).then_inc(w_hi, 1)

                @block.vector
                def _(dve):
                    dve.memset(one_c[:], 1.0)
                    made = dve.memset(eps_c[:], EPS)
                    if first:
                        made.then_inc(ln_e, 1)
                    dve.memset(sm[:, :, DR:S0], 1.0)
                    if first:
                        dve.wait_ge(small_in, 48)
                        dve.memset(spf[:, 0:HD], 0.0)
                        dve.tensor_reduce(m32[:], k["ident"][:].rearrange("p (c j) -> p j c", c=C), AX, ALU.max)\
                           .then_inc(prep, 1)
                        dve.wait_ge(prep, 1)
                        dve.tensor_tensor(spf[:, HD:].rearrange("p (t j) -> p t j", j=HD),
                                          spread(rw[:].rearrange("p t o -> p (t o)").unsqueeze(2), P, KD * 2, HD),
                                          spread(m32[:].unsqueeze(1), P, KD * 2, HD), ALU.mult)
                        dve.wait_ge(ln_e, 3)
                        dve.scalar_tensor_tensor(lnx[:, :, 1], k["ln1"][:, :, 0], -1.0, lnx[:, :, 0], ALU.mult, ALU.mult)
                    for i in range(parts):
                        dve.wait_ge(w_hi, i + 1)
                        part = slice(i * PT, (i + 1) * PT)
                        dve.tensor_tensor(wl[:, part], wraw[:, i % RW], wh[:, part], ALU.subtract).then_inc(w_lo, 1)

        sb, ps, sem = allocators(nc, ctx, tag)
        yraw = sb("w_y", [P, 1 if first else 2, KY, P])
        yh = sb("w_yh", [P, KY, P], F32R)
        yl = sb("w_yl", [P, KY, P], F32R)
        hin = sb("w_hin", [P, 2, D])
        hs = sb("w_hs", [P, D]) if first else None
        xin = None if first else sb("w_xin", [P, D])
        outs = sb("w_out", [P, 2, H])
        sp_ = sb("w_sp", [P, H + NA])
        delta = sb("w_delta", [P, H])
        gate = sb("w_gate", [P, 3, NA])
        ab = sb("w_ab", [P, C - 1, H])
        g = sb("w_g", [P, C - 1, H])
        ha = sb("w_ha", [P, C - 1, H])
        sk = sb("w_sk", [P, H])
        res = sb("w_res", [P, 2, D])
        hT = sb("w_hT", [P, KD, P])
        dlT = sb("w_dlT", [S0, P])
        st = sb("w_st", [P, 4])
        if first:
            yn = sb("w_yn", [P, 2, H])
            gT = sb("w_gT", [P, 2, KH, P])
            nst = sb("w_nst", [P, 2, 6])
            nmv = sb("w_nmv", [P, 2, 2])
            nsc = sb("w_nsc", [P, 3, 2])
        else:
            xn = sb("w_xn", [P, D])
            nst = sb("w_nst", [P, 4, 6])
            nsc = sb("w_nsc", [P, 1])

        if first:
            o_ok, o_mm = sem("o_ok"), sem("o_mm")
            hs_ok = sem("hs_ok")
            r_mm, n_e = sem("r_mm"), sem("n_e")
            nrm_ok = sem("nrm_ok")
            g_mm, g_ev, g_ev2 = sem("g_mm"), sem("g_ev"), sem("g_ev2")
        else:
            y_in = [sem(f"y_in{p}") for p in range(2)]
            xn_ok = sem("xn_ok")
            xin_in = sem("xin_in")
        h_in = [sem(f"h_in{p}") for p in range(2)]
        y_hi, y_lo = sem("y_hi"), sem("y_lo")
        ab_mm = sem("ab_mm")
        sm_ok, out_ok = sem("sm_ok"), sem("out_ok")
        dl_mm, dl_ok, d_mm = sem("dl_mm"), sem("dl_ok"), sem("d_mm")
        sp_e = sem("sp_e")
        gate_e = sem("gate_e")
        g_ok, skip_e = sem("g_ok"), sem("skip_e")
        bar_ok, ha_ok = sem("bar_ok"), sem("ha_ok")
        b_ok = sem("b_ok")
        res_e = sem("res_e")
        R = 2 if first else 3
        st_e = sem("st_e")
        t_mm, t_ev = sem("t_mm"), sem("t_ev")
        t_ev2 = sem("t_ev2")
        if not first:
            ln_e, sc_ok = sem("ln_e"), sem("sc_ok")
        st_out = [sem(f"st_out{p}") for p in range(2)]
        t_out = sem("t_out")
        NE = 7

        def place(tile):
            n = tile.at()
            return n // QT, n % QT

        def planes(ap, blocks=False):
            return ap.rearrange("p (t c j) -> p c t j" if blocks else "p (c t j) -> p c t j", c=C, j=HD)

        def cells(ap):
            return ap.rearrange("p c (t j) -> p c t j", j=HD)

        LAST = 4 if first else 3
        with nc.Block() as block:
            @block.sync
            def _(sp):
                def body(s, p, live):
                    if live(0) and not first:
                        if (s - 2).exists():
                            sp.wait_ge(y_lo, count(s - 2, 2, 2))
                        sp.sem_inc(k["settled"], 1)
                        sp.dma_start(yraw[:, p].rearrange("p t j -> p (t j)"),
                                     io["mlpT"][ds(s.at(), 1)].rearrange("o p f -> (o p) f")).then_inc(y_in[p], 16)
                    d = LAST + 1
                    if live(d):
                        ev, ev2, buf, name = (g_ev, g_ev2, gT, "giT") if first else (t_ev, t_ev2, hT, "xnT")
                        n = 1 if first else 2
                        sp.wait_ge(ev, count(s - d, n, n))
                        sp.sem_inc(k["settled"], 1)
                        sp.wait_ge(ev2, count(s - d, n, n))
                        sp.sem_inc(k["settled"], 1)
                        src = buf[:].rearrange("p o t j -> p (o t j)") if first else buf[:].rearrange("p t j -> p (t j)")
                        sp.dma_start(io[name][ds((s - d).at(), 1)].rearrange("o p f -> (o p) f"), src)\
                          .then_inc(t_out, 16)
                    if live(4):
                        sp.wait_ge(res_e, count(s - 4, R, R))
                        sp.sem_inc(k["settled"], 1)
                        sp.dma_start(io["hs2" if first else "x3"][ds((s - 4).at(P), P), :], res[:, p])\
                          .then_inc(st_out[p], 16)
                    if live(2) and not first:
                        if (s - 3).exists():
                            sp.wait_ge(res_e, count(s - 3, R, R))
                        sp.sem_inc(k["settled"], 1)
                        sp.dma_start(xin[:], io["xP"][ds((s - 2).at(P), P), :]).then_inc(xin_in, 16)
                    if live(1):
                        q = 1 - p
                        if first and (s - 3).exists():
                            sp.wait_ge(hs_ok, count(s - 3, 1, 1))
                        if not first and (s - 3).exists():
                            sp.wait_ge(ha_ok, count(s - 3, 1, 1))
                        sp.sem_inc(k["settled"], 1)
                        if not first and (s - 3).exists():
                            sp.wait_ge(res_e, count(s - 3, R, 1))
                        sp.sem_inc(k["settled"], 1)
                        sp.dma_start(hin[:, q], io["xP" if first else "hs2"][ds((s - 1).at(P), P), :])\
                          .then_inc(h_in[q], 16)
                steps(sp, TILES, LAST + 1, 2, body, LAST + 1)
                sp.wait_ge(t_out, 16 * TILES)
                for out in st_out:
                    sp.wait_ge(out, 16 * TILES // len(st_out))

            @block.tensor
            def _(pe):
                def turn_residual(s, p, groups):
                    src = res[:, 1 - p] if first else xn[:]
                    for j in groups:
                        if j == 0:
                            if first:
                                pe.wait_ge(res_e, count(s - 3, R, R))
                                pe.wait_ge(y_hi, count(s, 2, 2))
                                pe.wait_ge(y_lo, count(s, 2, 2))
                                if (s - 5).exists():
                                    pe.wait_ge(g_ev, count(s - 5, 1, 1))
                            else:
                                pe.wait_ge(xn_ok, count(s - 3, 1, 1))
                                if (s - 4).exists():
                                    pe.wait_ge(t_ev, count(s - 4, 2, 2))
                        elif j == 1:
                            if first and (s - 5).exists():
                                pe.wait_ge(g_ev2, count(s - 5, 1, 1))
                            if not first and (s - 4).exists():
                                pe.wait_ge(t_ev2, count(s - 4, 2, 2))
                        else:
                            pe.wait_ge((t_ev, t_ev2)[j % 2], count(s - 3, 2, 1))
                        for i in range(4):
                            kt = 4 * j + i
                            mm = pe.transpose(psT[j % 2][:, i], src[:, kt * P:(kt + 1) * P], k["ident"][:])
                        mm.then_inc(t_mm, 1)

                def read(s):
                    if (s - 4).exists():
                        pe.wait_ge(n_e, count(s - 4, NE, 2))
                    if (s - 4).exists():
                        pe.wait_ge(nrm_ok, count(s - 4, 2, 2))
                    pe.wait_ge(t_ev, count(s - 3, 2, 2))
                    pe.wait_ge(t_ev2, count(s - 3, 2, 2))
                    for half in range(2):
                        for i in reversed(range(8)):
                            kt = 8 * half + i
                            lead = HD if i else 0
                            mm = pe.matmul(psR[:, half, i * 2 * HD - lead:(i + 1) * 2 * HD], hT[:, kt],
                                           spf[:, HD + kt * 2 * HD - lead:HD + (kt + 1) * 2 * HD],
                                           start=True, stop=True)
                    mm.then_inc(r_mm, 1)

                def product(s):
                    if (s - 2).exists():
                        pe.wait_ge(sm_ok, count(s - 2, 2, 2))
                    if (s - 2).exists():
                        pe.wait_ge(out_ok, count(s - 2, 2, 2))
                    for kt in range(KY):
                        if kt % (KY // 2) == 0:
                            pe.wait_ge(y_hi, count(s - 1, 2, kt // (KY // 2) + 1))
                            pe.wait_ge(y_lo, count(s - 1, 2, kt // (KY // 2) + 1))
                        for a, b in ((yh, wh), (yh, wl), (yl, wh)):
                            for bank, cols in ((psA, slice(0, WA)), (psB, slice(WA, NW))):
                                mm = pe.matmul(bank[:, 0:cols.stop - cols.start], a[:, kt], b[:, kt, cols],
                                               start=(kt == 0 and b is wh and a is yh), stop=(kt == KY - 1 and a is yl))
                        if kt % (KY // 2) == KY // 2 - 1:
                            mm.then_inc(ab_mm, 1)

                def body(s, p, live):
                    if live(1):
                        product(s)
                    if live(0) and first:
                        pe.wait_ge(o_ok, count(s, 1, 1))
                        if (s - 5).exists():
                            pe.wait_ge(g_ev, count(s - 5, 1, 1))
                        if (s - 4).exists():
                            pe.wait_ge(t_ev, count(s - 4, 2, 2))
                        if (s - 1).exists():
                            pe.wait_ge(y_hi, count(s - 1, 2, 2))
                            pe.wait_ge(y_lo, count(s - 1, 2, 2))
                        for c in range(KH):
                            mm = pe.transpose(psT[0][:, c], yraw[:, 0, c], k["ident"][:])
                        mm.then_inc(o_mm, 1)
                    if live(1):
                        pe.wait_ge(sm_ok, count(s - 1, 2, 1))
                        if (s - 2).exists():
                            pe.wait_ge(dl_ok, count(s - 2, 1, 1))
                        pe.transpose(psL[0:S0, 0:P], sm[:, 1 - p, 0:S0], k["ident"][:]).then_inc(dl_mm, 1)
                    if live(3):
                        turn_residual(s, p, (0, 1))
                    if live(3):
                        turn_residual(s, p, (2, 3))
                    if live(1):
                        pe.wait_ge(dl_ok, count(s - 1, 1, 1))
                        if (s - 2).exists():
                            pe.wait_ge(gate_e, count(s - 2, 6, 1))
                        pe.matmul(psD[:], dlT[:], du[:], start=True, stop=True).then_inc(d_mm, 1)
                    if live(4) and first:
                        for o in range(2):
                            pe.wait_ge(nrm_ok, count(s - 4, 2, o + 1))
                            pe.wait_ge((t_ev, t_ev2)[o], count(s - 3, 2, 2))
                            if not live(3):
                                pe.wait_ge((g_ev, g_ev2)[o], count(s - 5, 1, 1))
                            for c in range(KH):
                                mm = pe.transpose(psT[o][:, c], yn[:, o, c * P:(c + 1) * P], k["ident"][:])
                            mm.then_inc(g_mm, 1)
                    if live(3) and first:
                        read(s)
                steps(pe, TILES, LAST, 2, body, LAST + 1)

            @block.scalar
            def _(act):
                act.add_instruction(mybir.InstLoadActFuncSet(
                    name=nc.get_next_instruction_name(), engine=mybir.EngineType.Activation, act_func_set_id=EXP_LN_SET))

                def hi_y(s, p, half):
                    part = slice(half * KY // 2, (half + 1) * KY // 2)
                    if (s - 1).exists():
                        act.wait_ge(ab_mm, count(s - 1, 2, half + 1))
                    if half == 0 and first:
                        act.wait_ge(o_mm, count(s, 1, 1))
                    if half == 0 and not first:
                        act.wait_ge(y_in[p], dma_count(s, 2, 1))
                    src = psT[0][:, part] if first else yraw[:, p, part]
                    act.activation(yh[:, part], src, ACT.Copy).then_inc(y_hi, 1)

                def outputs(s, r):
                    act.wait_ge(ab_mm, count(s - 1, 2, 2))
                    if (s - 3).exists():
                        act.wait_ge(g_ok, count(s - 3, 1, 1))
                    if (s - 3).exists():
                        act.wait_ge(skip_e, count(s - 3, 2, 2))
                    act.wait_ge(sm_ok, count(s - 1, 2, 1))
                    act.activation(outs[:, r, 0:HW], psA[:, 0:HW], ACT.Copy).then_inc(out_ok, 1)
                    act.wait_ge(sm_ok, count(s - 1, 2, 2))
                    act.activation(outs[:, r, HW:H], psB[:, 0:HW], ACT.Copy).then_inc(out_ok, 1)
                    act.wait_ge(dl_mm, count(s - 1, 1, 1))
                    if (s - 2).exists():
                        act.wait_ge(d_mm, count(s - 2, 1, 1))
                    act.activation(dlT[:], psL[0:S0, 0:P], ACT.Copy).then_inc(dl_ok, 1)

                def evacuate(s, j):
                    act.wait_ge(t_mm, count(s - 3, 4, j + 1))
                    if first and (s - 4).exists():
                        act.wait_ge(r_mm, count(s - 4, 1, 1))
                    if not first and (s - 4).exists():
                        act.wait_ge(t_out, dma_count(s - 4, 1, 1))
                    act.activation(hT[:, 4 * j:4 * j + 4], psT[0][:], ACT.Copy).then_inc(t_ev, 1)

                def body(s, p, live):
                    q = p
                    if live(0) and first:
                        b_, kt_ = place(s)
                        if (s - 1).exists():
                            act.wait_ge(o_mm, count(s - 1, 1, 1))
                        src = k["o_sb"][:].rearrange("p (b n) t d -> p b n t d", b=B)
                        src = src[:, ds(b_, 1), :, ds(kt_, 1), :].rearrange("p b n t d -> p (b n) (t d)")
                        act.activation(yraw[:, 0].rearrange("p t (n d) -> p (t n) d", d=HD), src, ACT.Copy)\
                           .then_inc(o_ok, 1)
                    if live(4) and first:
                        act.wait_ge(n_e, count(s - 4, NE, 4))
                        act.activation(nsc[:, 0], nmv[:, :, 1], ACT.Ln, bias=eps_c[:]).then_inc(n_e, 1)
                        act.wait_ge(n_e, count(s - 4, NE, 5))
                        act.activation(nsc[:, 1], nsc[:, 0], ACT.Exp, scale=-0.5).then_inc(n_e, 1)
                    if live(2):
                        act.wait_ge(d_mm, count(s - 2, 1, 1))
                        if (s - 3).exists():
                            act.wait_ge(gate_e, count(s - 3, 6, 2))
                        act.activation(sp_[:, 0:H], psD[:], ACT.Abs).then_inc(sp_e, 1)
                        act.wait_ge(sm_ok, count(s - 2, 2, 1))
                        act.activation(sp_[:, H:], sm[:, q, SA], ACT.Abs).then_inc(sp_e, 1)
                        act.wait_ge(sp_e, count(s - 2, 4, 2))
                        act.activation(sp_[:], sp_[:], ACT.Exp, scale=-1.0).then_inc(sp_e, 1)
                        act.wait_ge(sp_e, count(s - 2, 4, 3))
                        act.activation(sp_[:], sp_[:], ACT.Ln, bias=one_c[:]).then_inc(sp_e, 1)
                    if live(1) and first:
                        outputs(s, 1 - p)
                    if live(0) and first:
                        hi_y(s, p, 0)
                        hi_y(s, p, 1)
                    if live(2) and first:
                        act.wait_ge(st_e, count(s - 2, 1, 1))
                        act.wait_ge(h_in[q], dma_count(s - 2, 2, 1))
                        if (s - 3).exists():
                            act.wait_ge(ha_ok, count(s - 3, 1, 1))
                        if (s - 3).exists():
                            act.wait_ge(res_e, count(s - 3, R, 2))
                        act.activation(hs[:], hin[:, q], ACT.Identity, scale=st[:, 0:1], bias=st[:, 1:2])\
                           .then_inc(hs_ok, 1)
                    if live(3) and not first:
                        act.wait_ge(st_e, count(s - 3, 5, 5))
                        act.activation(nsc[:], st[:, 1:2], ACT.Ln, bias=eps_c[:]).then_inc(ln_e, 1)
                        act.wait_ge(ln_e, count(s - 3, 2, 1))
                        act.activation(st[:, 2:3], nsc[:], ACT.Exp, scale=-0.5).then_inc(ln_e, 1)
                        act.wait_ge(sc_ok, count(s - 3, 1, 1))
                        if (s - 4).exists():
                            act.wait_ge(t_mm, count(s - 4, 4, 4))
                        act.activation(xn[:], res[:, 1 - p], ACT.Identity, scale=st[:, 2:3], bias=st[:, 3:4])\
                           .then_inc(xn_ok, 1)
                    if live(2):
                        act.wait_ge(gate_e, count(s - 2, 6, 6))
                        act.activation(ab[:], ab[:], ACT.Exp).then_inc(bar_ok, 1)
                    if live(4) and first:
                        act.wait_ge(n_e, count(s - 4, NE, 7))
                        if (s - 5).exists():
                            act.wait_ge(g_mm, count(s - 5, 2, 2))
                        for o in range(2):
                            act.activation(yn[:, o].rearrange("p (b t j) -> p b t j", b=2, j=HD),
                                           psR[:].rearrange("p b (t o j) -> p b t o j", o=2, j=HD)[:, :, :, o],
                                           ACT.Identity, scale=nsc[:, 1, o:o + 1], bias=nsc[:, 2, o:o + 1])\
                               .then_inc(nrm_ok, 1)
                    if live(0) and not first:
                        hi_y(s, p, 0)
                    if live(1) and not first:
                        outputs(s, 1 - p)
                    if live(3):
                        evacuate(s, 0)
                    if live(0) and not first:
                        hi_y(s, p, 1)
                    if live(3):
                        evacuate(s, 2)
                    if live(4) and first:
                        act.wait_ge(g_mm, count(s - 4, 2, 1))
                        if (s - 5).exists():
                            act.wait_ge(t_out, dma_count(s - 5, 1, 1))
                        act.activation(gT[:, 0], psT[0][:], ACT.Copy).then_inc(g_ev, 1)
                steps(act, TILES, LAST, 2, body, LAST + 1)

            @block.gpsimd
            def _(pool):
                def body(s, p, live):
                    q = p
                    if live(2):
                        pool.wait_ge(gate_e, count(s - 2, 6, 1))
                        if (s - 3).exists():
                            pool.wait_ge(res_e, count(s - 3, R, 2))
                        pool.tensor_tensor(sk[:].rearrange("p (s r) -> p s r", r=RH),
                                           delta[:].rearrange("p (s r) -> p s r", r=RH),
                                           spread(sm[:, q, SK].unsqueeze(1), P, HS, RH), ALU.mult).then_inc(skip_e, 1)
                        pool.wait_ge(gate_e, count(s - 2, 6, 5))
                        pool.wait_ge(out_ok, count(s - 2, 2, 2))
                        for c in range(C - 1):
                            mm = pool.tensor_tensor(
                                g[:, c].rearrange("p (s r) -> p s r", r=RH),
                                outs[:, q].rearrange("p (s r) -> p s r", r=RH),
                                spread(gate[:, 2].rearrange("p (r c) -> p c r", c=C - 1)[:, c:c + 1], P, HS, RH), ALU.mult)
                        mm.then_inc(g_ok, 1)
                        pool.wait_ge(skip_e, count(s - 2, 2, 1))
                        pool.tensor_tensor(sk[:], sk[:], outs[:, q], ALU.mult).then_inc(skip_e, 1)
                        pool.wait_ge(bar_ok, count(s - 2, 1, 1))
                        if first:
                            pool.wait_ge(hs_ok, count(s - 2, 1, 1))
                            src = planes(hs[:])
                        else:
                            pool.wait_ge(h_in[q], dma_count(s - 2, 2, 1))
                            src = planes(hin[:, q], blocks=True)
                        pool.tensor_tensor(cells(ha[:]), cells(ab[:]), src[:, 0:C - 1], ALU.mult).then_inc(ha_ok, 1)
                steps(pool, TILES, LAST, 2, body, LAST + 1)

            @block.vector
            def _(dve):
                lin = lnx[:].rearrange("p t s -> p (t s)") if first else None

                def gates(s, q):
                    dve.wait_ge(sp_e, count(s - 2, 4, 4))
                    if (s - 3).exists():
                        dve.wait_ge(g_ok, count(s - 3, 1, 1))
                    if (s - 3).exists():
                        dve.wait_ge(skip_e, count(s - 3, 2, 1))
                    dve.scalar_tensor_tensor(delta[:], psD[:], 0.0, sp_[:, 0:H], ALU.max, ALU.add).then_inc(gate_e, 1)
                    dve.scalar_tensor_tensor(gate[:, 1], sm[:, q, SA], 0.0, sp_[:, H:], ALU.max, ALU.add)\
                       .then_inc(gate_e, 1)
                    dve.wait_ge(gate_e, count(s - 2, 6, 2))
                    dve.tensor_scalar(gate[:, 0], gate[:, 1], -1.0, None, ALU.mult)
                    dve.tensor_scalar(gate[:, 1], gate[:, 1], -1.0, -1e-5, ALU.mult, ALU.add).then_inc(gate_e, 1)
                    dve.wait_ge(gate_e, count(s - 2, 6, 3))
                    dve.reciprocal(gate[:, 1], gate[:, 1]).then_inc(gate_e, 1)
                    dve.wait_ge(gate_e, count(s - 2, 6, 4))
                    dve.tensor_tensor(gate[:, 2], gate[:, 1], sm[:, q, SB], ALU.mult).then_inc(gate_e, 1)
                    if (s - 3).exists():
                        dve.wait_ge(ha_ok, count(s - 3, 1, 1))
                    for c in range(C - 1):
                        mm = dve.tensor_tensor(
                            ab[:, c].rearrange("p (s r) -> p s r", r=RH), delta[:].rearrange("p (s r) -> p s r", r=RH),
                            spread(gate[:, 0].rearrange("p (r c) -> p c r", c=C - 1)[:, c:c + 1], P, HS, RH), ALU.mult)
                    mm.then_inc(gate_e, 1)

                flat = lambda b: b[:].rearrange("p c h -> p (c h)")

                def update(s, q):
                    dve.wait_ge(bar_ok, count(s - 2, 1, 1))
                    dve.wait_ge(g_ok, count(s - 2, 1, 1))
                    dve.scalar_tensor_tensor(flat(g), flat(ab), -1.0, flat(g), ALU.add, ALU.mult).then_inc(b_ok, 1)
                    dve.wait_ge(skip_e, count(s - 2, 2, 2))
                    if (s - 4).exists():
                        if first:
                            dve.wait_ge(t_mm, count(s - 4, 4, 4))
                        else:
                            dve.wait_ge(xn_ok, count(s - 4, 1, 1))
                        dve.wait_ge(st_out[q], dma_count(s - 4, 2, 1))
                    if first:
                        dst, src = planes(res[:, q], blocks=True), planes(hs[:])
                        dve.wait_ge(hs_ok, count(s - 2, 1, 1))
                    else:
                        dst, src = planes(res[:, q]), planes(hin[:, q], blocks=True)
                        dve.wait_ge(h_in[q], dma_count(s - 2, 2, 1))
                    dve.tensor_tensor(dst[:, C - 1], sk[:].rearrange("p (t j) -> p t j", j=HD), src[:, C - 1], ALU.add)\
                       .then_inc(res_e, 1)

                def join(s, q):
                    row = res[:, q]
                    dst = planes(row, blocks=first)
                    dve.wait_ge(ha_ok, count(s - 3, 1, 1))
                    dve.wait_ge(b_ok, count(s - 3, 1, 1))
                    dve.tensor_tensor(dst[:, 0:C - 1], cells(ha[:]), cells(g[:]), ALU.add).then_inc(res_e, 1)
                    if not first:
                        dve.wait_ge(xin_in, dma_count(s - 3, 1, 1))
                        dve.wait_ge(res_e, count(s - 3, R, 2))
                        dve.tensor_tensor(row, row, xin[:], ALU.add).then_inc(res_e, 1)

                def statistics(s, q):
                    row = res[:, q]
                    dve.wait_ge(res_e, count(s - 3, R, 3))
                    for j in range(4):
                        dve.bn_stats(nst[:, j], row[:, j * 512:(j + 1) * 512]).then_inc(st_e, 1)
                    dve.wait_ge(st_e, count(s - 3, 5, 4))
                    dve.sem_inc(k["settled"], 1)
                    dve.bn_aggr(st[:, 0:2], nst[:]).then_inc(st_e, 1)
                    dve.wait_ge(ln_e, count(s - 3, 2, 2))
                    dve.scalar_tensor_tensor(st[:, 3:4], st[:, 0:1], -1.0, st[:, 2:3], ALU.mult, ALU.mult)\
                       .then_inc(sc_ok, 1)

                def small(s, r):
                    dve.wait_ge(ab_mm, count(s - 1, 2, 2))
                    dve.tensor_tensor(sm[:, r, 0:DR], psA[:, HW:HW + DR], bsm[:, 0:DR], ALU.add)
                    dve.tensor_tensor(sm[:, r, SA], psA[:, HW + DR:WA], bsm[:, DR:DR + NA], ALU.add)\
                       .then_inc(sm_ok, 1)
                    dve.tensor_tensor(sm[:, r, S0 + NA:], psB[:, HW:WB], bsm[:, DR + NA:], ALU.add).then_inc(sm_ok, 1)

                def lo_y(s, p, half):
                    part = slice(half * KY // 2, (half + 1) * KY // 2)
                    dve.wait_ge(y_hi, count(s, 2, 2 if first else half + 1))
                    src = psT[0][:, part] if first else yraw[:, p, part]
                    dve.tensor_tensor(yl[:, part], src, yh[:, part], ALU.subtract).then_inc(y_lo, 1)

                def body(s, p, live):
                    q = p
                    if live(3):
                        join(s, 1 - p)
                    if live(4) and first:
                        dve.wait_ge(r_mm, count(s - 4, 1, 1))
                        view = psR[:].rearrange("p b (t o j) -> p b t o j", o=2, j=HD)
                        for o in range(2):
                            dve.bn_stats(nst[:, o], view[:, :, :, o]).then_inc(n_e, 1)
                        dve.wait_ge(n_e, count(s - 4, NE, 2))
                        dve.sem_inc(k["settled"], 1)
                        for o in range(2):
                            dve.bn_aggr(nmv[:, o], nst[:, o:o + 1]).then_inc(n_e, 1)
                    if live(2) and first:
                        if (s - 3).exists():
                            dve.wait_ge(hs_ok, count(s - 3, 1, 1))
                        dve.tensor_copy(st[:, 0:2], lin[:, ds((s - 2).at(2), 2)]).then_inc(st_e, 1)
                    if live(4) and first:
                        dve.wait_ge(n_e, count(s - 4, NE, 6))
                        dve.scalar_tensor_tensor(nsc[:, 2], nmv[:, :, 0], -1.0, nsc[:, 1], ALU.mult, ALU.mult)\
                           .then_inc(n_e, 1)
                    if live(1) and first:
                        small(s, 1 - p)
                    if live(2):
                        gates(s, q)
                    if live(3) and not first:
                        statistics(s, 1 - p)
                    if live(0) and first:
                        lo_y(s, p, 0)
                        lo_y(s, p, 1)
                    if live(0) and not first:
                        lo_y(s, p, 0)
                    if live(1) and not first:
                        small(s, 1 - p)
                    if live(0) and not first:
                        lo_y(s, p, 1)
                    if live(3):
                        for j in (1, 3):
                            dve.wait_ge(t_mm, count(s - 3, 4, j + 1))
                            if first and (s - 4).exists():
                                dve.wait_ge(r_mm, count(s - 4, 1, 1))
                            if not first and (s - 4).exists():
                                dve.wait_ge(t_out, dma_count(s - 4, 1, 1))
                            dve.tensor_copy(hT[:, 4 * j:4 * j + 4], psT[1][:]).then_inc(t_ev2, 1)
                    if live(2):
                        update(s, q)
                    if live(4) and first:
                        dve.wait_ge(g_mm, count(s - 4, 2, 2))
                        if (s - 5).exists():
                            dve.wait_ge(t_out, dma_count(s - 5, 1, 1))
                        dve.tensor_copy(gT[:, 1], psT[1][:]).then_inc(g_ev2, 1)
                steps(dve, TILES, LAST, 2, body, LAST + 1)


def build_mlp(nc, io, k):
    CH = 4
    NC_ = TILES // CH
    with ExitStack() as ctx:
        sb, ps, sem = allocators(nc, ctx, "s4_")
        RR = 4
        xh = sb("m_xh", [P, TILES, 2 * KH, P], F32R)
        xl = sb("m_xl", [P, TILES, 2 * KH, P], F32R)
        raw = sb("m_raw", [P, RR, 2 * KH, P])
        gam = sb("m_gam", [P, 2 * KH])
        bet = sb("m_bet", [P, 2 * KH])
        wraw = sb("m_wraw", [P, 2, 2 * KH, P])
        wh = sb("m_wh", [P, 2, 2 * KH, P], F32R)
        wl = sb("m_wl", [P, 2, 2 * KH, P], F32R)
        sil = sb("m_sil", [P, 2, CH * P])
        mo = sb("m_mo", [P, 2, NC_, CH * P])
        psG = [ps(f"m_psG{i}", [P, CH * P]) for i in range(NC_)]
        psU = [ps(f"m_psU{i}", [P, CH * P]) for i in range(NC_)]

        small_in = sem("small_in")
        r_in = [sem(f"r_in{p}") for p in range(RR)]
        gam_ok, bet_ok, x_hi, x_lo = sem("gam_ok"), sem("bet_ok"), sem("x_hi"), sem("x_lo")
        w_in = [sem(f"w_in{p}") for p in range(2)]
        w_hi, w_lo = sem("w_hi"), sem("w_lo")
        mm_g, mm_u = sem("mm_g"), sem("mm_u")
        sil_ok, mo_ok = sem("sil_ok"), sem("mo_ok")
        mo_out = [sem(f"mo_out{p}") for p in range(2)]

        with nc.Block() as block:
            @block.sync
            def _(sp):
                sp.dma_start(gam[:], io["g2"]).then_inc(small_in, 16)
                sp.dma_start(bet[:], io["b2"]).then_inc(small_in, 16)

                def load_weights(s, p):
                    if (s - 2).exists():
                        sp.wait_ge(w_lo, count(s - 2, 1, 1))
                    sp.sem_inc(k["settled"], 1)
                    sp.dma_start(wraw[:, p].rearrange("p t j -> p (t j)"),
                                 io["wmlp"][ds(s.at(), 1)].rearrange("o p f -> (o p) f")).then_inc(w_in[p], 16)

                def load_reads(s, p, live):
                    if not live(0):
                        return
                    if (s - RR).exists():
                        sp.wait_ge(x_lo, count(s - RR, 1, 1))
                    sp.sem_inc(k["settled"], 1)
                    sp.dma_start(raw[:, p].rearrange("p t j -> p (t j)"),
                                 io["giT"][ds(s.at(), 1)].rearrange("o p f -> (o p) f")).then_inc(r_in[p], 16)

                def body(s, p, live):
                    if live(0) and not (s.reg is None and s.off < 2):
                        load_weights(s, p)
                    if live(2):
                        sp.wait_ge(mo_ok, count(s - 2, NC_, NC_))
                        sp.sem_inc(k["settled"], 1)
                        dst = io["mlpT"].rearrange("t p (m j) -> p t m j", j=P)[:, :, ds((s - 2).at(), 1), :]
                        dst = dst.rearrange("p t o j -> p t (o j)")
                        sp.dma_start(dst, mo[:, p].rearrange("p c (t j) -> p (c t) j", j=P)).then_inc(mo_out[p], 16)
                for i in range(2):
                    load_weights(Step(None, i, KM), i)
                steps(sp, TILES, RR, RR, load_reads)
                steps(sp, KM, 2, 2, body)
                for p in range(2):
                    sp.wait_ge(mo_out[p], 16 * KM // 2)

            @block.gpsimd
            def _(pool):
                pool.wait_ge(small_in, 32)

                def shift(s, p, live):
                    pool.wait_ge(gam_ok, count(s, 1, 1))
                    pool.tensor_tensor(raw[:, p], raw[:, p], spread(bet[:].unsqueeze(2), P, 2 * KH, P), ALU.add)\
                        .then_inc(bet_ok, 1)
                steps(pool, TILES, 0, RR, shift)

            @block.scalar
            def _(act):
                def hi_x(s, p, live):
                    act.wait_ge(bet_ok, count(s, 1, 1))
                    dst = xh[:].rearrange("p t k j -> p (t k j)")[:, ds(s.at(2 * KH * P), 2 * KH * P)]
                    act.activation(dst, raw[:, p].rearrange("p k j -> p (k j)"), ACT.Copy).then_inc(x_hi, 1)

                def split(s, p):
                    act.wait_ge(w_in[p], dma_count(s, 2, 1))
                    if (s - 2).exists():
                        act.wait_ge(mm_u, count(s - 2, NC_, NC_))
                    act.activation(wh[:, p], wraw[:, p], ACT.Copy).then_inc(w_hi, 1)

                def body(s, p, live):
                    if live(0) and not (s.reg is None and s.off < 2):
                        split(s, p)
                    if live(1):
                        for c in range(NC_):
                            act.wait_ge(mm_g, count(s - 1, NC_, c + 1))
                            if c >= 2:
                                act.wait_ge(mo_ok, count(s - 1, NC_, c - 1))
                            else:
                                if (s - 2).exists():
                                    act.wait_ge(mo_ok, count(s - 2, NC_, c + 3))
                            act.activation(sil[:, c % 2], psG[c][:], ACT.Silu).then_inc(sil_ok, 1)
                for i in range(2):
                    split(Step(None, i, KM), i)
                steps(act, TILES, 0, RR, hi_x)
                steps(act, KM, 1, 2, body)

            @block.tensor
            def _(pe):
                def body(s, p, live):
                    for c in range(NC_):
                        if c == 0:
                            pe.wait_ge(w_hi, count(s, 1, 1))
                            pe.wait_ge(w_lo, count(s, 1, 1))
                        if s.reg is None and s.off == 0:
                            pe.wait_ge(x_lo, CH * (c + 1))
                        for side, bank, done, freed in ((0, psG, mm_g, sil_ok), (1, psU, mm_u, mo_ok)):
                            if (s - 1).exists():
                                pe.wait_ge(freed, count(s - 1, NC_, c + 1))
                            for i in range(KH):
                                kt = side * KH + i
                                for w, x in ((wh, xh), (wh, xl), (wl, xh)):
                                    mm = pe.matmul(bank[c][:], w[:, p, kt], x[:, CH * c:CH * (c + 1), kt],
                                                   start=(i == 0 and w is wh and x is xh),
                                                   stop=(i == KH - 1 and w is wl))
                            mm.then_inc(done, 1)
                steps(pe, KM, 2, 2, lambda s, p, live: body(s, p, live) if live(0) else None)

            @block.vector
            def _(dve):
                def scale(s, p):
                    if s.reg is None and s.off == 0:
                        dve.wait_ge(small_in, 32)
                    dve.wait_ge(r_in[p], dma_count(s, RR, 1))
                    dve.tensor_tensor(raw[:, p], raw[:, p], spread(gam[:].unsqueeze(2), P, 2 * KH, P), ALU.mult)\
                       .then_inc(gam_ok, 1)

                def lo_x(s, p):
                    dve.wait_ge(x_hi, count(s, 1, 1))
                    at = ds(s.at(2 * KH * P), 2 * KH * P)
                    dve.tensor_tensor(xl[:].rearrange("p t k j -> p (t k j)")[:, at],
                                      raw[:, p].rearrange("p k j -> p (k j)"),
                                      xh[:].rearrange("p t k j -> p (t k j)")[:, at], ALU.subtract).then_inc(x_lo, 1)

                def reads(s, p, live):
                    if live(0):
                        scale(s, p)
                    if live(1):
                        lo_x(s - 1, (p - 1) % RR)

                def split(s, p):
                    dve.wait_ge(w_hi, count(s, 1, 1))
                    dve.tensor_tensor(wl[:, p], wraw[:, p], wh[:, p], ALU.subtract).then_inc(w_lo, 1)

                def body(s, p, live):
                    if live(0) and not (s.reg is None and s.off < 2):
                        split(s, p)
                    if live(1):
                        if (s - 3).exists():
                            dve.wait_ge(mo_out[1 - p], dma_count(s - 3, 2, 1))
                        for c in range(NC_):
                            dve.wait_ge(sil_ok, count(s - 1, NC_, c + 1))
                            dve.wait_ge(mm_u, count(s - 1, NC_, c + 1))
                            dve.tensor_tensor(mo[:, 1 - p, c], psU[c][:], sil[:, c % 2], ALU.mult).then_inc(mo_ok, 1)
                for i in range(2):
                    split(Step(None, i, KM), i)
                steps(dve, TILES, 1, RR, reads)
                steps(dve, KM, 1, 2, body, 3)


def timeline(eng, end, unroll, spans, body):
    def alive(s):
        return frozenset(n for n, (a, c) in spans.items() if a <= s < a + c)

    def run(reg, off, s0, slot):
        names = alive(s0)
        body(lambda n, back=0: Step(reg, off - spans[n][0] - back, spans[n][1]), slot, lambda n: n in names)

    signs = [tuple(alive(s) for s in range(t, min(t + unroll, end))) for t in range(0, end, unroll)]
    t = 0
    while t < len(signs):
        n = 1
        while t and t + n < len(signs) and signs[t + n] == signs[t]:
            n += 1
        if n > 1:
            with eng.Fori(0, n) as i:
                base = i * unroll
                for j in range(unroll):
                    run(base, t * unroll + j, t * unroll + j, j)
        else:
            for j in range(len(signs[t])):
                run(None, t * unroll + j, t * unroll + j, j)
        t += n


def build_ffn(nc, io, k):
    NP = C
    PIECES = NP * KD
    GR = P // (G // C)
    with ExitStack() as ctx:
        sb, ps, sem = allocators(nc, ctx, "s6_")
        wh = sb("f_wh", [P, 2, KD, H], F32R)
        wl = sb("f_wl", [P, 2, KD, H], F32R)
        xr = sb("f_xr", [P, 2, KD, P])
        xh = sb("f_xh", [P, 2, KD, P], F32R)
        xl = sb("f_xl", [P, 2, KD, P], F32R)
        q = sb("f_q", [P, 4, H], I32)
        w = q[:].bitcast(F32)
        sz = sb("f_sz", [P, 2, 2, H])
        xb = sb("f_xb", [P, 2, H])
        fb = sb("f_fb", [P, D])
        psF = [ps(f"psF{i}", [P, H]) for i in range(2)]

        q_in = [sem(f"q_in{p}") for p in range(4)]
        sz_in = [sem(f"sz_in{p}") for p in range(2)]
        x_in = [sem(f"fx_in{p}") for p in range(2)]
        xb_in = [sem(f"xb_in{p}") for p in range(2)]
        y_out = [sem(f"y_out{p}") for p in range(2)]
        less_zp, w_ok, w_hi, w_lo = sem("less_zp"), sem("w_ok"), sem("fw_hi"), sem("fw_lo")
        x_hi, x_lo, mm_ok, y_ok = sem("fx_hi"), sem("fx_lo"), sem("mm_ok"), sem("y_ok")
        fb_in, b_ok = sem("fb_in"), sem("b_ok")

        assert TILES == KD
        U = NP * TILES
        spans = {"piece": (0, PIECES), "lo": (1, PIECES), "x": (KD, U), "mm": (KD + 1, U), "done": (KD + 2, U),
                 "out": (KD + 3, U)}
        end = KD + 3 + U
        UN = 8

        def at_piece(v):
            n = v.at()
            return n // KD % 2, n % C * KH + n % KD // C

        def plane(u):
            n = u.at()
            return n // TILES, n % TILES

        with nc.Block() as block:
            @block.sync
            def _(sp):
                sp.dma_start(fb[:], io["fbias"]).then_inc(fb_in, 16)

                def body(tile, j, live):
                    p = j % 2
                    if live("piece"):
                        v = tile("piece")
                        if j % 4 == 0:
                            r = j // 4
                            if (tile("piece", 8)).exists():
                                sp.wait_ge(w_ok, count(tile("piece", 8), 1, 4))
                            sp.sem_inc(k["settled"], 1)
                            for i, name in enumerate(("scT", "zpT")):
                                src = io[name][ds(v.at() // 4, 1)].rearrange("o g n -> (o g) n")
                                src = spread(src.unsqueeze(1), GR, P // GR, H)
                                sp.dma_start(sz[:, r, i], src).then_inc(sz_in[r], 16)
                        if tile("piece", 4).exists():
                            sp.wait_ge(w_lo, count(tile("piece", 4), 1, 1))
                        sp.sem_inc(k["settled"], 1)
                        sp.dma_start(q[:, j % 4], io["wq"][ds(v.at(), 1)].rearrange("o p f -> (o p) f"))\
                          .then_inc(q_in[j % 4], 16)
                    if live("x"):
                        c_, t_ = plane(tile("x"))
                        if tile("x", 2).exists():
                            sp.wait_ge(x_lo, count(tile("x", 2), 1, 1))
                        sp.sem_inc(k["settled"], 1)
                        sp.dma_start(xr[:, p].rearrange("p t j -> p (t j)"),
                                     io["xnT"][ds(t_, 1)].rearrange("o p f -> (o p) f")).then_inc(x_in[p], 16)
                    if live("out"):
                        c_, t_ = plane(tile("out"))
                        sp.wait_ge(y_ok, count(tile("out"), 1, 1))
                        sp.sem_inc(k["settled"], 1)
                        sp.dma_start(io["y"][ds(t_ * P, P), ds(c_ * H, H)], xb[:, 1 - p]).then_inc(y_out[1 - p], 16)
                    if live("mm"):
                        c_, t_ = plane(tile("mm"))
                        if tile("mm", 2).exists():
                            sp.wait_ge(y_out[1 - p], dma_count(tile("mm", 2), 2, 1))
                        sp.sem_inc(k["settled"], 1)
                        sp.dma_start(xb[:, 1 - p], io["x3"][ds(t_ * P, P), ds(c_ * H, H)]).then_inc(xb_in[1 - p], 16)
                timeline(sp, end, UN, spans, body)
                for p in range(2):
                    sp.wait_ge(y_out[p], 16 * U // 2)

            @block.gpsimd
            def _(pool):
                pool.wait_ge(fb_in, 16)

                def body(tile, j, live):
                    if live("piece"):
                        p = j % 2
                        pool.wait_ge(less_zp, count(tile("piece"), 1, 1))
                        pool.tensor_tensor(w[:, j % 4], w[:, j % 4], sz[:, j // 4, 0], ALU.mult).then_inc(w_ok, 1)
                    if live("mm"):
                        u, r = tile("mm"), (j - 1) % 2
                        pool.wait_ge(xb_in[r], dma_count(u, 2, 1))
                        cols = ds(u.at() // TILES * H, H)
                        pool.tensor_tensor(xb[:, r], xb[:, r], fb[:, cols], ALU.add).then_inc(b_ok, 1)
                timeline(pool, end, UN, spans, body)

            @block.scalar
            def _(act):
                def body(tile, j, live):
                    p = j % 2
                    if live("x"):
                        act.wait_ge(x_in[p], dma_count(tile("x"), 2, 1))
                        if live("mm"):
                            if (tile("mm", 1)).exists():
                                act.wait_ge(mm_ok, count(tile("mm", 1), 1, 1))
                        act.activation(xh[:, p], xr[:, p], ACT.Copy).then_inc(x_hi, 1)
                    if live("piece"):
                        v = tile("piece")
                        b_, kt_ = at_piece(v)
                        act.wait_ge(w_ok, count(v, 1, 1))
                        if live("mm"):
                            act.wait_ge(mm_ok, count(tile("mm"), 1, 1))
                        dst = wh[:].rearrange("p b k n -> p (b k n)")[:, ds(b_ * (KD * H) + kt_ * H, H)]
                        act.activation(dst, w[:, j % 4], ACT.Copy).then_inc(w_hi, 1)
                timeline(act, end, UN, spans, body)

            @block.tensor
            def _(pe):
                def body(tile, j, live):
                    if not live("mm"):
                        return
                    u, p = tile("mm"), (j - 1) % 2
                    pe.wait_ge(x_hi, count(u, 1, 1))
                    pe.wait_ge(x_lo, count(u, 1, 1))
                    if live("piece"):
                        pe.wait_ge(w_lo, count(tile("piece", 2), 1, 1))
                    else:
                        pe.wait_ge(w_lo, PIECES)
                    if (tile("mm", 2)).exists():
                        pe.wait_ge(y_ok, count(tile("mm", 2), 1, 1))
                    buf = (u.at() // TILES) % 2
                    for kt in range(KD):
                        rh = wh[:].rearrange("p b k n -> p (b k n)")[:, ds(buf * (KD * H) + kt * H, H)]
                        rl = wl[:].rearrange("p b k n -> p (b k n)")[:, ds(buf * (KD * H) + kt * H, H)]
                        pe.matmul(psF[p][:], xh[:, p, kt], rh, start=(kt == 0), stop=False)
                        pe.matmul(psF[p][:], xh[:, p, kt], rl, start=False, stop=False)
                        mm = pe.matmul(psF[p][:], xl[:, p, kt], rh, start=False, stop=(kt == KD - 1))
                    mm.then_inc(mm_ok, 1)
                timeline(pe, end, UN, spans, body)

            @block.vector
            def _(dve):
                def body(tile, j, live):
                    p = j % 2
                    if live("x"):
                        dve.wait_ge(x_hi, count(tile("x"), 1, 1))
                        dve.tensor_tensor(xl[:, p], xr[:, p], xh[:, p], ALU.subtract).then_inc(x_lo, 1)
                    if live("piece"):
                        v = tile("piece")
                        dve.wait_ge(q_in[j % 4], dma_count(v, 4, 1))
                        if j % 4 == 0:
                            dve.wait_ge(sz_in[j // 4], v.turn(8, 32, 32))
                        dve.tensor_tensor(w[:, j % 4], q[:, j % 4], sz[:, j // 4, 1], ALU.subtract).then_inc(less_zp, 1)
                    if live("done"):
                        dve.wait_ge(mm_ok, count(tile("done"), 1, 1))
                        dve.wait_ge(b_ok, count(tile("done"), 1, 1))
                        dve.tensor_tensor(xb[:, p], psF[p][:], xb[:, p], ALU.add).then_inc(y_ok, 1)
                    if live("lo"):
                        v = tile("lo")
                        b_, kt_ = at_piece(v)
                        dve.wait_ge(w_hi, count(v, 1, 1))
                        at = ds(b_ * (KD * H) + kt_ * H, H)
                        dve.tensor_tensor(wl[:].rearrange("p b k n -> p (b k n)")[:, at], w[:, (j - 1) % 4],
                                          wh[:].rearrange("p b k n -> p (b k n)")[:, at], ALU.subtract).then_inc(w_lo, 1)
                timeline(dve, end, UN, spans, body)


def build(nc, io):
    for name, shape in (("qkT", (2, 2, HEADS * HD, L)), ("hs2", (T, D)), ("giT", (TILES, P, 2 * H)),
                        ("mlpT", (TILES, P, M)), ("xnT", (TILES, P, D)), ("x3", (T, D))):
        io[name] = nc.dram_tensor(name, shape, F32).ap()
    TAKEN.clear()
    with ExitStack() as ctx:
        k = build_constants(nc, ctx, io)
        with ExitStack() as ctx_v:
            allocate_values(nc, ctx_v, k)
            build_qkv(nc, io, k)
            sb, _, _ = allocators(nc, ctx_v)
            k["o_sb"] = sb("o_sb", [P, HEADS, QT, HD])
            build_attention(nc, io, k)
            retire(nc, k["settled"])
            build_write(nc, io, k, True)
        build_mlp(nc, io, k)
        build_write(nc, io, k, False)
        build_ffn(nc, io, k)


def kernel(x, pos_BxS, ctx_1024, L0_xattn_attn_read_w, L0_xattn_attn_read_g, L0_xattn_attn_read_b, L0_xattn_qkv_w,
           L0_xattn_attn_wod_w, L0_xattn_attn_wab_w, L0_xattn_attn_wab_b, L0_xattn_attn_du_w, L0_xattn_attn_du_b,
           L0_xattn_mlp_read_w, L0_xattn_mlp_read_g, L0_xattn_mlp_read_b, L0_xattn_mlp_wod_w, L0_xattn_mlp_wab_w,
           L0_xattn_mlp_wab_b, L0_xattn_mlp_du_w, L0_xattn_mlp_du_b, L0_ffn_weight_q, L0_ffn_scale, L0_ffn_zp,
           L0_ffn_bias):
    import concourse.bacc as bacc
    from concourse.bass_utils import run_bass_kernel_spmd

    def columns(w, outputs):
        return w.reshape(outputs, KH, P).transpose(2, 0, 1)

    def rows(v):
        return np.broadcast_to(v, (P,) + v.shape)

    def write_weights(wod, wab):
        w = np.concatenate([wod[:H // 2], wod[H:], wab[:NA], wod[H // 2:H], wab[NA:]], 0)
        return w.T.reshape(-1, P, NW).transpose(1, 0, 2)

    def small_bias(b):
        return rows(np.concatenate([np.zeros(DR, np.float32), b]))

    def delta_weights(w, b):
        return np.concatenate([w.T, b[None]], 0)

    def groups(s):
        return s.reshape(H, C, KH, KD // 2).transpose(1, 2, 3, 0).reshape(C * KH, KD // 2, H)

    a = {n: np.asarray(v) for n, v in dict(
        x=x, pos=pos_BxS, win=ctx_1024, arw=L0_xattn_attn_read_w, arg=L0_xattn_attn_read_g, arb=L0_xattn_attn_read_b,
        qkv=L0_xattn_qkv_w, awod=L0_xattn_attn_wod_w, awab=L0_xattn_attn_wab_w, awabb=L0_xattn_attn_wab_b,
        aduw=L0_xattn_attn_du_w, adub=L0_xattn_attn_du_b, mrw=L0_xattn_mlp_read_w, mrg=L0_xattn_mlp_read_g,
        mrb=L0_xattn_mlp_read_b, mwod=L0_xattn_mlp_wod_w, mwab=L0_xattn_mlp_wab_w, mwabb=L0_xattn_mlp_wab_b,
        mduw=L0_xattn_mlp_du_w, mdub=L0_xattn_mlp_du_b, wq=L0_ffn_weight_q, sc=L0_ffn_scale, zp=L0_ffn_zp,
        bias=L0_ffn_bias).items()}
    xt = a["x"].reshape(T, D)
    arrays = {
        "xT": xt.T.reshape(KD, P, T).transpose(1, 0, 2),
        "xP": xt.reshape(T, H, C).transpose(0, 2, 1).reshape(T, D),
        "pos": a["pos"].reshape(TILES, P).T,
        "wr1": a["arw"].transpose(0, 2, 1).reshape(KD, P, 3).transpose(1, 0, 2),
        "g1": columns(a["arg"], 3),
        "b1": columns(a["arb"], 3),
        "wqkv": a["qkv"].transpose(2, 0, 1).reshape(KH, P, 3 * H).transpose(1, 0, 2),
        "wo1": write_weights(a["awod"], a["awab"]),
        "bsm1": small_bias(a["awabb"]),
        "du1": delta_weights(a["aduw"], a["adub"]),
        "wr2": a["mrw"].reshape(KD, HD, 2, C).transpose(3, 1, 0, 2).reshape(P, KD, 2),
        "g2": columns(a["mrg"], 2).reshape(P, 2 * KH),
        "b2": columns(a["mrb"], 2).reshape(P, 2 * KH),
        "wmlp": a["win"].reshape(2, KM, P, KH, P).transpose(1, 4, 0, 3, 2).reshape(KM, P, 2 * H),
        "wo2": write_weights(a["mwod"], a["mwab"]),
        "bsm2": small_bias(a["mwabb"]),
        "du2": delta_weights(a["mduw"], a["mdub"]),
        "fbias": rows(a["bias"].reshape(H, C).T.reshape(D)),
        "wq": a["wq"].reshape(H, C, KH, P, C).transpose(1, 2, 4, 3, 0).reshape(C * KD, P, H),
        "scT": groups(a["sc"]),
        "zpT": groups(a["zp"]),
    }
    arrays = {n: np.ascontiguousarray(v) for n, v in arrays.items()}
    nc = bacc.Bacc("TRN2", target_bir_lowering=False, num_devices=1)
    io = {n: nc.dram_tensor(n, v.shape, mybir.dt.from_np(v.dtype), kind="ExternalInput").ap() for n, v in arrays.items()}
    io["y"] = nc.dram_tensor("y", (T, D), F32, kind="ExternalOutput").ap()
    build(nc, io)
    r = run_bass_kernel_spmd(nc, [arrays], core_ids=[0])
    return r.results[0]["y"].reshape(B, L, C, H).transpose(0, 1, 3, 2).reshape(B, L, D)
```
